# Optimizing a Trainium2 kernel written in Bass

```python
import numpy as np
import jax
import jax.numpy as jnp

def _softmax(x, axis=-1):
    return jax.nn.softmax(x, axis=axis)

def _gelu(x):
    return jax.nn.gelu(x, approximate=True)

def _silu(x):
    return jax.nn.silu(x)

def _sigmoid(x):
    return jax.nn.sigmoid(x)

def _layernorm(x, axis=-1, eps=1e-05):
    m = jnp.mean(x, axis=axis, keepdims=True)
    v = jnp.var(x, axis=axis, keepdims=True)
    return (x - m) / jnp.sqrt(v + eps)

def _scatter_add(tgt, idx, src, axis=0):
    return tgt.at[idx].add(src)

def _segment_sum(src, seg, n):
    return jax.ops.segment_sum(src, seg, n)
kernel_name = 'mk_xattn_ffn_d4_seqx_r8_061701'

def setup_inputs(seed: int=0):
    np.random.seed(seed)
    _w = jnp.asarray

    def _rec_inputs():
        import jax
        import jax.numpy as jnp
        _rk = jax.random.key(seed)
        x = -0.0002928 + 1 * jax.random.normal(jax.random.fold_in(_rk, 1), (8, 256, 128), jnp.float32)
        _lenS = 256 - jax.random.randint(jax.random.fold_in(_rk, 7), (8,), 0, max(1, 256 // 4) + 1, jnp.int32)
        _lenS2 = 512 - jax.random.randint(jax.random.fold_in(_rk, 8), (8,), 0, max(1, 512 // 4) + 1, jnp.int32)
        _ctx_1024P = jax.random.normal(jax.random.fold_in(_rk, 11), (8, 16, 128), jnp.float32)
        _ctx_1024c = jax.random.dirichlet(jax.random.fold_in(_rk, 511), 0.3 * jnp.ones((16,), jnp.float32), (8, 512))
        _ctx_1024t = jnp.einsum('bsk,bkd->bsd', _ctx_1024c, _ctx_1024P)
        _ctx_1024t = _ctx_1024t * jax.lax.rsqrt(jnp.mean(jnp.square(_ctx_1024t)) + 1e-12) * 0.953939
        ctx_1024 = -1.39393e-06 + 0.999914 * (_ctx_1024t + 0.3 * jax.random.normal(jax.random.fold_in(_rk, 611), (8, 512, 128), jnp.float32))
        _validS = jnp.arange(256)[None, :] < _lenS[:, None]
        _validS2 = jnp.arange(512)[None, :] < _lenS2[:, None]
        _causal = jnp.tril(jnp.ones((256, 256), dtype=bool))
        mask_1x1xSxS2_ff0 = jnp.where(jnp.ones((1, 1, 256, 512), dtype=bool), 0.0, -1000000000.0).astype(jnp.float32)
        return (x, ctx_1024, mask_1x1xSxS2_ff0)
    x, ctx_1024, mask_1x1xSxS2_ff0 = _rec_inputs()

    def _L0_xattn_setup():
        import jax, jax.numpy as jnp
        import numpy as np
        B, L, H, NH = (2, 256, 128, 16)
        DEPTH = H // NH

        def _split_heads(t):
            b, l, _ = t.shape
            return t.reshape(b, l, NH, DEPTH).transpose(0, 2, 1, 3)
        key = jax.random.key(seed)
        ks = jax.random.split(key, 7)
        s = 1.0 / np.sqrt(H)
        return {'x': jax.random.normal(ks[0], (B, L, H), dtype=jnp.float32), 'y': jax.random.normal(ks[1], (B, L, H), dtype=jnp.float32), 'bias': jnp.zeros((1, 1, L, L), dtype=jnp.float32), 'Wq': jax.random.normal(ks[2], (H, H), dtype=jnp.float32) * s, 'Wk': jax.random.normal(ks[3], (H, H), dtype=jnp.float32) * s, 'Wv': jax.random.normal(ks[4], (H, H), dtype=jnp.float32) * s, 'Wo': jax.random.normal(ks[5], (H, H), dtype=jnp.float32) * s}
    _L0_xattn_all = _L0_xattn_setup()
    _L0_xattn_in = {k: v for k, v in _L0_xattn_all.items() if k in ('Wq', 'Wk', 'Wv', 'Wo')}
    del _L0_xattn_all

    def _L0_ffn_setup():
        import jax, jax.numpy as jnp
        import numpy as np
        DIM = 128
        N_EXPERTS = 16
        TOP_K = 4
        N_GROUP = 4
        TOPK_GROUP = 2
        MOE_INTER = 64
        SHARED_INTER = 256
        ROUTED_SCALE = 2.5

        def relu2(x):
            return jnp.square(jax.nn.relu(x))

        def _router(x2, gate_w, bias_e):
            T = x2.shape[0]
            logits = x2 @ gate_w.T
            scores = jax.nn.sigmoid(logits)
            sc = jax.lax.stop_gradient(scores + bias_e[None, :])
            grp = sc.reshape(T, N_GROUP, N_EXPERTS // N_GROUP)
            top2, _ = jax.lax.top_k(grp, 2)
            group_scores = top2.sum(-1)
            _, gidx = jax.lax.top_k(group_scores, TOPK_GROUP)
            rows = jnp.arange(T)[:, None]
            gmask = jnp.zeros((T, N_GROUP), dtype=sc.dtype).at[rows, gidx].set(1.0)
            smask = jnp.repeat(gmask, N_EXPERTS // N_GROUP, axis=1)
            masked = jnp.where(smask > 0, sc, 0.0)
            _, topk_idx = jax.lax.top_k(masked, TOP_K)
            topk_w = jnp.take_along_axis(scores, topk_idx, axis=1)
            topk_w = topk_w / (topk_w.sum(-1, keepdims=True) + 1e-20)
            topk_w = topk_w * ROUTED_SCALE
            return (topk_idx, topk_w)
        key = jax.random.key(seed)
        ks = jax.random.split(key, 6)
        hidden_states = jax.random.normal(ks[0], (2, 256, DIM), dtype=jnp.float32)
        gate_w = jax.random.normal(ks[1], (N_EXPERTS, DIM), dtype=jnp.float32) * 0.02
        bias_e = jnp.zeros((N_EXPERTS,), dtype=jnp.float32)
        up_w = jax.random.normal(ks[2], (N_EXPERTS, MOE_INTER, DIM), dtype=jnp.float32) * 0.02
        down_w = jax.random.normal(ks[3], (N_EXPERTS, DIM, MOE_INTER), dtype=jnp.float32) * 0.02
        shared_up = jax.random.normal(ks[4], (SHARED_INTER, DIM), dtype=jnp.float32) * 0.02
        shared_down = jax.random.normal(ks[5], (DIM, SHARED_INTER), dtype=jnp.float32) * 0.02
        return {'hidden_states': hidden_states, 'gate_w': gate_w, 'bias_e': bias_e, 'up_w': up_w, 'down_w': down_w, 'shared_up': shared_up, 'shared_down': shared_down}
    _L0_ffn_all = _L0_ffn_setup()
    _L0_ffn_in = {k: v for k, v in _L0_ffn_all.items() if k in ('gate_w', 'bias_e', 'up_w', 'down_w', 'shared_up', 'shared_down')}
    del _L0_ffn_all

    def _L1_xattn_setup():
        import jax, jax.numpy as jnp
        import numpy as np
        D1, D2, D3 = (128, 128, 128)
        key = jax.random.key(seed)
        k1, k2, kw, kb = jax.random.split(key, 4)
        x1 = jax.random.normal(k1, (8, 256, D1), dtype=jnp.float32)
        x2 = jax.random.normal(k2, (8, 256, D2), dtype=jnp.float32)
        bound = 1.0 / np.sqrt(D1 + D2)
        W = jax.random.uniform(kw, (D3, D1 + D2), minval=-bound, maxval=bound, dtype=jnp.float32)
        b = jax.random.uniform(kb, (D3,), minval=-bound, maxval=bound, dtype=jnp.float32)
        return {'x1': x1, 'x2': x2, 'W': W, 'b': b}
    _L1_xattn_all = _L1_xattn_setup()
    _L1_xattn_in = {k: v for k, v in _L1_xattn_all.items() if k in ('W', 'b')}
    del _L1_xattn_all

    def _L1_ffn_setup():
        import jax, jax.numpy as jnp
        import numpy as np
        DIM = 128
        HID = 512
        E = 8
        TOPK = 2
        ALPHA = 2.0
        B, T = (1, 256)
        DOWN_SCALE = 0.01
        key = jax.random.key(seed)
        ks = jax.random.split(key, 8)
        s = 1.0 / np.sqrt(DIM)
        sh = 1.0 / np.sqrt(HID)
        return {'x': jax.random.normal(ks[0], (B, T, DIM), jnp.float32), 'w_router': jax.random.uniform(ks[1], (DIM, E), jnp.float32, -s, s), 'w_up': jax.random.uniform(ks[2], (E - 1, DIM, HID), jnp.float32, -s, s), 'w_gate': jax.random.uniform(ks[3], (E - 1, DIM, HID), jnp.float32, -s, s), 'w_down': jax.random.normal(ks[4], (E - 1, HID, DIM), jnp.float32) * DOWN_SCALE, 'ws_up': jax.random.uniform(ks[5], (DIM, HID), jnp.float32, -s, s), 'ws_gate': jax.random.uniform(ks[6], (DIM, HID), jnp.float32, -s, s), 'ws_down': jax.random.normal(ks[7], (HID, DIM), jnp.float32) * DOWN_SCALE}
    _L1_ffn_all = _L1_ffn_setup()
    _L1_ffn_in = {k: v for k, v in _L1_ffn_all.items() if k in ('w_router', 'w_up', 'w_gate', 'w_down', 'ws_up', 'ws_gate', 'ws_down')}
    del _L1_ffn_all

    def _L2_xattn_setup():
        import jax, jax.numpy as jnp
        import numpy as np
        N_EMBD = 128
        N_HEAD = 16
        R = 16
        SCALING = 1.0 / 16.0

        def lora_linear(x, W, b, A, B):
            return x @ W.T + b + x @ A.T @ B.T * SCALING
        key = jax.random.key(seed)
        ks = jax.random.split(key, 16)
        B, T, S, C = (8, 128, 32, N_EMBD)
        std = 0.02
        return {'x': jax.random.normal(ks[0], (B, T, C), jnp.float32), 'feature': jax.random.normal(ks[1], (B, S, C), jnp.float32), 'Wq': jax.random.normal(ks[2], (C, C), jnp.float32) * std, 'bq': jnp.zeros((C,), jnp.float32), 'Aq': jax.random.normal(ks[3], (R, C), jnp.float32) * std, 'Bq': jnp.zeros((C, R), jnp.float32), 'Wf': jax.random.normal(ks[4], (2 * C, C), jnp.float32) * std, 'bf': jnp.zeros((2 * C,), jnp.float32), 'Af': jax.random.normal(ks[5], (R, C), jnp.float32) * std, 'Bf': jnp.zeros((2 * C, R), jnp.float32), 'Wp': jax.random.normal(ks[6], (C, C), jnp.float32) * std, 'bp': jnp.zeros((C,), jnp.float32), 'Ap': jax.random.normal(ks[7], (R, C), jnp.float32) * std, 'Bp': jnp.zeros((C, R), jnp.float32)}
    _L2_xattn_all = _L2_xattn_setup()
    _L2_xattn_in = {k: v for k, v in _L2_xattn_all.items() if k in ('Wq', 'bq', 'Aq', 'Bq', 'Wf', 'bf', 'Af', 'Bf', 'Wp', 'bp', 'Ap', 'Bp')}
    del _L2_xattn_all

    def _L2_ffn_setup():
        import jax, jax.numpy as jnp
        import numpy as np
        W_SCALE = 0.02
        TOP_K = 2
        key = jax.random.key(seed)
        ks = jax.random.split(key, 5)
        B, S, H, I, E = (2, 128, 128, 512, 8)
        return {'x': jax.random.normal(ks[0], (B, S, H), dtype=jnp.float32), 'gate': jax.random.normal(ks[1], (H, E), dtype=jnp.float32) * W_SCALE, 'experts_w1': jax.random.normal(ks[2], (E, H, I), dtype=jnp.float32) * W_SCALE, 'experts_w2': jax.random.normal(ks[3], (E, I, H), dtype=jnp.float32) * W_SCALE, 'experts_w3': jax.random.normal(ks[4], (E, H, I), dtype=jnp.float32) * W_SCALE}
    _L2_ffn_all = _L2_ffn_setup()
    _L2_ffn_in = {k: v for k, v in _L2_ffn_all.items() if k in ('gate', 'experts_w1', 'experts_w2', 'experts_w3')}
    del _L2_ffn_all

    def _L3_xattn_setup():
        import jax, jax.numpy as jnp
        import numpy as np
        D_MODEL = 128
        key = jax.random.key(seed)
        ks = jax.random.split(key, 11)
        B, Sq, Skv, D = (16, 256, 256, D_MODEL)
        s = 1.0 / np.sqrt(D)
        return {'q': jax.random.normal(ks[0], (B, Sq, D), jnp.float32), 'k': jax.random.normal(ks[1], (B, Skv, D), jnp.float32), 'v': jax.random.normal(ks[2], (B, Skv, D), jnp.float32), 'Wq': jax.random.normal(ks[3], (D, D), jnp.float32) * s, 'bq': jnp.zeros((D,), jnp.float32), 'Wk': jax.random.normal(ks[4], (D, D), jnp.float32) * s, 'bk': jnp.zeros((D,), jnp.float32), 'Wv': jax.random.normal(ks[5], (D, D), jnp.float32) * s, 'bv': jnp.zeros((D,), jnp.float32), 'Wo': jax.random.normal(ks[6], (D, D), jnp.float32) * s, 'bo': jnp.zeros((D,), jnp.float32)}
    _L3_xattn_all = _L3_xattn_setup()
    _L3_xattn_in = {k: v for k, v in _L3_xattn_all.items() if k in ('Wq', 'bq', 'Wk', 'bk', 'Wv', 'bv', 'Wo', 'bo')}
    del _L3_xattn_all

    def _L3_ffn_setup():
        import jax, jax.numpy as jnp
        import numpy as np
        N_HEADS = 4
        key = jax.random.key(seed)
        k1, k2, k3, k4 = jax.random.split(key, 4)
        dmodel, n_experts, expert_size = (128, 64, 128)
        B, S = (4, 256)
        x = jax.random.normal(k1, (B, S, dmodel), dtype=jnp.float32)
        expert_sel = jax.random.normal(k2, (n_experts, dmodel), dtype=jnp.float32) * dmodel ** (-0.5)
        keys = jax.random.normal(k3, (n_experts, dmodel, expert_size), dtype=jnp.float32) * dmodel ** (-0.5)
        values = jax.random.normal(k4, (n_experts, expert_size, dmodel), dtype=jnp.float32) * (n_experts * expert_size) ** (-0.5)
        return {'x': x, 'expert_sel': expert_sel, 'keys': keys, 'values': values}
    _L3_ffn_all = _L3_ffn_setup()
    _L3_ffn_in = {k: v for k, v in _L3_ffn_all.items() if k in ('expert_sel', 'keys', 'values')}
    del _L3_ffn_all
    return {'x': x, 'ctx_1024': ctx_1024, 'mask_1x1xSxS2_ff0': mask_1x1xSxS2_ff0, 'L0_xattn_Wq': _L0_xattn_in['Wq'], 'L0_xattn_Wk': _L0_xattn_in['Wk'], 'L0_xattn_Wv': _L0_xattn_in['Wv'], 'L0_xattn_Wo': _L0_xattn_in['Wo'], 'L0_ffn_gate_w': _L0_ffn_in['gate_w'], 'L0_ffn_bias_e': _L0_ffn_in['bias_e'], 'L0_ffn_up_w': _L0_ffn_in['up_w'], 'L0_ffn_down_w': _L0_ffn_in['down_w'], 'L0_ffn_shared_up': _L0_ffn_in['shared_up'], 'L0_ffn_shared_down': _L0_ffn_in['shared_down'], 'L1_xattn_W': _L1_xattn_in['W'], 'L1_xattn_b': _L1_xattn_in['b'], 'L1_ffn_w_router': _L1_ffn_in['w_router'], 'L1_ffn_w_up': _L1_ffn_in['w_up'], 'L1_ffn_w_gate': _L1_ffn_in['w_gate'], 'L1_ffn_w_down': _L1_ffn_in['w_down'], 'L1_ffn_ws_up': _L1_ffn_in['ws_up'], 'L1_ffn_ws_gate': _L1_ffn_in['ws_gate'], 'L1_ffn_ws_down': _L1_ffn_in['ws_down'], 'L2_xattn_Wq': _L2_xattn_in['Wq'], 'L2_xattn_bq': _L2_xattn_in['bq'], 'L2_xattn_Aq': _L2_xattn_in['Aq'], 'L2_xattn_Bq': _L2_xattn_in['Bq'], 'L2_xattn_Wf': _L2_xattn_in['Wf'], 'L2_xattn_bf': _L2_xattn_in['bf'], 'L2_xattn_Af': _L2_xattn_in['Af'], 'L2_xattn_Bf': _L2_xattn_in['Bf'], 'L2_xattn_Wp': _L2_xattn_in['Wp'], 'L2_xattn_bp': _L2_xattn_in['bp'], 'L2_xattn_Ap': _L2_xattn_in['Ap'], 'L2_xattn_Bp': _L2_xattn_in['Bp'], 'L2_ffn_gate': _L2_ffn_in['gate'], 'L2_ffn_experts_w1': _L2_ffn_in['experts_w1'], 'L2_ffn_experts_w2': _L2_ffn_in['experts_w2'], 'L2_ffn_experts_w3': _L2_ffn_in['experts_w3'], 'L3_xattn_Wq': _L3_xattn_in['Wq'], 'L3_xattn_bq': _L3_xattn_in['bq'], 'L3_xattn_Wk': _L3_xattn_in['Wk'], 'L3_xattn_bk': _L3_xattn_in['bk'], 'L3_xattn_Wv': _L3_xattn_in['Wv'], 'L3_xattn_bv': _L3_xattn_in['bv'], 'L3_xattn_Wo': _L3_xattn_in['Wo'], 'L3_xattn_bo': _L3_xattn_in['bo'], 'L3_ffn_expert_sel': _L3_ffn_in['expert_sel'], 'L3_ffn_keys': _L3_ffn_in['keys'], 'L3_ffn_values': _L3_ffn_in['values']}

def reference(x, ctx_1024, mask_1x1xSxS2_ff0, L0_xattn_Wq, L0_xattn_Wk, L0_xattn_Wv, L0_xattn_Wo, L0_ffn_gate_w, L0_ffn_bias_e, L0_ffn_up_w, L0_ffn_down_w, L0_ffn_shared_up, L0_ffn_shared_down, L1_xattn_W, L1_xattn_b, L1_ffn_w_router, L1_ffn_w_up, L1_ffn_w_gate, L1_ffn_w_down, L1_ffn_ws_up, L1_ffn_ws_gate, L1_ffn_ws_down, L2_xattn_Wq, L2_xattn_bq, L2_xattn_Aq, L2_xattn_Bq, L2_xattn_Wf, L2_xattn_bf, L2_xattn_Af, L2_xattn_Bf, L2_xattn_Wp, L2_xattn_bp, L2_xattn_Ap, L2_xattn_Bp, L2_ffn_gate, L2_ffn_experts_w1, L2_ffn_experts_w2, L2_ffn_experts_w3, L3_xattn_Wq, L3_xattn_bq, L3_xattn_Wk, L3_xattn_bk, L3_xattn_Wv, L3_xattn_bv, L3_xattn_Wo, L3_xattn_bo, L3_ffn_expert_sel, L3_ffn_keys, L3_ffn_values):
    import jax
    import jax.numpy as jnp

    def _L0_xattn_ref(x, y, bias, Wq, Wk, Wv, Wo):
        import jax, jax.numpy as jnp
        import numpy as np
        B, L, H, NH = (2, 256, 128, 16)
        DEPTH = H // NH

        def _split_heads(t):
            b, l, _ = t.shape
            return t.reshape(b, l, NH, DEPTH).transpose(0, 2, 1, 3)
        q = _split_heads(x @ Wq)
        k = _split_heads(y @ Wk)
        v = _split_heads(y @ Wv)
        scale = DEPTH ** (-0.5)
        logits = jnp.einsum('bhqd,bhkd->bhqk', q * scale, k) + bias
        weights = jax.nn.softmax(logits, axis=-1)
        attn = jnp.einsum('bhqk,bhkd->bhqd', weights, v)
        attn = attn.transpose(0, 2, 1, 3).reshape(x.shape[0], x.shape[1], H)
        return attn @ Wo

    def _L0_ffn_ref(hidden_states, gate_w, bias_e, up_w, down_w, shared_up, shared_down):
        import jax, jax.numpy as jnp
        import numpy as np
        DIM = 128
        N_EXPERTS = 16
        TOP_K = 4
        N_GROUP = 4
        TOPK_GROUP = 2
        MOE_INTER = 64
        SHARED_INTER = 256
        ROUTED_SCALE = 2.5

        def relu2(x):
            return jnp.square(jax.nn.relu(x))

        def _router(x2, gate_w, bias_e):
            T = x2.shape[0]
            logits = x2 @ gate_w.T
            scores = jax.nn.sigmoid(logits)
            sc = jax.lax.stop_gradient(scores + bias_e[None, :])
            grp = sc.reshape(T, N_GROUP, N_EXPERTS // N_GROUP)
            top2, _ = jax.lax.top_k(grp, 2)
            group_scores = top2.sum(-1)
            _, gidx = jax.lax.top_k(group_scores, TOPK_GROUP)
            rows = jnp.arange(T)[:, None]
            gmask = jnp.zeros((T, N_GROUP), dtype=sc.dtype).at[rows, gidx].set(1.0)
            smask = jnp.repeat(gmask, N_EXPERTS // N_GROUP, axis=1)
            masked = jnp.where(smask > 0, sc, 0.0)
            _, topk_idx = jax.lax.top_k(masked, TOP_K)
            topk_w = jnp.take_along_axis(scores, topk_idx, axis=1)
            topk_w = topk_w / (topk_w.sum(-1, keepdims=True) + 1e-20)
            topk_w = topk_w * ROUTED_SCALE
            return (topk_idx, topk_w)
        B, S, D = hidden_states.shape
        x2 = hidden_states.reshape(-1, D)
        T = x2.shape[0]
        topk_idx, topk_w = _router(x2, gate_w, bias_e)
        rows = jnp.arange(T)[:, None]
        combine = jnp.zeros((T, N_EXPERTS), dtype=topk_w.dtype).at[rows, topk_idx].add(topk_w)

        def body(acc, inp):
            wu, wd, cw = inp
            y = relu2(x2 @ wu.T) @ wd.T
            return (acc + cw[:, None] * y, None)
        routed, _ = jax.lax.scan(body, jnp.zeros_like(x2), (up_w, down_w, combine.T))
        shared = relu2(x2 @ shared_up.T) @ shared_down.T
        out = routed + shared
        return out.reshape(B, S, D)

    def _L1_xattn_ref(x1, x2, W, b):
        import jax, jax.numpy as jnp
        import numpy as np
        D1, D2, D3 = (128, 128, 128)
        d1 = x1.shape[-1]
        W1 = W[:, :d1]
        W2 = W[:, d1:]
        part1 = jnp.einsum('bld,ed->ble', x1, W1)
        part2 = jnp.einsum('bld,ed->be', x2, W2) / x2.shape[1]
        return part1 + part2[:, None, :] + b

    def _L1_ffn_ref(x, w_router, w_up, w_gate, w_down, ws_up, ws_gate, ws_down):
        import jax, jax.numpy as jnp
        import numpy as np
        DIM = 128
        HID = 512
        E = 8
        TOPK = 2
        ALPHA = 2.0
        B, T = (1, 256)
        DOWN_SCALE = 0.01
        logits = x @ w_router
        probs = jax.nn.softmax(logits.astype(jnp.float32), axis=-1).astype(logits.dtype)
        topk_vals, topk_idx = jax.lax.top_k(probs, TOPK)
        up = jnp.einsum('btd,edh->ebth', x, w_up)
        gate = jax.nn.silu(jnp.einsum('btd,edh->ebth', x, w_gate))
        exp_out = jnp.einsum('ebth,ehd->ebtd', up * gate, w_down)
        out = jnp.zeros_like(x)
        eids = jnp.arange(E - 1)
        for i in range(TOPK - 1):
            idx_i = topk_idx[..., i]
            sel = (idx_i[None, :, :] == eids[:, None, None]).astype(x.dtype)
            gathered = jnp.einsum('ebt,ebtd->btd', sel, exp_out)
            out = out + ALPHA * topk_vals[..., i:i + 1] * gathered
        shared = x @ ws_up * jax.nn.silu(x @ ws_gate) @ ws_down
        return out + shared

    def _L2_xattn_ref(x, feature, Wq, bq, Aq, Bq, Wf, bf, Af, Bf, Wp, bp, Ap, Bp):
        import jax, jax.numpy as jnp
        import numpy as np
        N_EMBD = 128
        N_HEAD = 16
        R = 16
        SCALING = 1.0 / 16.0

        def lora_linear(x, W, b, A, B):
            return x @ W.T + b + x @ A.T @ B.T * SCALING
        Bsz, T, C = x.shape
        S = feature.shape[1]
        H = N_HEAD
        D = C // H
        q = lora_linear(x, Wq, bq, Aq, Bq).reshape(Bsz, T, H, D).transpose(0, 2, 1, 3)
        kv = lora_linear(feature, Wf, bf, Af, Bf)
        k, v = (kv[..., :C], kv[..., C:])
        k = k.reshape(Bsz, S, H, D).transpose(0, 2, 1, 3)
        v = v.reshape(Bsz, S, H, D).transpose(0, 2, 1, 3)
        att = jnp.einsum('bhtd,bhsd->bhts', q, k) * (1.0 / np.sqrt(D))
        mask = jnp.tril(jnp.ones((T, S), bool))
        att = jnp.where(mask, att, -jnp.inf)
        att = jax.nn.softmax(att, axis=-1)
        y = jnp.einsum('bhts,bhsd->bhtd', att, v)
        y = y.transpose(0, 2, 1, 3).reshape(Bsz, T, C)
        return lora_linear(y, Wp, bp, Ap, Bp)

    def _L2_ffn_ref(x, gate, experts_w1, experts_w2, experts_w3):
        import jax, jax.numpy as jnp
        import numpy as np
        W_SCALE = 0.02
        TOP_K = 2
        E = experts_w1.shape[0]
        router_logits = jnp.einsum('bsh,he->bse', x, gate)
        routing_weights, selected = jax.lax.top_k(router_logits, TOP_K)
        routing_weights = jax.nn.softmax(routing_weights, axis=-1)
        onehot = jax.nn.one_hot(selected, E, dtype=x.dtype)
        tok_w = jnp.einsum('bsk,bske->bse', routing_weights, onehot)
        g = jnp.einsum('bsh,ehi->ebsi', x, experts_w1)
        u = jnp.einsum('bsh,ehi->ebsi', x, experts_w3)
        hid = jax.nn.silu(g) * u
        eo = jnp.einsum('ebsi,eih->ebsh', hid, experts_w2)
        out = jnp.einsum('ebsh,bse->bsh', eo, tok_w)
        return out

    def _L3_xattn_ref(q, k, v, Wq, bq, Wk, bk, Wv, bv, Wo, bo):
        import jax, jax.numpy as jnp
        import numpy as np
        D_MODEL = 128
        D = q.shape[-1]
        query = q @ Wq + bq
        key_p = k @ Wk + bk
        value = v @ Wv + bv
        scores = jnp.einsum('bqd,bkd->bqk', query / jnp.sqrt(jnp.float32(D)), key_p)
        attn = jax.nn.softmax(scores, axis=-1)
        out = jnp.einsum('bqk,bkd->bqd', attn, value)
        return out @ Wo + bo

    def _L3_ffn_ref(x, expert_sel, keys, values):
        import jax, jax.numpy as jnp
        import numpy as np
        N_HEADS = 4
        B, S, d = x.shape
        n_experts = keys.shape[0]
        xf = x.reshape(-1, d)
        N = xf.shape[0]
        logits = xf @ expert_sel.T
        sel = jax.nn.sigmoid(logits)
        sel_val, sel_idx = jax.lax.top_k(sel, N_HEADS)
        gates = jnp.zeros((N, n_experts), dtype=x.dtype)
        gates = gates.at[jnp.arange(N)[:, None], sel_idx].set(sel_val)
        h = jnp.einsum('nd,kde->nke', xf, keys)
        scores = jax.nn.relu(h) * gates[:, :, None]
        out = jnp.einsum('nke,kev->nv', scores, values)
        return out.reshape(B, S, -1)
    x = x + _L0_xattn_ref(_layernorm(x, axis=-1), ctx_1024, mask_1x1xSxS2_ff0, L0_xattn_Wq, L0_xattn_Wk, L0_xattn_Wv, L0_xattn_Wo)
    x = x + _L0_ffn_ref(_layernorm(x, axis=-1), L0_ffn_gate_w, L0_ffn_bias_e, L0_ffn_up_w, L0_ffn_down_w, L0_ffn_shared_up, L0_ffn_shared_down)
    x = x + _L1_xattn_ref(_layernorm(x, axis=-1), ctx_1024, L1_xattn_W, L1_xattn_b)
    x = x + _L1_ffn_ref(_layernorm(x, axis=-1), L1_ffn_w_router, L1_ffn_w_up, L1_ffn_w_gate, L1_ffn_w_down, L1_ffn_ws_up, L1_ffn_ws_gate, L1_ffn_ws_down)
    x = x + _L2_xattn_ref(_layernorm(x, axis=-1), ctx_1024, L2_xattn_Wq, L2_xattn_bq, L2_xattn_Aq, L2_xattn_Bq, L2_xattn_Wf, L2_xattn_bf, L2_xattn_Af, L2_xattn_Bf, L2_xattn_Wp, L2_xattn_bp, L2_xattn_Ap, L2_xattn_Bp)
    x = x + _L2_ffn_ref(_layernorm(x, axis=-1), L2_ffn_gate, L2_ffn_experts_w1, L2_ffn_experts_w2, L2_ffn_experts_w3)
    x = x + _L3_xattn_ref(_layernorm(x, axis=-1), ctx_1024, ctx_1024, L3_xattn_Wq, L3_xattn_bq, L3_xattn_Wk, L3_xattn_bk, L3_xattn_Wv, L3_xattn_bv, L3_xattn_Wo, L3_xattn_bo)
    x = x + _L3_ffn_ref(_layernorm(x, axis=-1), L3_ffn_expert_sel, L3_ffn_keys, L3_ffn_values)
    return x

_drawn_inputs = setup_inputs


def setup_inputs(seed=0):
    import zlib

    import numpy as np

    out = dict(_drawn_inputs(seed))
    spreads = {'L0_ffn_bias_e': (0.0, 0.409),
     'L2_xattn_bq': (0.0, 0.8),
     'L2_xattn_Bq': (0.0, 0.8),
     'L2_xattn_bf': (0.0, 0.275),
     'L2_xattn_Bf': (0.0, 0.8),
     'L2_xattn_bp': (0.0, 0.1),
     'L2_xattn_Bp': (0.0, 0.8),
     'L3_xattn_bq': (0.0, 0.285),
     'L3_xattn_bk': (0.0, 0.8),
     'L3_xattn_bv': (0.0, 0.1),
     'L3_xattn_bo': (0.0, 0.1)}
    factors = {'L0_ffn_gate_w': 3.881,
     'L0_ffn_up_w': 3.434,
     'L0_ffn_down_w': 3.205,
     'L1_ffn_w_gate': 2.765,
     'L2_xattn_Wq': 8.0,
     'L2_xattn_Aq': 8.0,
     'L2_xattn_Af': 8.0,
     'L2_xattn_Ap': 8.0,
     'L2_ffn_gate': 4.937,
     'L2_ffn_experts_w1': 4.64,
     'L2_ffn_experts_w2': 4.597,
     'L2_ffn_experts_w3': 4.996}
    for name, (base, spread) in spreads.items():
        noise = np.random.default_rng([zlib.crc32(name.encode()), seed]).standard_normal(out[name].shape)
        drawn = base * np.exp(spread * noise) if base else spread * noise
        out[name] = jnp.asarray(drawn.astype(out[name].dtype))
    for name, factor in factors.items():
        out[name] = (out[name] * factor).astype(out[name].dtype)
    return out
```

```python
from contextlib import ExitStack

import numpy as np
import concourse.bass as bass
from concourse import mybir

F32 = mybir.dt.float32
BF16 = mybir.dt.bfloat16
F16 = mybir.dt.float16
I32 = mybir.dt.int32
U32 = mybir.dt.uint32
ACT = mybir.ActivationFunctionType
ALU = mybir.AluOpType
AX = mybir.AxisListType
ds = bass.ds

P = 128
B = 8
TOK = 256
N = B * TOK
NT = N // P
TPB = TOK // P
CTX = 512
H = 16
D = P // H
J = H // 2
PARTS = 3
SLOTS = 6
QROWS = SLOTS * D
AUG = QROWS + PARTS
PVC = PARTS * (D + 1)
EPS = 1e-5
E_GATED = 8
HID = 512
GATED_COLS = 2 * HID + 4 * P
E3 = 64
TABLE = 128 * P
ROUTED_SCALE = 2.5
L0_AT = E_GATED * GATED_COLS
ZERO_AT = L0_AT + 2 * 10 * P + 16
IOTA_AT, TRI_AT, PART_AT, BEFORE_AT, CONSTS = 0, 64, 192, 193, 209


class Count:

    def __init__(self, eng, sem, base=0):
        self.eng, self.sem, self.base, self.n = eng, sem, base, 0

    def add(self, ins):
        ins.then_inc(self.sem, 1)
        self.n += 1

    def wait(self):
        self.eng.wait_ge(self.sem, self.base + self.n)

    def link(self, ins):
        self.add(ins)
        self.wait()


class Core:

    def __init__(self, nc, ctx):
        self.nc, self.ctx = nc, ctx
        self.x = self.sb("x", [P, NT + TPB, P], F32)
        self.xn = self.sb("xn", [P, NT, P], F32)
        self.xnT = self.sb("xnT", [P, N], F32)
        self.wa = self.sb("wa", [P, 64 * 256], F32)
        self.wb = self.sb("wb", [P, 8 * 1536], F32)
        self.ident = self.sb("ident", [P, P], F32)
        self.ident_bf = self.sb("ident_bf", [P, P], BF16)
        self.ones = self.sb("ones", [P, P], F32)
        self.stats = self.sb("stats", [P, NT, 6], F32)
        self.mean_var = self.sb("mean_var", [P, NT, 2], F32)
        self.std = self.sb("std", [P, NT], F32)
        self.rstd = self.sb("rstd", [P, NT], F32)
        self.ctx_sum = self.sb("ctx_sum", [P, B], F32)
        self.const = self.sb("const", [P, CONSTS], F32)
        self.w0_in, self.w1_in, self.w2_in, self.w3_in = (self.sem(f"w{n}_in") for n in range(4))
        self.rows_zero = self.sem("rows_zero")
        self.scattered, self.back_in = self.sem("scattered"), [self.sem(f"back_in{k}") for k in range(8)]
        self.rows_in = nc.dram_tensor("rows_in", [TABLE, P], F32)
        self.bank = [ctx.enter_context(nc.psum_tensor(f"bank{i}", [P, 512], F32)) for i in range(8)]

    def sb(self, name, shape, dt):
        return self.ctx.enter_context(self.nc.sbuf_tensor(name, shape, dt))

    def sem(self, name):
        return self.ctx.enter_context(self.nc.semaphore(name))


class Phase:

    def __init__(self, c, tag):
        self.c, self.tag, self.ctx, self.sems = c, tag, ExitStack(), []

    def __enter__(self):
        self.ctx.__enter__()
        return self

    def sb(self, name, shape, dt):
        return self.ctx.enter_context(self.c.nc.sbuf_tensor(self.tag + name, shape, dt))

    def sem(self, name):
        s = self.ctx.enter_context(self.c.nc.semaphore(self.tag + name))
        self.sems.append(s)
        return s

    def __exit__(self, *error):
        if error[0] is None:
            with self.c.nc.Block() as block:
                @block.sync
                def _(sp):
                    numbers = sorted(s.num for s in self.sems)
                    while numbers:
                        first = last = numbers.pop(0)
                        while numbers and numbers[0] == last + 1:
                            last = numbers.pop(0)
                        sp.sem_clear(range(first, last + 1))
        return self.ctx.__exit__(*error)


def need(eng, sem, n):
    if not isinstance(n, int) or n > 0:
        eng.wait_ge(sem, n)


def start_phase(c, arg):
    nc = c.nc
    loaded, const, moved = c.sem("x_loaded"), c.sem("const_ready"), c.sem("const_copied")
    with nc.Block() as block:
        @block.sync
        def _(sp):
            sp.dma_start(c.x[:, TPB:, :], arg["x"].rearrange("b (t p) d -> p (b t) d", p=P)).then_inc(loaded, 16)
            sp.dma_start(c.const[:, :], arg["const"]).then_inc(loaded, 16)
            sp.dma_start(c.wa[:, L0_AT:ZERO_AT], arg["f0_w"]).then_inc(c.w0_in, 16)
            sp.wait_ge(loaded, 32)

        @block.gpsimd
        def _(pool):
            nc.gpsimd.memset(c.ident[:, :], 0.0).then_inc(const, 1)
            pool.wait_ge(const, 1)
            nc.gpsimd.affine_select(out=c.ident[:, :], in_=c.ident[:, :], compare_op=ALU.not_equal, fill=1.0,
                                    base=0, pattern=[[-1, P]], channel_multiplier=1).then_inc(const, 1)

        @block.vector
        def _(dve):
            nc.vector.memset(c.ones[:, :], 1.0)
            nc.vector.memset(c.x[:, 0:TPB, :], 0.0)
            nc.vector.memset(c.wa[:, ZERO_AT:ZERO_AT + 1024], 0.0)
            dve.wait_ge(const, 2)
            nc.vector.tensor_copy(c.ident_bf[:, :], c.ident[:, :]).then_inc(moved, 1)


def norm_phase(c, tag):
    nc = c.nc
    with Phase(c, tag) as ph:
        stat, var, std, xn_ready, turned, kept = (ph.sem(n) for n in ("_stats", "_var", "_std", "_xn", "_turned", "_kept"))
        norm_block(c, stat, var, std, xn_ready, turned, kept)


def norm_block(c, stat, var, std, xn_ready, turned, kept):
    nc = c.nc
    with nc.Block() as block:
        @block.vector
        def _(dve):
            for t in range(NT):
                nc.vector.bn_stats(c.stats[:, t, :], c.x[:, TPB + t, :]).then_inc(stat, 1)
            for t in range(NT):
                dve.wait_ge(stat, t + 1)
                nc.vector.bn_aggr(c.mean_var[:, t, :], c.stats[:, t, :]).then_inc(stat, 1)
            dve.wait_ge(stat, 2 * NT)
            nc.vector.tensor_scalar(c.rstd[:, :], c.mean_var[:, :, 1], EPS, None, ALU.add).then_inc(var, 1)
            dve.wait_ge(std, 1)
            nc.vector.reciprocal(c.rstd[:, :], c.std[:, :]).then_inc(var, 1)
            dve.wait_ge(var, 2)
            for t in range(NT):
                nc.vector.tensor_scalar(c.xn[:, t, :], c.x[:, TPB + t, :], c.mean_var[:, t, 0:1],
                                        c.rstd[:, t:t + 1], ALU.subtract, ALU.mult).then_inc(xn_ready, 1)

        @block.scalar
        def _(act):
            act.wait_ge(var, 1)
            nc.scalar.activation(c.std[:, :], c.rstd[:, :], ACT.Sqrt).then_inc(std, 1)
            for q in range(NT // 4):
                act.wait_ge(turned, q + 1)
                nc.scalar.copy(c.xnT[:, 512 * q:512 * q + 512], c.bank[q % 4][:, :]).then_inc(kept, 1)

        @block.tensor
        def _(pe):
            for t in range(NT):
                pe.wait_ge(xn_ready, t + 1)
                last = nc.tensor.transpose(c.bank[t // 4][:, P * (t % 4):P * (t % 4) + P], c.xn[:, t, :], c.ident[:, :])
                if t % 4 == 3:
                    last.then_inc(turned, 1)


def background(c, layer, arg, sp, i):
    if layer == 0:
        cols, rows = L0_AT // 8, TABLE // 8
        sp.dma_start(c.wa[:, ds(cols * i, cols)], arg["f1_w"][:, ds(cols * i, cols)]).then_inc(c.w1_in, 16)
        zeros = c.wa[:, ZERO_AT:ZERO_AT + 1024].unsqueeze(1).to_broadcast([P, rows // 1024, 1024])
        sp.dma_start(c.rows_in[ds(rows * i, rows), :].rearrange("(p n r) d -> p n (r d)", p=P, r=8), zeros).then_inc(c.rows_zero, 16)
    else:
        cols = 2 * P * E3 // 8
        sp.dma_start(c.wa[:, ds(cols * i, cols)], arg["f3_w"][:, ds(cols * i, cols)]).then_inc(c.w3_in, 16)


def attention_phase(c, layer, arg):
    nc = c.nc
    causal = layer == 2
    keys = 2 * P if causal else CTX
    kt_n = keys // P
    NA = NB = 1 if causal else 2
    SPAN = 384 if causal else 1024
    scale = float(D) ** -0.5
    tag = f"a{layer}_"
    with Phase(c, tag) as ph:
        sb, sem = ph.sb, ph.sem
        w = sb("w", [P, 4, P], F32)
        ctxT = sb("ctxT", [P, 2, CTX], F32)
        k_full = sb("k_full", [P, keys], F32)
        q_full = sb("q_full", [P, TOK], F32)
        v_full = sb("v_full", [P, kt_n, P], F32)
        k_part = sb("k_part", [P, PARTS, keys], BF16)
        q_part = sb("q_part", [P, PARTS, TOK], BF16)
        KS = sb("KS", [P, 2, J, keys], BF16)
        QS = sb("QS", [P, 2, J, TOK], BF16)
        V = sb("V", [P, 2, kt_n, H, PVC], BF16)
        neg_max = sb("neg_max", [P, 2, TPB, H // 2], F32)
        m_part = sb("m_part", [P, 2, TPB, 2, PARTS, 4], BF16)
        m_rest = sb("m_rest", [P, 2, TPB, 8], F32)
        m_rows = sb("m_rows", [2 * PARTS * 4, 2, TOK], BF16)
        E = sb("E", [P, 2, SPAN], F32)
        E1 = sb("E1", [P, 2, SPAN], F16)
        E2 = sb("E2", [P, 2, SPAN], F16)
        heads = sb("heads", [P, TPB, H, D + 1], F32)
        rsum = sb("rsum", [P, TPB, H], F32)
        attn = sb("attn", [P, TPB, P], F32)
        attnT = sb("attnT", [P, TOK], F32)
        k_dram = nc.dram_tensor(tag + "k_dram", [2, SLOTS, P, keys], BF16)
        q_dram = nc.dram_tensor(tag + "q_dram", [2, SLOTS, P, TOK], BF16)
        a_bank, b_bank, o_bank, misc, m_bank = c.bank[0:2], c.bank[2:4], c.bank[4:6], c.bank[6], c.bank[7]
        bfview = c.wb[:, :].bitcast(BF16)
        if causal:
            bias_qk = sb("bias_qk", [P, 2], F32)
            bias_q = sb("bias_q", [P, 1], F32)
            bias_row = sb("bias_row", [1, 2, P], F32)
            lora_a = sb("lora_a", [16, 3, P], F32)
            lora_b = sb("lora_b", [16, 4, P], F32)
            tri = sb("tri", [P, 2, P], BF16)
            tri_f = sb("tri_f", [P, 2, P], F32)
        else:
            mask_q = bfview[:, 0:3072].rearrange("p (m t k) -> p m t k", m=PARTS, t=TPB)
            mask_k = bfview[:, 3072:6144].rearrange("p (m t k) -> p m t k", m=PARTS, t=kt_n)
            mask_f = c.wb[:, 6144:8192].rearrange("p (m k) -> p m k", m=2)
            any_mask = sb("any_mask", [P, 4], F32)
            any_mask_i = sb("any_mask_i", [P, 1], I32)

        LOADS = 16 * (8 if causal else 6)
        SETUP = 6 if causal else 11
        ANY_MASK = 6
        bias_scaled = sem("bias_scaled")
        loaded = sem("loaded")
        ctx_in = [sem(f"ctx_in{p}") for p in range(2)]
        setup, setup_pool = sem("setup"), sem("setup_pool")
        lora_done = sem("lora_done")
        proj_k, proj_q, proj_v = sem("proj_k"), sem("proj_q"), sem("proj_v")
        full_k, full_q, full_v = sem("full_k"), sem("full_q"), sem("full_v")
        parts_k, parts_q, parts_v = sem("parts_k"), sem("parts_q"), sem("parts_v")
        pool_step = sem("pool_step")
        out_k, out_q = sem("out_k"), sem("out_q")
        stack = [sem(f"stack{p}") for p in range(2)]
        logits_a, max_done = sem("logits_a"), sem("max_done")
        parts_m, turned_m, rows_m = sem("parts_m"), sem("turned_m"), sem("rows_m")
        aug = [[sem(f"aug{p}{g}") for g in range(2)] for p in range(2)]
        logits_b, exp_done = sem("logits_b"), sem("exp_done")
        e1_done, e2_done, pv_done = sem("e1_done"), sem("e2_done"), sem("pv_done")
        norm_step, o_free, norm_done = sem("norm_step"), sem("o_free"), sem("norm_done")
        turned_o, kept_o, out_o, x_done = sem("turned_o"), sem("kept_o"), sem("out_o"), sem("x_done")
        summed = sem("summed")

        START = {max_done: 3, parts_m: 2, turned_m: 2, rows_m: 1, exp_done: 2, e1_done: 2, e2_done: 2, pv_done: 17,
                 o_free: 2, norm_done: 1, parts_k: 1, parts_q: 1, parts_v: 1, turned_o: 1, out_o: 1, out_k: 16, out_q: 16,
                 aug[0][0]: 16, aug[0][1]: 16, aug[1][0]: 16, aug[1][1]: 16}

        def reach(eng, s, n):
            eng.wait_ge(s, START.get(s, 0) + n)

        def head(h):
            return h // 2, h % 2, 64 * (h % 2)

        def logits_slot(bb, p, h):
            if h < LAG:
                return bb, p, H - LAG + h
            return bb + p, 1 - p, h - LAG

        LAG = 4
        STEP_LINKS = 3 * 5
        FIRST_LINKS = 3 * 6

        with nc.Block() as block:
            @block.sync
            def _(sp):
                def load_ctx(bb, p):
                    sp.dma_start(ctxT[:, p, :], arg["ctxT"][:, ds(2 * bb + p, 1), :].rearrange("d o k -> d (o k)")).then_inc(ctx_in[p], 16)

                def parts_out(bb, p, stacked=None):
                    b = 2 * bb + p
                    reach(sp, parts_k, b + 1)
                    if stacked is not None:
                        sp.wait_ge(stack[p], stacked)
                    for first, n, part in ((0, 3, 0), (3, 2, 1), (5, 1, 2)):
                        sp.dma_start(k_dram[p, first:first + n].rearrange("s r k -> r s k"),
                                     k_part[:, part:part + 1, :].to_broadcast([P, n, keys])).then_inc(out_k, 16)
                    reach(sp, parts_q, b + 1)
                    for first, n in ((0, 3), (3, 2), (5, 1)):
                        sp.dma_start(q_dram[p, first:first + n].rearrange("s r k -> r s k"),
                                     q_part[:, 0:n, :]).then_inc(out_q, 16)

                def stack_in(bb, p):
                    b = 2 * bb + p
                    reach(sp, out_k, 48 * (b + 1))
                    reach(sp, out_q, 48 * (b + 1))
                    for par in range(2):
                        rows = slice(64 * par, 64 * par + 64)
                        dst = slice(64 * par, 64 * par + QROWS)
                        sp.dma_start(KS[dst, p, :, :], k_dram[p, :, rows, :].rearrange("s (d j) k -> s d (j k)", d=D)).then_inc(stack[p], 16)
                        sp.dma_start(QS[dst, p, :, :], q_dram[p, :, rows, :].rearrange("s (d j) k -> s d (j k)", d=D)).then_inc(stack[p], 16)

                def aug_in(bb, p, g):
                    reach(sp, rows_m, 2 * (2 * bb + p) + g + 1)
                    for par in range(2):
                        sp.dma_start(QS[64 * par + QROWS:64 * par + AUG, p, 4 * g:4 * g + 4, :],
                                     m_rows[12 * par:12 * par + 12, g, :]).then_inc(aug[p][g], 16)

                if causal:
                    for n, name in enumerate(("wq", "wk", "wv", "wp")):
                        sp.dma_start(w[:, n, :], arg["a2_" + name]).then_inc(loaded, 16)
                    sp.dma_start(bias_qk[:, :], arg["a2_bias_qk"]).then_inc(loaded, 16)
                    sp.dma_start(bias_row[:, :, :], arg["a2_bias_row"]).then_inc(loaded, 16)
                    sp.dma_start(lora_a[:, :, :], arg["a2_lora_a"]).then_inc(loaded, 16)
                    sp.dma_start(lora_b[:, :, :], arg["a2_lora_b"]).then_inc(loaded, 16)
                else:
                    for n, name in enumerate(("wq", "wk", "wv", "wo")):
                        sp.dma_start(w[:, n, :], arg["a0_" + name]).then_inc(loaded, 16)
                    sp.dma_start(mask_f[:, 0, :].rearrange("q (t k) -> q t k", t=TPB), arg["mask"].rearrange("(t q) k -> q t k", t=TPB)).then_inc(loaded, 16)
                    sp.dma_start(mask_f[:, 1, :].rearrange("k (t q) -> k t q", t=kt_n), arg["maskT"].rearrange("(t k) q -> k t q", t=kt_n)).then_inc(loaded, 16)
                load_ctx(0, 0)
                load_ctx(0, 1)
                for p in range(2):
                    parts_out(0, p)
                    if p == 0:
                        reach(sp, setup, SETUP)
                    stack_in(0, p)
                aug_in(0, 0, 0)

                def step(bb, p, more=True, last=False):
                    i = 2 * bb + p
                    aug_in(bb, p, 1)
                    background(c, layer, arg, sp, i)
                    if more:
                        reach(sp, proj_v, i + 1)
                        if not causal:
                            reach(sp, summed, i + 1)
                        load_ctx(bb + 1, p)
                        parts_out(bb + 1, p, stacked=64 * bb + 64)
                    if not last:
                        aug_in(bb + p, 1 - p, 0)
                    if more:
                        reach(sp, logits_b, NB * H * (i + 1))
                        stack_in(bb + 1, p)

                with sp.Fori(0, 3) as bb:
                    for p in range(2):
                        step(bb, p)
                step(3, 0, more=False)
                step(3, 1, more=False, last=True)

            @block.gpsimd
            def _(pool):
                def one(like):
                    ap = c.ones[:, 0:1]
                    for _ in range(len(like.shape) - 2):
                        ap = ap.unsqueeze(2)
                    return ap.to_broadcast(list(like.shape))

                def split(chain, full, parts, done):
                    chain.link(nc.gpsimd.tensor_tensor(parts[0], full, one(full), ALU.mult))
                    chain.link(nc.gpsimd.tensor_tensor(full, full, parts[0], ALU.subtract))
                    chain.link(nc.gpsimd.tensor_tensor(parts[1], full, one(full), ALU.mult))
                    nc.gpsimd.tensor_tensor(parts[2], full, parts[1], ALU.subtract).then_inc(done, 1)

                def split_k(chain, b):
                    reach(pool, full_k, b + 1)
                    reach(pool, out_k, 48 * b)
                    split(chain, k_full[:, :], [k_part[:, m, :] for m in range(PARTS)], parts_k)

                def split_q(chain, b):
                    reach(pool, full_q, b + 1)
                    reach(pool, out_q, 48 * b)
                    split(chain, q_full[:, :], [q_part[:, m, :] for m in range(PARTS)], parts_q)

                def split_v(chain, b, p):
                    reach(pool, full_v, b + 1)
                    reach(pool, pv_done, H * (b - 1))
                    full = v_full[:, :, :].rearrange("k t (h d) -> k t h d", h=H)
                    split(chain, full, [V[:, p, :, :, (D + 1) * m:(D + 1) * m + D] for m in range(PARTS)], parts_v)

                def split_max(chain, b, g):
                    reach(pool, max_done, 2 * (H * b + 8 * g + 8))
                    reach(pool, turned_m, 2 * (b - 1) + g + 1)
                    parts = [m_part[:, g, :, :, m, :] for m in range(PARTS)]
                    neg = neg_max[:, g, :, :].rearrange("q t (r j) -> q t r j", r=2)
                    rest = m_rest[:, g, :, :].rearrange("q t (r j) -> q t r j", r=2)
                    chain.link(nc.gpsimd.tensor_tensor(parts[0], neg, one(neg), ALU.mult))
                    chain.link(nc.gpsimd.tensor_tensor(rest, neg, parts[0], ALU.subtract))
                    chain.link(nc.gpsimd.tensor_tensor(parts[1], rest, one(rest), ALU.mult))
                    nc.gpsimd.tensor_tensor(parts[2], rest, parts[1], ALU.subtract).then_inc(parts_m, 1)

                def residual(b, h):
                    n = H * b + h
                    reach(pool, e1_done, n + 1)
                    reach(pool, pv_done, n - 1)
                    nc.gpsimd.tensor_tensor(E2[:, h % 2, :], E[:, h % 2, :], E1[:, h % 2, :], ALU.subtract).then_inc(e2_done, 1)

                if causal:
                    nc.gpsimd.memset(tri_f[:, :, :], 0.0).then_inc(setup_pool, 1)
                    pool.wait_ge(setup_pool, 1)
                    nc.gpsimd.affine_select(out=tri_f[:, 0, :], in_=tri_f[:, 0, :], compare_op=ALU.is_ge, fill=-1e30,
                                            base=0, pattern=[[-1, P]], channel_multiplier=1).then_inc(setup_pool, 1)
                    nc.gpsimd.affine_select(out=tri_f[:, 1, :], in_=tri_f[:, 1, :], compare_op=ALU.is_ge, fill=-1e30,
                                            base=0, pattern=[[1, P]], channel_multiplier=-1).then_inc(setup_pool, 1)
                else:
                    pool.wait_ge(setup, ANY_MASK)
                    nc.gpsimd.partition_all_reduce(any_mask[:, 2:3], any_mask[:, 1:2], P, bass.bass_isa.ReduceOp.max).then_inc(setup_pool, 1)
                chain = Count(pool, pool_step)
                for b in range(2):
                    split_k(chain, b)
                    split_q(chain, b)
                split_v(chain, 0, 0)
                split_max(chain, 0, 0)
                residual(0, 0)
                assert chain.n == FIRST_LINKS

                def step(bb, p, more=True, last=False):
                    i = 2 * bb + p
                    chain = Count(pool, pool_step, FIRST_LINKS + STEP_LINKS * i)
                    if not more and p:
                        chain.base -= 6
                    for h in range(1, H + 1):
                        if h < H:
                            residual(i, h)
                        elif not last:
                            residual(i + 1, 0)
                        if h == LAG - 1:
                            split_max(chain, i, 1)
                        if h == 7 and more:
                            split_k(chain, i + 2)
                        if h == 8 and more:
                            split_q(chain, i + 2)
                        if h == 10 and not last:
                            split_v(chain, i + 1, 1 - p)
                        if h == LAG + 7 and not last:
                            split_max(chain, i + 1, 0)
                    assert chain.n == (STEP_LINKS if more else 3 if last else 9)

                with pool.Fori(0, 3) as bb:
                    for p in range(2):
                        step(bb, p)
                step(3, 0, more=False)
                step(3, 1, more=False, last=True)

            @block.vector
            def _(dve):
                for s, n in START.items():
                    dve.sem_inc(s, n)
                nc.vector.memset(KS[:, :, :, :], 1.0).then_inc(setup, 1)
                nc.vector.memset(V[:, :, :, :, :], 0.0).then_inc(setup, 1)
                nc.vector.memset(attn[:, :, :], 0.0).then_inc(setup, 1)
                dve.wait_ge(setup, 3)
                nc.vector.memset(V[:, :, :, :, D:D + 1], 1.0).then_inc(setup, 1)
                dve.wait_ge(loaded, LOADS)
                if causal:
                    dve.wait_ge(setup_pool, 3)
                    nc.vector.tensor_copy(tri[:, :, :], tri_f[:, :, :]).then_inc(setup, 1)
                    dve.wait_ge(lora_done, 1)
                    nc.vector.scalar_tensor_tensor(out=w[:, :, :], in0=misc[:, :].rearrange("p (n k) -> p n k", n=4), scalar=1.0 / 16.0,
                                                   in1=w[:, :, :], op0=ALU.mult, op1=ALU.add).then_inc(setup, 1)
                else:
                    nc.vector.tensor_scalar(E[:, :, :], mask_f[:, :, :], 0.0, None, ALU.not_equal).then_inc(setup, 1)
                    dve.wait_ge(setup, 5)
                    nc.vector.tensor_reduce(any_mask[:, 1:2], E[:, :, :], AX.XY, ALU.max).then_inc(setup, 1)
                    assert ANY_MASK == 6
                    chain = Count(dve, setup, 6)
                    flat = mask_f[:, :, :].rearrange("p m k -> p (m k)")
                    parts = [bfview[:, 0:6144].rearrange("p (l m k) -> p l m k", l=2, m=PARTS)[:, :, m, :] for m in range(PARTS)]
                    full = mask_f[:, :, :]
                    chain.link(nc.vector.tensor_copy(parts[0], full))
                    chain.link(nc.vector.tensor_tensor(full, full, parts[0], ALU.subtract))
                    chain.link(nc.vector.tensor_copy(parts[1], full))
                    chain.add(nc.vector.tensor_tensor(parts[2], full, parts[1], ALU.subtract))
                    dve.wait_ge(setup_pool, 1)
                    chain.add(nc.vector.tensor_copy(any_mask_i[:, :], any_mask[:, 2:3]))
                    assert chain.base + chain.n == SETUP

                def maximum(b, h):
                    n = H * b + h
                    j, par, _ = head(h)
                    g, col = j // 4, 4 * par + j % 4
                    if h % 8 == 0:
                        reach(dve, parts_m, 2 * (b - 1) + g + 1)
                    for t in range(TPB):
                        if causal:
                            reach(dve, logits_a, n + 1)
                            src = a_bank[h % 2][:, 0:P] if t == 0 else a_bank[h % 2][:, P:3 * P]
                        else:
                            reach(dve, logits_a, 2 * n + t + 1)
                            src = a_bank[t][:, :]
                        nc.vector.tensor_reduce(neg_max[:, g, t, col:col + 1], src, AX.X, ALU.max, negate=True).then_inc(max_done, 1)

                def first_part(b, h):
                    n = H * b + h
                    reach(dve, exp_done, NB * (n + 1))
                    reach(dve, pv_done, n - 1)
                    nc.vector.tensor_copy(E1[:, h % 2, :], E[:, h % 2, :]).then_inc(e1_done, 1)

                def normalise(b, links):
                    reach(dve, pv_done, H * (b + 1))
                    for t in range(TPB):
                        nc.vector.tensor_reduce(heads[:, t, :, :], o_bank[t][:, 0:H * PVC].rearrange("q (h m c) -> q h c m", h=H, m=PARTS),
                                                AX.X, ALU.add).then_inc(o_free, 1)
                    reach(dve, o_free, 2 * (b + 1))
                    nc.vector.reciprocal(rsum[:, :, :], heads[:, :, :, D]).then_inc(norm_step, 1)
                    reach(dve, norm_step, b + 1)
                    reach(dve, turned_o, b + 1)
                    nc.vector.tensor_tensor(attn[:, :, :].rearrange("q t (h d) -> q t h d", h=H), heads[:, :, :, 0:D],
                                            rsum[:, :, :].unsqueeze(3).to_broadcast([P, TPB, H, D]), ALU.mult).then_inc(norm_done, 1)

                def add_to_x(b1):
                    reach(dve, out_o, b1 + 1)
                    xs = c.x[:, ds(TPB * b1, TPB), :]
                    nc.vector.tensor_tensor(xs, xs, misc[:, 0:TOK].rearrange("q (t d) -> q t d", t=TPB), ALU.add).then_inc(x_done, 1)

                def sum_ctx(bb, p):
                    dve.wait_ge(ctx_in[p], 16 * (bb + 1))
                    nc.vector.tensor_reduce(c.ctx_sum[:, ds(2 * bb + p, 1)], ctxT[:, p, :], AX.X, ALU.add).then_inc(summed, 1)

                if not causal:
                    sum_ctx(0, 0)
                    sum_ctx(0, 1)
                for h in range(H - LAG + 1):
                    maximum(0, h)
                first_part(0, 0)

                def step(bb, p, more=True, last=False):
                    i = 2 * bb + p
                    for h in range(1, H + 1):
                        if h < H:
                            if h < LAG or not last:
                                _, _, ah = logits_slot(bb, p, h)
                                maximum(i if h < LAG else i + 1, ah)
                            first_part(i, h)
                        else:
                            if not last:
                                maximum(i + 1, H - LAG)
                                first_part(i + 1, 0)
                            normalise(i, None)
                        if h == 3:
                            add_to_x(i)
                        if h == 8 and more and not causal:
                            sum_ctx(bb + 1, p)

                with dve.Fori(0, 3) as bb:
                    for p in range(2):
                        step(bb, p)
                step(3, 0, more=False)
                step(3, 1, more=False, last=True)
                add_to_x(B)

            @block.scalar
            def _(act):
                def exps(b, h):
                    n = H * b + h
                    for u in range(NB):
                        reach(act, logits_b, NB * n + u + 1)
                        if u == 0:
                            reach(act, e2_done, n - 1)
                        if causal:
                            nc.scalar.activation(E[:, h % 2, :], b_bank[h % 2][:, 0:SPAN], ACT.Exp).then_inc(exp_done, 1)
                        else:
                            nc.scalar.activation(E[:, h % 2, 512 * u:512 * u + 512], b_bank[u][:, :], ACT.Exp).then_inc(exp_done, 1)

                def keep_k(b):
                    reach(act, proj_k, b + 1)
                    reach(act, parts_k, b)
                    bias = bias_qk[:, 1:2] if causal else 0.0
                    nc.scalar.activation(k_full[:, :], misc[:, 0:keys], ACT.Identity, bias=bias).then_inc(full_k, 1)

                def keep_q(b):
                    reach(act, proj_q, b + 1)
                    reach(act, parts_q, b)
                    bias = bias_q[:, :] if causal else 0.0
                    nc.scalar.activation(q_full[:, :], misc[:, 0:TOK], ACT.Identity, bias=bias, scale=scale).then_inc(full_q, 1)

                def keep_v(b):
                    reach(act, proj_v, b + 1)
                    reach(act, parts_v, b)
                    nc.scalar.copy(v_full[:, :, :], misc[:, 0:keys].rearrange("k (t c) -> k t c", t=kt_n)).then_inc(full_v, 1)

                def keep_max(b, g, other, count):
                    reach(act, turned_m, 2 * b + g + 1)
                    reach(act, aug[other][g], 32 * count)
                    nc.scalar.copy(m_rows[:, g, :], m_bank[:, :].bitcast(BF16)[0:2 * PARTS * 4, TOK * g:TOK * g + TOK]).then_inc(rows_m, 1)

                def keep_o(b1):
                    reach(act, turned_o, b1 + 1)
                    reach(act, out_o, b1)
                    nc.scalar.copy(attnT[:, :], misc[:, 0:TOK]).then_inc(kept_o, 1)

                if causal:
                    act.wait_ge(loaded, LOADS)
                    nc.scalar.mul(bias_q[:, :], bias_qk[:, 0:1], scale).then_inc(bias_scaled, 1)
                    act.wait_ge(bias_scaled, 1)
                for b in range(2):
                    keep_k(b)
                    keep_q(b)
                keep_v(0)
                keep_max(0, 0, 1, 0)
                exps(0, 0)

                def step(bb, p, more=True, last=False):
                    i = 2 * bb + p
                    for h in range(1, H + 1):
                        if h < H:
                            exps(i, h)
                        elif not last:
                            exps(i + 1, 0)
                        if h == 2:
                            keep_o(i)
                        if h == LAG:
                            keep_max(i, 1, 1 - p, bb + p)
                        if h == 6 and more:
                            keep_k(i + 2)
                        if h == 7 and more:
                            keep_q(i + 2)
                        if h == 9 and not last:
                            keep_v(i + 1)
                        if h == LAG + 8 and not last:
                            keep_max(i + 1, 0, p, bb + 1)

                with act.Fori(0, 3) as bb:
                    for p in range(2):
                        step(bb, p)
                step(3, 0, more=False)
                step(3, 1, more=False, last=True)
                keep_o(B)

            @block.tensor
            def _(pe):
                def project_k(bb, p):
                    pe.wait_ge(ctx_in[p], 16 * (bb + 1))
                    nc.tensor.matmul(misc[:, 0:keys], w[:, 1, :], ctxT[:, p, 0:keys], start=True, stop=True).then_inc(proj_k, 1)

                def project_q(b):
                    nc.tensor.matmul(misc[:, 0:TOK], w[:, 0, :], c.xnT[:, ds(TOK * b, TOK)], start=True, stop=True).then_inc(proj_q, 1)

                def project_v(p):
                    for t in range(kt_n):
                        out = misc[:, P * t:P * t + P]
                        last = nc.tensor.matmul(out, ctxT[:, p, P * t:P * t + P], w[:, 2, :], start=True, stop=not causal)
                        if causal:
                            last = nc.tensor.matmul(out, c.ones[0:1, :], bias_row[0:1, 0, :], start=False, stop=True)
                    last.then_inc(proj_v, 1)

                def logits_qk(masked, b, p, h, t):
                    n = H * b + h
                    j, _, row = head(h)
                    rows = slice(row, row + QROWS)
                    if causal:
                        reach(pe, max_done, 2 * n - 2)
                        for t in range(TPB):
                            out = a_bank[h % 2][:, P * t:P * t + P * (t + 1)]
                            nc.tensor.matmul(out, QS[rows, p, j, P * t:P * t + P], KS[rows, p, j, 0:P * (t + 1)], start=True, stop=True)
                            last = nc.tensor.matmul(a_bank[h % 2][:, 2 * P * t:2 * P * t + P], c.ident_bf[:, :], tri[:, 0, :],
                                                    start=False, stop=True, skip_group_check=True)
                        last.then_inc(logits_a, 1)
                        return
                    reach(pe, max_done, 2 * n + t - 1)
                    last = nc.tensor.matmul(a_bank[t][:, :], QS[rows, p, j, P * t:P * t + P], KS[rows, p, j, :], start=True, stop=True)
                    for m in range(PARTS if masked else 0):
                        last = nc.tensor.matmul(a_bank[t][:, :], c.ident_bf[:, :], mask_q[:, m, t, :], start=False, stop=True,
                                                skip_group_check=True)
                    last.then_inc(logits_a, 1)

                def logits_kq(masked, b, p, h, u):
                    n = NB * (H * b + h) + u
                    j, _, row = head(h)
                    rows = slice(row, row + AUG)
                    reach(pe, exp_done, n - 1)
                    if causal:
                        out = b_bank[h % 2]
                        for t in range(TPB):
                            nc.tensor.matmul(out[:, 2 * P * t:2 * P + P * t], KS[rows, p, j, P * t:P * t + P], QS[rows, p, j, P * t:TOK],
                                             start=True, stop=True)
                            last = nc.tensor.matmul(out[:, 2 * P * t:2 * P * t + P], c.ident_bf[:, :], tri[:, 1, :], start=False, stop=True,
                                                    skip_group_check=True)
                        last.then_inc(logits_b, 1)
                        return
                    for t in (2 * u, 2 * u + 1):
                        out = b_bank[u][:, TOK * (t % 2):TOK * (t % 2) + TOK]
                        last = nc.tensor.matmul(out, KS[rows, p, j, P * t:P * t + P], QS[rows, p, j, :], start=True, stop=True)
                        for m in range(PARTS if masked else 0):
                            last = nc.tensor.matmul(out, c.ident_bf[:, :], mask_k[:, m, t, :], start=False, stop=True,
                                                    skip_group_check=True)
                    last.then_inc(logits_b, 1)

                def weigh_v(b, p, h):
                    n = H * b + h
                    reach(pe, e2_done, n + 1)
                    if h == 0:
                        reach(pe, o_free, 2 * b)
                        reach(pe, parts_v, b + 1)
                    for t in range(TPB):
                        key_tiles = range(t + 1) if causal else range(kt_n)
                        for k in key_tiles:
                            at = P * (t + k) if causal else TOK * k + P * t
                            for e in (E1, E2):
                                last = nc.tensor.matmul(o_bank[t][:, PVC * h:PVC * h + PVC], e[:, h % 2, at:at + P], V[:, p, k, h, :],
                                                        start=(k == 0 and e is E1), stop=(k == key_tiles[-1] and e is E2))
                    last.then_inc(pv_done, 1)

                def turn_max(b, g):
                    reach(pe, parts_m, 2 * b + g + 1)
                    reach(pe, rows_m, 2 * b + g)
                    out = m_bank[:, :].bitcast(BF16)
                    for t in range(TPB):
                        last = nc.tensor.transpose(out[0:2 * PARTS * 4, TOK * g + P * t:TOK * g + P * t + P],
                                                   m_part[:, g, t, :, :, :].rearrange("q r m j -> q (r m j)"), c.ident_bf[:, :])
                    last.then_inc(turned_m, 1)

                def turn_o(b1):
                    reach(pe, norm_done, b1)
                    for t in range(TPB):
                        last = nc.tensor.transpose(misc[:, P * t:P * t + P], attn[:, t, :], c.ident[:, :])
                    last.then_inc(turned_o, 1)

                def project_o(b1):
                    reach(pe, kept_o, b1 + 1)
                    for t in range(TPB):
                        out = misc[:, P * t:P * t + P]
                        last = nc.tensor.matmul(out, attnT[:, P * t:P * t + P], w[:, 3, :], start=True, stop=not causal)
                        if causal:
                            last = nc.tensor.matmul(out, c.ones[0:1, :], bias_row[0:1, 1, :], start=False, stop=True)
                    last.then_inc(out_o, 1)

                def heads_together(masked, b, p, h, ab, ap, ah):
                    for u in range(2):
                        if u < NB and b is not None:
                            logits_kq(masked, b, p, h, u)
                        if u < NA and ab is not None:
                            logits_qk(masked, ab, ap, ah, u)

                def program(masked):
                    for p in range(2):
                        project_k(0, p)
                        reach(pe, full_k, p + 1)
                        project_q(p)
                        reach(pe, full_q, p + 1)
                    project_v(0)
                    pe.wait_ge(stack[0], 64)
                    for h in range(H - LAG):
                        heads_together(masked, None, None, None, 0, 0, h)
                        if h == 8:
                            turn_max(0, 0)
                    reach(pe, aug[0][0], 32)
                    heads_together(masked, 0, 0, 0, 0, 0, H - LAG)

                    def step(bb, p, more=True, last=False):
                        i = 2 * bb + p
                        for h in range(1, H + 1):
                            if h == LAG and not last:
                                pe.wait_ge(stack[1 - p], 64 * (bb + p + 1))
                            if h == 8:
                                reach(pe, aug[p][1], 32 * (bb + 1))
                            if h < H:
                                with_a = h < LAG or not last
                                _, ap, ah = logits_slot(bb, p, h)
                                heads_together(masked, i, p, h, (i if h < LAG else i + 1) if with_a else None, ap, ah)
                            elif not last:
                                reach(pe, aug[1 - p][0], 32 * (bb + p + 1))
                                heads_together(masked, i + 1, 1 - p, 0, i + 1, 1 - p, H - LAG)
                            weigh_v(i, p, h - 1)
                            if h == 2:
                                reach(pe, full_v, i + 1)
                                turn_o(i)
                            if h == 3:
                                project_o(i)
                            if h == LAG:
                                turn_max(i, 1)
                            if h == 6 and more:
                                reach(pe, x_done, i + 1)
                                project_k(bb + 1, p)
                            if h == 7 and more:
                                reach(pe, full_k, i + 3)
                                project_q(i + 2)
                            if h == 9 and not last:
                                if more:
                                    reach(pe, full_q, i + 3)
                                else:
                                    reach(pe, x_done, i + 1)
                                project_v(1 - p)
                            if h == LAG + 8 and not last:
                                turn_max(i + 1, 0)

                    with pe.Fori(0, 3) as bb:
                        for p in range(2):
                            step(bb, p)
                    step(3, 0, more=False)
                    step(3, 1, more=False, last=True)
                    reach(pe, x_done, B)
                    turn_o(B)
                    project_o(B)

                pe.wait_ge(loaded, LOADS)
                if causal:
                    for n, (a, b) in enumerate(((0, 0), (1, 1), (1, 2), (2, 3))):
                        last = nc.tensor.matmul(misc[:, P * n:P * n + P], lora_a[:, a, :], lora_b[:, b, :], start=True, stop=True)
                    last.then_inc(lora_done, 1)
                pe.wait_ge(setup, SETUP)
                if causal:
                    program(False)
                else:
                    masked = pe.value_load(any_mask_i[0:1, 0:1], min_val=0, max_val=1)
                    with pe.If(masked > 0):
                        program(True)
                    with pe.Else():
                        program(False)


CHUNK = 512
NC = N // CHUNK
TPC = CHUNK // P
E0 = 16
HID0 = 8 + 2


def dense_block(c, ph, up, gate, down, weighted, router, hidden):
    nc = c.nc
    tiles = len(up)
    order = list(range(weighted, tiles)) + list(range(weighted))
    r = ph.sb("relu", [P, 3, CHUNK], F32)
    prod = ph.sb("prod", [P, 2, CHUNK], F32)
    hT = hidden[:, 0:2 * tiles * CHUNK].rearrange("p (b i t) -> p b i t", b=2, i=tiles)
    up_bank, side_bank, down_bank = c.bank[0:2], c.bank[2:4], c.bank[4:6]
    sides = tiles if gate else weighted
    up_done, side_done, act_done, prod_done, h_done = (ph.sem(n) for n in ("up_done", "side_done", "act_done", "prod_done", "h_done"))
    down_done, x_done = ph.sem("down_done"), ph.sem("x_done")
    if gate:
        h_done = prod_done
    X_AT = 4

    def side_number(q, k):
        if gate:
            return tiles * q + k
        return None if order[k] >= weighted else weighted * q + k - (tiles - weighted)

    with nc.Block() as block:
        @block.sync
        def _(sp):
            router.loads(sp)

        @block.tensor
        def _(pe):
            def up_product(q, k):
                n, i, m = tiles * q + k, order[k], side_number(q, k)
                need(pe, act_done if not gate else prod_done, n - 1)
                rhs = c.xnT[:, CHUNK * q:CHUNK * q + CHUNK]
                nc.tensor.matmul(up_bank[n % 2][:, :], up[i], rhs, start=True, stop=True).then_inc(up_done, 1)
                if m is None:
                    return
                need(pe, act_done if gate else prod_done, m - 1)
                if gate:
                    nc.tensor.matmul(side_bank[m % 2][:, :], gate[i], rhs, start=True, stop=True).then_inc(side_done, 1)
                else:
                    lhsT, rows = router.scale_rows(i, q)
                    nc.tensor.matmul(side_bank[m % 2][:, :], lhsT, rows, start=True, stop=True).then_inc(side_done, 1)

            def down_product(q):
                pe.wait_ge(h_done, tiles * (q + 1))
                need(pe, x_done, q - 1)
                for t in range(TPC):
                    for i in range(tiles):
                        last = nc.tensor.matmul(down_bank[q % 2][:, P * t:P * t + P], hT[:, q % 2, i, P * t:P * t + P], down[i],
                                                start=(i == 0), stop=(i == tiles - 1))
                last.then_inc(down_done, 1)

            router.pe(pe)
            for q in range(NC):
                for k in range(tiles):
                    if q == 0 and k == tiles - weighted and not gate:
                        router.pe_weights(pe)
                    up_product(q, k)
                    if k == 1 and q:
                        down_product(q - 1)
            down_product(NC - 1)

        @block.scalar
        def _(act):
            router.act(act)
            for q in range(NC):
                for k in range(tiles):
                    n = tiles * q + k
                    if q == 0 and k == tiles - weighted and not gate:
                        router.act_weights(act)
                    if gate:
                        act.wait_ge(side_done, n + 1)
                        need(act, h_done, n - 2)
                        nc.scalar.activation(r[:, n % 3, :], side_bank[n % 2][:, :], ACT.Silu).then_inc(act_done, 1)
                    else:
                        act.wait_ge(up_done, n + 1)
                        need(act, h_done, n - 2)
                        nc.scalar.activation(r[:, n % 3, :], up_bank[n % 2][:, :], ACT.Relu).then_inc(act_done, 1)

        @block.vector
        def _(dve):
            def add_to_x(q):
                dve.wait_ge(down_done, q + 1)
                xs = c.x[:, TPB + TPC * q:TPB + TPC * (q + 1), :]
                nc.vector.tensor_tensor(xs, xs, down_bank[q % 2][:, :].rearrange("p (t d) -> p t d", t=TPC), ALU.add).then_inc(x_done, 1)

            router.dve(dve)
            for q in range(NC):
                for k in range(tiles):
                    n, m = tiles * q + k, side_number(q, k)
                    if k == min(X_AT, tiles - 1) and q:
                        add_to_x(q - 1)
                    if m is None:
                        continue
                    dve.wait_ge(act_done, n + 1)
                    if gate:
                        dve.wait_ge(up_done, n + 1)
                        need(dve, down_done, q - 1)
                        nc.vector.tensor_tensor(hT[:, q % 2, k, :], r[:, n % 3, :], up_bank[n % 2][:, :], ALU.mult).then_inc(prod_done, 1)
                    else:
                        dve.wait_ge(side_done, m + 1)
                        need(dve, h_done, n - 1)
                        nc.vector.tensor_tensor(prod[:, m % 2, :], r[:, n % 3, :], side_bank[m % 2][:, :], ALU.mult).then_inc(prod_done, 1)
            add_to_x(NC - 1)

        @block.gpsimd
        def _(pool):
            router.pool(pool)
            if not gate:
                for q in range(NC):
                    for k in range(tiles):
                        n, m = tiles * q + k, side_number(q, k)
                        need(pool, down_done, q - 1)
                        if m is None:
                            pool.wait_ge(act_done, n + 1)
                            first = r[:, n % 3, :]
                        else:
                            pool.wait_ge(prod_done, m + 1)
                            first = prod[:, m % 2, :]
                        nc.gpsimd.tensor_tensor(hT[:, q % 2, order[k], :], first, r[:, n % 3, :], ALU.mult).then_inc(h_done, 1)


class Router0:

    def __init__(self, c, ph, arg):
        self.c, self.arg = c, arg
        self.w = c.wa[:, L0_AT + 2 * HID0 * P:L0_AT + 2 * HID0 * P + E0]
        sb = ph.sb
        self.bias = sb("bias", [P, E0], F32)
        self.spread_f = sb("spread_f", [PARTS * E0, 8 * P], F32)
        self.spread = sb("spread", [PARTS * E0, 8 * P], BF16)
        self.scores = sb("scores", [P, NT, E0], F32)
        self.sc = sb("sc", [P, NT, E0], F32)
        self.pair = sb("pair", [P, 6, NT * 4], F32)
        self.group = sb("group", [P, NT, 4], F32)
        self.beats = sb("beats", [P, 2, NT, 4, 4], F32)
        self.rank = sb("rank", [P, NT, 4], F32)
        self.masked = sb("masked", [P, NT, E0], F32)
        self.top = sb("top", [P, NT, 8], F32)
        self.at = sb("at", [P, NT, 8], U32)
        self.at_f = sb("at_f", [P, NT, 4], F32)
        self.hot = sb("hot", [P, NT, 4, E0], F32)
        self.weight = sb("weight", [P, NT, E0], F32)
        self.den = sb("den", [P, NT], F32)
        self.part = sb("part", [P, NT, PARTS, E0], BF16)
        self.partT = sb("partT", [PARTS * E0, N], BF16)
        self.loaded, self.logits, self.scored = ph.sem("r_loaded"), ph.sem("r_logits"), ph.sem("r_scored")
        self.step, self.ready = ph.sem("r_step"), ph.sem("r_ready")
        self.turned, self.kept, self.copied = ph.sem("r_turned"), ph.sem("r_kept"), ph.sem("r_copied")

    def loads(self, sp):
        sp.dma_start(self.bias[:, :], self.arg["f0_bias"]).then_inc(self.loaded, 16)
        sp.dma_start(self.spread_f[:, :], self.arg["spread0"]).then_inc(self.loaded, 16)

    def pe(self, pe):
        nc, c = self.c.nc, self.c
        pe.wait_ge(c.w0_in, 16)
        for t in range(NT):
            last = nc.tensor.matmul(c.bank[7][:, E0 * t:E0 * t + E0], c.xnT[:, P * t:P * t + P], self.w, start=True, stop=True)
        last.then_inc(self.logits, 1)

    def pe_weights(self, pe):
        nc, c = self.c.nc, self.c
        pe.wait_ge(self.ready, 1)
        for t in range(NT):
            out = c.bank[6 + t // 8][:, :].bitcast(BF16)[0:PARTS * E0, P * (t % 8):P * (t % 8) + P]
            last = nc.tensor.transpose(out, self.part[:, t, :, :].rearrange("p m e -> p (m e)"), c.ident_bf[:, :])
            if t % 8 == 7:
                last.then_inc(self.turned, 1)
        pe.wait_ge(self.kept, 2)
        pe.wait_ge(self.copied, 1)

    def scale_rows(self, i, q):
        return self.spread[:, P * i:P * i + P], self.partT[:, CHUNK * q:CHUNK * q + CHUNK]

    def act(self, act):
        nc, c = self.c.nc, self.c
        act.wait_ge(self.logits, 1)
        nc.scalar.activation(self.scores[:, :, :], c.bank[7][:, 0:NT * E0].rearrange("p (t e) -> p t e", t=NT), ACT.Sigmoid).then_inc(self.scored, 1)

    def act_weights(self, act):
        nc, c = self.c.nc, self.c
        for half in range(2):
            act.wait_ge(self.turned, half + 1)
            nc.scalar.copy(self.partT[:, 1024 * half:1024 * half + 1024],
                           c.bank[6 + half][:, :].bitcast(BF16)[0:PARTS * E0, :]).then_inc(self.kept, 1)

    def pool(self, pool):
        pool.wait_ge(self.loaded, 32)
        self.c.nc.gpsimd.tensor_copy(self.spread[:, :], self.spread_f[:, :]).then_inc(self.copied, 1)

    def dve(self, dve):
        nc, c = self.c.nc, self.c
        v = nc.vector
        step = Count(dve, self.step)
        dve.wait_ge(self.loaded, 32)
        dve.wait_ge(self.scored, 1)
        step.link(v.tensor_tensor(self.sc[:, :, :], self.scores[:, :, :], self.bias[:, :].unsqueeze(1).to_broadcast([P, NT, E0]), ALU.add))
        a, b, cc, d = (self.sc[:, :, :].rearrange("p t (g m) -> p (t g) m", g=4)[:, :, m] for m in range(4))
        hi1, lo1, hi2, lo2, both, rest = (self.pair[:, m, :] for m in range(6))
        step.add(v.tensor_tensor(hi1, a, b, ALU.max))
        step.add(v.tensor_tensor(lo1, a, b, ALU.min))
        step.add(v.tensor_tensor(hi2, cc, d, ALU.max))
        step.link(v.tensor_tensor(lo2, cc, d, ALU.min))
        step.add(v.tensor_tensor(both, hi1, hi2, ALU.min))
        step.add(v.tensor_tensor(rest, lo1, lo2, ALU.max))
        step.link(v.tensor_tensor(hi1, hi1, hi2, ALU.max))
        step.link(v.tensor_tensor(both, both, rest, ALU.max))
        group = self.group[:, :, :]
        step.link(v.tensor_tensor(group.rearrange("p t g -> p (t g)"), hi1, both, ALU.add))
        mine = group.unsqueeze(3).to_broadcast([P, NT, 4, 4])
        other = group.unsqueeze(2).to_broadcast([P, NT, 4, 4])
        more, same = self.beats[:, 0, :, :, :], self.beats[:, 1, :, :, :]
        before = c.const[:, BEFORE_AT:BEFORE_AT + 16].rearrange("p (g h) -> p g h", g=4).unsqueeze(1).to_broadcast([P, NT, 4, 4])
        step.add(v.tensor_tensor(more, other, mine, ALU.is_gt))
        step.link(v.tensor_tensor(same, other, mine, ALU.is_ge))
        step.link(v.tensor_tensor(same, same, before, ALU.mult))
        step.link(v.tensor_tensor(more, more, same, ALU.max))
        step.link(v.tensor_reduce(self.rank[:, :, :], more, AX.X, ALU.add))
        step.link(v.tensor_scalar(self.rank[:, :, :], self.rank[:, :, :], 1.5, None, ALU.is_lt))
        step.link(v.tensor_tensor(self.masked[:, :, :].rearrange("p t (g m) -> p t g m", g=4), self.sc[:, :, :].rearrange("p t (g m) -> p t g m", g=4),
                                  self.rank[:, :, :].unsqueeze(3).to_broadcast([P, NT, 4, 4]), ALU.mult))
        for t in range(NT):
            step.add(v.max(self.top[:, t, :], self.masked[:, t, :]))
        step.wait()
        for t in range(NT):
            step.add(v.max_index(self.at[:, t, :], self.top[:, t, :], self.masked[:, t, :]))
        step.wait()
        step.link(v.tensor_copy(self.at_f[:, :, :], self.at[:, :, 0:4]))
        step.link(v.tensor_tensor(self.hot[:, :, :, :], c.const[:, IOTA_AT:IOTA_AT + E0].unsqueeze(1).unsqueeze(1).to_broadcast([P, NT, 4, E0]),
                                  self.at_f[:, :, :].unsqueeze(3).to_broadcast([P, NT, 4, E0]), ALU.is_equal))
        step.link(v.tensor_reduce(self.weight[:, :, :], self.hot[:, :, :, :].rearrange("p t k e -> p t e k"), AX.X, ALU.add))
        weight = self.weight[:, :, :]
        step.link(v.tensor_tensor(weight, weight, self.scores[:, :, :], ALU.mult))
        step.link(v.tensor_reduce(self.den[:, :], weight, AX.X, ALU.add))
        step.link(v.tensor_scalar(self.den[:, :], self.den[:, :], 1e-20, None, ALU.add))
        step.link(v.reciprocal(self.den[:, :], self.den[:, :]))
        step.link(v.scalar_tensor_tensor(out=weight, in0=weight, scalar=ROUTED_SCALE, in1=self.den[:, :].unsqueeze(2).to_broadcast([P, NT, E0]),
                                         op0=ALU.mult, op1=ALU.mult))
        part = [self.part[:, :, m, :] for m in range(PARTS)]
        step.link(v.tensor_copy(part[0], weight))
        step.link(v.tensor_tensor(weight, weight, part[0], ALU.subtract))
        step.link(v.tensor_copy(part[1], weight))
        v.tensor_tensor(part[2], weight, part[1], ALU.subtract).then_inc(self.ready, 1)


def layer0_ffn(c, arg):
    with Phase(c, "f0_") as ph:
        router = Router0(c, ph, arg)
        up = [c.wa[:, L0_AT + P * i:L0_AT + P * i + P] for i in range(HID0)]
        down = [c.wa[:, L0_AT + P * (HID0 + i):L0_AT + P * (HID0 + i) + P] for i in range(HID0)]
        dense_block(c, ph, up, None, down, 8, router, c.wb)


def layer1_attention(c, arg):
    nc = c.nc
    with Phase(c, "a1_") as ph:
        w = ph.sb("w", [P, 2, P], F32)
        bias = ph.sb("bias", [1, P], F32)
        one_hot = ph.sb("one_hot", [B, B, P], F32)
        mean = ph.sb("mean", [P, B], F32)
        rows = ph.sb("rows", [B, P], F32)
        loaded, mean_ready, rows_out, rows_ready, out_done = (ph.sem(n) for n in ("loaded", "mean", "rows_out", "rows_ready", "out_done"))
        with nc.Block() as block:
            @block.sync
            def _(sp):
                sp.dma_start(w[:, :, :], arg["a1_w"].rearrange("n p d -> p n d")).then_inc(loaded, 16)
                sp.dma_start(bias[:, :], arg["a1_bias"]).then_inc(loaded, 16)
                sp.dma_start(one_hot[:, :, :], arg["one_hot8"]).then_inc(loaded, 16)
                cols = E_GATED * GATED_COLS // 8
                for n in range(8):
                    sp.dma_start(c.wb[:, cols * n:cols * n + cols], arg["f2_w"][:, cols * n:cols * n + cols]).then_inc(c.w2_in, 16)

            @block.tensor
            def _(pe):
                pe.wait_ge(loaded, 48)
                pe.wait_ge(mean_ready, 1)
                nc.tensor.matmul(c.bank[7][0:B, 0:P], mean[:, :], w[:, 1, :], start=True, stop=False)
                nc.tensor.matmul(c.bank[7][0:B, 0:P], c.ones[0:1, 0:B], bias[:, :], start=False, stop=True).then_inc(rows_out, 1)
                pe.wait_ge(rows_ready, 1)
                for t in range(NT):
                    out = c.bank[t // 4][:, P * (t % 4):P * (t % 4) + P]
                    nc.tensor.matmul(out, c.xnT[:, P * t:P * t + P], w[:, 0, :], start=True, stop=False)
                    nc.tensor.matmul(out, one_hot[:, t // TPB, :], rows[:, :], start=False, stop=True).then_inc(out_done, 1)

            @block.scalar
            def _(act):
                nc.scalar.mul(mean[:, :], c.ctx_sum[:, :], 1.0 / CTX).then_inc(mean_ready, 1)
                act.wait_ge(rows_out, 1)
                nc.scalar.copy(rows[:, :], c.bank[7][0:B, 0:P]).then_inc(rows_ready, 1)

            @block.vector
            def _(dve):
                for q in range(NT // 4):
                    dve.wait_ge(out_done, 4 * (q + 1))
                    xs = c.x[:, TPB + 4 * q:TPB + 4 * q + 4, :]
                    nc.vector.tensor_tensor(xs, xs, c.bank[q][:, :].rearrange("p (t d) -> p t d", t=4), ALU.add)


class NoRouter:

    def __init__(self, c):
        self.c = c

    def pe(self, pe):
        pe.wait_ge(self.c.w1_in, 16 * 8)

    def loads(self, sp): pass
    def act(self, act): pass
    def dve(self, dve): pass
    def pool(self, pool): pass


def layer1_shared(c, arg):
    with Phase(c, "s1_") as ph:
        at = (E_GATED - 1) * GATED_COLS
        gate, up, down = ([c.wa[:, at + first + P * i:at + first + P * i + P] for i in range(4)] for first in (0, HID, 2 * HID))
        dense_block(c, ph, up, gate, down, 0, NoRouter(c), c.wa[:, L0_AT:])


def layer3_attention(c, arg):
    nc = c.nc
    KT = CTX // P
    with Phase(c, "a3_") as ph:
        sb, sem = ph.sb, ph.sem
        w = sb("w", [P, 4, P], F32)
        bias_qk = sb("bias_qk", [P, 2], F32)
        bias_q = sb("bias_q", [P, 1], F32)
        bias_vo = sb("bias_vo", [P, 2, P], F32)
        ctxT = sb("ctxT", [P, 2, CTX], F32)
        qT = sb("qT", [P, 2, TOK], F32)
        kT = sb("kT", [P, 2, CTX], F32)
        v = sb("v", [P, 2, KT, P], F32)
        neg_max = sb("neg_max", [P, 2, TPB], F32)
        total = sb("total", [P, 2, TPB], F32)
        inverse = sb("inverse", [P, 2, TPB], F32)
        prob = sb("prob", [P, 2, TPB, CTX], F32)
        probT = sb("probT", [P, KT, TOK], F32)
        headT = sb("headT", [P, TOK], F32)
        loaded, biased = sem("loaded"), sem("biased")
        ctx_in = [sem(f"ctx_in{p}") for p in range(2)]
        proj_q, proj_k, proj_v = sem("proj_q"), sem("proj_k"), sem("proj_v")
        full_q, full_k, full_v = sem("full_q"), sem("full_k"), sem("full_v")
        logits, max_done, exp_done = sem("logits"), sem("max_done"), sem("exp_done")
        turned, kept = sem("turned"), sem("kept")
        head_out, head_kept, out_done = sem("head_out"), sem("head_kept"), sem("out_done")
        inv_done, x_done, bias_added = sem("inv_done"), sem("x_done"), sem("bias_added")
        k_bank, q_bank, v_bank, l_bank, p_bank, o_bank = c.bank[0], c.bank[1], c.bank[2], c.bank[3:5], c.bank[5:7], c.bank[7]
        scale = float(P) ** -0.5

        def slots(eng, first, step, last):
            for b in first:
                step(b, b % 2, b // 2)
            with eng.Fori(1, 3) as g:
                for p in range(2):
                    step(2 * g + p, p, g)
            for b in last:
                step(b, b % 2, b // 2)

        with nc.Block() as block:
            @block.sync
            def _(sp):
                for n, name in enumerate(("wq", "wk", "wv", "wo")):
                    sp.dma_start(w[:, n, :], arg["a3_" + name]).then_inc(loaded, 16)
                sp.dma_start(bias_qk[:, :], arg["a3_bias_qk"]).then_inc(loaded, 16)
                sp.dma_start(bias_vo[:, :, :], arg["a3_bias_vo"]).then_inc(loaded, 16)

                def step(b, p, g):
                    need(sp, proj_k, b - 1)
                    need(sp, proj_v, b - 1)
                    sp.dma_start(ctxT[:, p, :], arg["ctxT"][:, ds(b, 1), :].rearrange("d o k -> d (o k)")).then_inc(ctx_in[p], 16)

                slots(sp, (0, 1), step, (6, 7))

            @block.tensor
            def _(pe):
                def project(b, p, g):
                    pe.wait_ge(ctx_in[p], 16 * g + 16)
                    need(pe, full_k, b)
                    nc.tensor.matmul(k_bank[:, :], w[:, 1, :], ctxT[:, p, :], start=True, stop=True).then_inc(proj_k, 1)
                    need(pe, full_q, b)
                    nc.tensor.matmul(q_bank[:, 0:TOK], w[:, 0, :], c.xnT[:, ds(TOK * b, TOK)], start=True, stop=True).then_inc(proj_q, 1)
                    need(pe, full_v, b)
                    for t in range(KT):
                        last = nc.tensor.matmul(v_bank[:, P * t:P * t + P], ctxT[:, p, P * t:P * t + P], w[:, 2, :], start=True, stop=True)
                    last.then_inc(proj_v, 1)

                def find_logits(b, p, g):
                    pe.wait_ge(full_q, b + 1)
                    pe.wait_ge(full_k, b + 1)
                    for t in range(TPB):
                        need(pe, exp_done, 2 * b + t - 1)
                        nc.tensor.matmul(l_bank[t][:, :], qT[:, p, P * t:P * t + P], kT[:, p, :], start=True, stop=True).then_inc(logits, 1)

                def turn(b, p, g):
                    for t in range(TPB):
                        pe.wait_ge(exp_done, 2 * b + t + 1)
                        need(pe, kept, 2 * b + t - 1)
                        for k in range(KT):
                            last = nc.tensor.transpose(p_bank[t][:, P * k:P * k + P], prob[:, p, t, P * k:P * k + P], c.ident[:, :])
                        last.then_inc(turned, 1)

                def weigh(b, p, g):
                    pe.wait_ge(kept, 2 * b + 2)
                    pe.wait_ge(full_v, b + 1)
                    need(pe, x_done, b)
                    for k in range(KT):
                        last = nc.tensor.matmul(o_bank[:, 0:TOK], v[:, p, k, :], probT[:, k, :], start=(k == 0), stop=(k == KT - 1))
                    last.then_inc(head_out, 1)

                def project_out(b, p, g):
                    pe.wait_ge(head_kept, b + 1)
                    for t in range(TPB):
                        last = nc.tensor.matmul(o_bank[:, TOK + P * t:TOK + P * t + P], headT[:, P * t:P * t + P], w[:, 3, :],
                                                start=True, stop=True)
                    last.then_inc(out_done, 1)

                def step(b, p, g):
                    turn(b, p, g)
                    if not isinstance(b, int) or b < B - 1:
                        project(b + 1, 1 - p, g + p)
                    weigh(b, p, g)
                    if not isinstance(b, int) or b < B - 1:
                        find_logits(b + 1, 1 - p, g + p)
                    project_out(b, p, g)

                pe.wait_ge(loaded, 96)
                project(0, 0, 0)
                find_logits(0, 0, 0)
                slots(pe, (0, 1), step, (6, 7))

            @block.scalar
            def _(act):
                def project(b, p, g):
                    act.wait_ge(proj_k, b + 1)
                    need(act, logits, 2 * b - 2)
                    nc.scalar.activation(kT[:, p, :], k_bank[:, :], ACT.Identity, bias=bias_qk[:, 1:2]).then_inc(full_k, 1)
                    act.wait_ge(proj_q, b + 1)
                    nc.scalar.activation(qT[:, p, :], q_bank[:, 0:TOK], ACT.Identity, bias=bias_q[:, :], scale=scale).then_inc(full_q, 1)

                def exps(b, p, g):
                    for t in range(TPB):
                        act.wait_ge(max_done, 2 * b + t + 1)
                        need(act, turned, 2 * b - 3 + t)
                        need(act, inv_done, b - 1)
                        nc.scalar.activation(prob[:, p, t, :], l_bank[t][:, :], ACT.Exp, bias=neg_max[:, p, t:t + 1],
                                             accum_out=total[:, p, t:t + 1]).then_inc(exp_done, 1)

                def step(b, p, g):
                    more = not isinstance(b, int) or b < B - 1
                    if more:
                        project(b + 1, 1 - p, g + p)
                    act.wait_ge(head_out, b + 1)
                    need(act, out_done, b)
                    nc.scalar.copy(headT[:, :], o_bank[:, 0:TOK]).then_inc(head_kept, 1)
                    if more:
                        exps(b + 1, 1 - p, g + p)

                act.wait_ge(loaded, 96)
                nc.scalar.mul(bias_q[:, :], bias_qk[:, 0:1], scale).then_inc(biased, 1)
                act.wait_ge(biased, 1)
                project(0, 0, 0)
                exps(0, 0, 0)
                slots(act, (0, 1), step, (6, 7))

            @block.vector
            def _(dve):
                def keep_v(b, p, g):
                    dve.wait_ge(proj_v, b + 1)
                    need(dve, head_out, b - 1)
                    nc.vector.tensor_tensor(v[:, p, :, :], v_bank[:, :].rearrange("p (t d) -> p t d", t=KT),
                                            bias_vo[:, 0:1, :].to_broadcast([P, KT, P]), ALU.add).then_inc(full_v, 1)

                def maxima(b, p, g):
                    for t in range(TPB):
                        dve.wait_ge(logits, 2 * b + t + 1)
                        nc.vector.tensor_reduce(neg_max[:, p, t:t + 1], l_bank[t][:, :], AX.X, ALU.max, negate=True).then_inc(max_done, 1)

                def step(b, p, g):
                    more = not isinstance(b, int) or b < B - 1
                    for t in range(TPB):
                        dve.wait_ge(turned, 2 * b + t + 1)
                        need(dve, head_out, b)
                        nc.vector.tensor_copy(probT[:, :, P * t:P * t + P], p_bank[t][:, :].rearrange("p (k q) -> p k q", k=KT)).then_inc(kept, 1)
                    nc.vector.reciprocal(inverse[:, p, :], total[:, p, :]).then_inc(inv_done, 1)
                    if more:
                        keep_v(b + 1, 1 - p, g + p)
                        maxima(b + 1, 1 - p, g + p)
                    dve.wait_ge(out_done, b + 1)
                    dve.wait_ge(inv_done, b + 1)
                    dve.wait_ge(bias_added, 1)
                    for t in range(TPB):
                        xs = c.x[:, ds(TPB * b + TPB + t, 1), :].rearrange("p o d -> p (o d)")
                        last = nc.vector.scalar_tensor_tensor(out=xs, in0=o_bank[:, TOK + P * t:TOK + P * t + P], scalar=inverse[:, p, t:t + 1],
                                                              in1=xs, op0=ALU.mult, op1=ALU.add)
                    last.then_inc(x_done, 1)

                dve.wait_ge(loaded, 96)
                keep_v(0, 0, 0)
                maxima(0, 0, 0)
                slots(dve, (0, 1), step, (6, 7))

            @block.gpsimd
            def _(pool):
                pool.wait_ge(loaded, 96)
                xs = c.x[:, TPB:, :]
                nc.gpsimd.tensor_tensor(xs, xs, bias_vo[:, 1:2, :].to_broadcast([P, NT, P]), ALU.add).then_inc(bias_added, 1)


class Experts:

    def __init__(self, layer):
        self.layer = layer
        self.gated = layer != 3
        self.E = E3 if layer == 3 else E_GATED
        self.K = {1: 1, 2: 2, 3: 4}[layer]
        self.last = self.E - 2 if layer == 1 else self.E - 1
        self.before = {1: 0, 2: NT, 3: 3 * NT}[layer]
        self.tiles = N * self.K // P + self.E
        self.per_step = 1 if self.gated else 4
        self.steps = self.tiles // self.per_step
        assert self.steps % 4 == 0 and self.tiles * P <= TABLE and self.tiles <= P


def in_slots(eng, T, slot):
    for k in range(6):
        slot(0, k)
    with eng.Fori(1, T // 4 - 1) as g:
        for k in range(2, 6):
            slot(g, k)
    for k in range(2, 6):
        slot(T // 4 - 1, k)


def experts_phase(c, layer, arg):
    nc = c.nc
    m = Experts(layer)
    E, K, T, W = m.E, m.K, m.steps, m.per_step * P
    weights, weights_in = (c.wb, c.w2_in) if layer == 2 else (c.wa, c.w1_in if layer == 1 else c.w3_in)
    with Phase(c, f"e{layer}_") as ph:
        sb, sem = ph.sb, ph.sem
        w_router = sb("w_router", [P, E], F32)
        key = sb("key", [P, NT, E], F32)
        top = sb("top", [P, NT, 8], F32)
        at = sb("at", [P, NT, 8], U32)
        at_f = sb("at_f", [P, NT, K], F32)
        gate = sb("gate", [P, NT, K], F32)
        small = sb("small", [P, 2, NT], F32)
        hot = sb("hot", [P, NT, K, E], BF16)
        chosen = sb("chosen", [P, NT, E], BF16)
        sums = sb("sums", [P, 2, NT + 1, E], BF16)
        tri = sb("tri", [P, P], BF16)
        ones_bf = sb("ones_bf", [P, P], BF16)
        tiles_i = sb("tiles_i", [P, E], I32)
        cum = sb("cum", [P, 3, E], F32)
        place = sb("place", [P, NT, E], F32)
        if layer == 3:
            spread = c.wb[:, 0:NT * K * E].rearrange("p (t k e) -> p t k e", t=NT, k=K)
        else:
            spread = sb("spread", [P, NT, K, E], F32)[:, :, :, :]
        pos_f = sb("pos_f", [P, NT * K], F32)
        pos = sb("pos", [P, NT * K], I32)
        owner_f = sb("owner_f", [P, 2], F32)
        owner_i = sb("owner_i", [P, 1], I32)
        owner = sb("owner", [1, P], I32)
        xs = sb("xs", [P, 4, W], F32)
        xT = sb("xT", [P, 2, W], F32)
        silu = sb("silu", [P, 2, HID], F32) if m.gated else None
        h = sb("h", [P, 2, HID], F32)
        hT = sb("hT", [P, 2, HID], F32)
        y = sb("y", [P, 4, W], F32)
        back = sb("back", [P, 8, P], F32)

        rows_out = nc.dram_tensor(f"rows_out{layer}", [m.tiles * P, P], F32)

        loaded, logits_done, key_done, step_done = sem("loaded"), sem("logits_done"), sem("key_done"), sem("step_done")
        const_bf, sums_done, counted, pos_done = sem("const_bf"), sem("sums_done"), sem("counted"), sem("pos_done")
        silu_go, gate_go = sem("silu_go"), sem("gate_go")
        owner_done, owner_in = sem("owner_done"), sem("owner_in")
        x_in = [sem(f"x_in{k}") for k in range(4)]
        turned_x, xT_ready, up_done, silu_done, h_done = (sem(n) for n in ("turned_x", "xT_ready", "up_done", "silu_done", "h_done"))
        turned_h, hT_ready, down_done, y_ready = (sem(n) for n in ("turned_h", "hT_ready", "down_done", "y_ready"))
        stored = [sem(f"stored{k}") for k in range(4)]
        back_used = sem("back_used")
        x_bank, h_bank, y_bank = c.bank[4], c.bank[6], (c.bank[5], c.bank[7])

        def rows_of(table, g, k):
            rows = table[ds(W * (4 * g + k), W), :]
            return rows.rearrange("(j p) d -> p j d", p=P)

        def columns(buffer, k):
            return buffer[:, k % 4, :].rearrange("p (j d) -> p j d", d=P)

        def alive(g, k, d=0):
            s = 4 * g + k + d if isinstance(g, int) else 2
            return 0 <= s < T

        with nc.Block() as block:
            @block.sync
            def _(sp):
                sp.dma_start(w_router[:, :], arg[f"e{layer}_router"]).then_inc(loaded, 16)
                sp.wait_ge(owner_done, 1)
                sp.dma_start(owner[:, :], owner_i[:, :]).then_inc(owner_in, 16)

                def load(g, k):
                    need(sp, turned_x, 4 * g + k - 3)
                    sp.dma_start(columns(xs, k), rows_of(c.rows_in, g, k)).then_inc(x_in[k % 4], 16)

                def store(g, k):
                    sp.wait_ge(y_ready, 4 * g + k + 1)
                    sp.dma_start(rows_of(rows_out, g, k), columns(y, k)).then_inc(stored[k % 4], 16)

                def slot(g, k):
                    if alive(g, k, 2):
                        load(g, k + 2)
                    if alive(g, k, -2):
                        store(g, k - 2)

                sp.wait_ge(c.scattered, 16 * (m.before + NT * K))
                for k in range(2):
                    load(0, k)
                in_slots(sp, T, slot)

            @block.gpsimd
            def _(pool):
                pool.wait_ge(pos_done, 1)
                pool.wait_ge(c.rows_zero, 16 * 8)
                for t in range(NT):
                    for j in range(K):
                        pool.indirect_dma_start(out=c.rows_in[:, :], out_offset=bass.IndirectOffsetOnAxis(ap=pos[:, K * t + j:K * t + j + 1], axis=0),
                                                in_=c.xn[:, t, :], in_offset=None).then_inc(c.scattered, 16)
                for k in range(4):
                    pool.wait_ge(stored[k], 16 * T // 4)
                for n in range(NT * K):
                    need(pool, back_used, n - 7)
                    pool.indirect_dma_start(out=back[:, n % 8, :], out_offset=None, in_=rows_out[:, :],
                                            in_offset=bass.IndirectOffsetOnAxis(ap=pos[:, n:n + 1], axis=0)).then_inc(c.back_in[n % 8], 16)

            @block.tensor
            def _(pe):
                pe.wait_ge(loaded, 16)
                for t in range(NT):
                    out = c.bank[t * E // 512][:, E * t % 512:E * t % 512 + E]
                    last = nc.tensor.matmul(out, c.xnT[:, P * t:P * t + P], w_router[:, :], start=True, stop=True)
                last.then_inc(logits_done, 1)
                pe.wait_ge(const_bf, 2)
                pe.wait_ge(sums_done, 1)
                half = max(1, NT * E // 512)
                per = NT // half
                for b in range(half):
                    out = c.bank[2 + b][:, 0:per * E]
                    nc.tensor.matmul(out, tri[:, :], chosen[:, per * b:per * b + per, :].rearrange("p t e -> p (t e)"), start=True, stop=False)
                    nc.tensor.matmul(out, ones_bf[:, :], sums[:, 0, per * b:per * b + per, :].rearrange("p t e -> p (t e)"), start=False, stop=True)
                nc.tensor.matmul(c.bank[4][:, 0:E], ones_bf[:, :], sums[:, 0, NT, :], start=True, stop=True).then_inc(counted, 1)

                def expert(g, k, j):
                    n = m.per_step * (4 * g + k) + j
                    return pe.value_load(owner[0:1, ds(n, 1)] if not isinstance(n, int) else owner[0:1, n:n + 1], min_val=0, max_val=m.last)

                def turn_x(g, k):
                    s = 4 * g + k
                    pe.wait_ge(x_in[k % 4], 16 * (g + k // 4) + 16)
                    need(pe, xT_ready, s)
                    for j in range(m.per_step):
                        last = nc.tensor.transpose(x_bank[:, P * j:P * j + P], xs[:, k % 4, P * j:P * j + P], c.ident[:, :])
                    last.then_inc(turned_x, 1)

                def up(g, k):
                    s = 4 * g + k
                    e_s = [expert(g, k, j) for j in range(m.per_step)]
                    pe.wait_ge(xT_ready, s + 1)
                    need(pe, h_done, s - 1)
                    if m.gated:
                        e = e_s[0]
                        nc.tensor.matmul(c.bank[k % 2][:, :], xT[:, k % 2, :], weights[:, ds(e * GATED_COLS, HID)], start=True, stop=True).then_inc(silu_go, 1)
                        nc.tensor.matmul(c.bank[2 + k % 2][:, :], xT[:, k % 2, :], weights[:, ds(e * GATED_COLS + HID, HID)],
                                         start=True, stop=True).then_inc(up_done, 1)
                        return
                    for j, e in enumerate(e_s):
                        last = nc.tensor.matmul(c.bank[k % 2][:, P * j:P * j + P], xT[:, k % 2, P * j:P * j + P], weights[:, ds(e * (2 * P), P)],
                                                start=True, stop=True)
                    last.then_inc(up_done, 1)

                def turn_h(g, k):
                    s = 4 * g + k
                    pe.wait_ge(h_done, s + 1)
                    need(pe, hT_ready, s)
                    for j in range(4):
                        last = nc.tensor.transpose(h_bank[:, P * j:P * j + P], h[:, k % 2, P * j:P * j + P], c.ident[:, :])
                    last.then_inc(turned_h, 1)

                def down(g, k):
                    s = 4 * g + k
                    e_s = [expert(g, k, j) for j in range(m.per_step)]
                    pe.wait_ge(hT_ready, s + 1)
                    need(pe, y_ready, s - 1)
                    e = e_s[0]
                    for j in range(4):
                        lhsT = hT[:, k % 2, P * j:P * j + P]
                        if m.gated:
                            last = nc.tensor.matmul(y_bank[k % 2][:, 0:P], lhsT, weights[:, ds(e * GATED_COLS + (2 * HID + P * j), P)],
                                                    start=(j == 0), stop=(j == 3))
                        else:
                            e = e_s[j]
                            last = nc.tensor.matmul(y_bank[k % 2][:, P * j:P * j + P], lhsT, weights[:, ds(e * (2 * P) + P, P)], start=True, stop=True)
                    last.then_inc(down_done, 1)

                def slot(g, k):
                    if alive(g, k, 1):
                        turn_x(g, k + 1)
                    if alive(g, k):
                        up(g, k)
                    if alive(g, k, -1):
                        turn_h(g, k - 1)
                    if alive(g, k, -2):
                        down(g, k - 2)

                pe.wait_ge(owner_in, 16)
                pe.wait_ge(pos_done, 1)
                pe.wait_ge(weights_in, 16 * 8)
                turn_x(0, 0)
                in_slots(pe, T, slot)

            @block.scalar
            def _(act):
                act.wait_ge(logits_done, 1)
                if layer == 1:
                    act.wait_ge(step_done, 3)
                    nc.scalar.activation(key[:, :, :], key[:, :, :], ACT.Exp).then_inc(key_done, 1)
                if layer == 2:
                    act.wait_ge(gate_go, 1)
                    nc.scalar.activation(gate[:, :, 1], small[:, 0, :], ACT.Exp).then_inc(key_done, 1)
                if layer == 3:
                    for b in range(2):
                        nc.scalar.activation(key[:, 8 * b:8 * b + 8, :], c.bank[b][:, :].rearrange("p (t e) -> p t e", t=8), ACT.Sigmoid).then_inc(key_done, 1)

                def activate(g, k):
                    s = 4 * g + k
                    if m.gated:
                        act.wait_ge(silu_go, s + 1)
                        need(act, h_done, s - 1)
                        nc.scalar.activation(silu[:, k % 2, :], c.bank[k % 2][:, :], ACT.Silu).then_inc(silu_done, 1)
                    else:
                        act.wait_ge(up_done, s + 1)
                        need(act, turned_h, s - 1)
                        nc.scalar.activation(h[:, k % 2, :], c.bank[k % 2][:, :], ACT.Relu).then_inc(h_done, 1)

                def keep_h(g, k):
                    s = 4 * g + k
                    act.wait_ge(turned_h, s + 1)
                    need(act, down_done, s - 1)
                    nc.scalar.copy(hT[:, k % 2, :], h_bank[:, :]).then_inc(hT_ready, 1)

                def slot(g, k):
                    if alive(g, k):
                        activate(g, k)
                    if alive(g, k, -1):
                        keep_h(g, k - 1)

                in_slots(act, T, slot)

            @block.vector
            def _(dve):
                v = nc.vector
                step = Count(dve, step_done)
                v.tensor_copy(tri[:, :], c.const[:, TRI_AT:TRI_AT + P]).then_inc(const_bf, 1)
                v.memset(ones_bf[:, :], 1.0).then_inc(const_bf, 1)
                step.link(v.memset(sums[:, :, 0:1, :], 0.0))
                dve.wait_ge(logits_done, 1)
                if layer == 1:
                    logits = c.bank[0][:, 0:NT * E].rearrange("p (t e) -> p t e", t=NT)
                    wide = [P, NT, E]
                    step.link(v.tensor_reduce(small[:, 0, :], logits, AX.X, ALU.max))
                    step.add(v.tensor_tensor(key[:, :, :], logits, small[:, 0, :].unsqueeze(2).to_broadcast(wide), ALU.subtract))
                    dve.wait_ge(key_done, 1)
                    step.link(v.tensor_reduce(small[:, 0, :], key[:, :, :], AX.X, ALU.add))
                    step.link(v.reciprocal(small[:, 1, :], small[:, 0, :]))
                    step.link(v.tensor_tensor(key[:, :, :], key[:, :, :], small[:, 1, :].unsqueeze(2).to_broadcast(wide), ALU.mult))
                elif layer == 2:
                    step.link(v.tensor_copy(key[:, :, :], c.bank[0][:, 0:NT * E].rearrange("p (t e) -> p t e", t=NT)))
                else:
                    dve.wait_ge(key_done, 2)
                for t in range(NT):
                    step.add(v.max(top[:, t, :], key[:, t, :]))
                step.wait()
                if layer == 2:
                    v.tensor_tensor(small[:, 0, :], top[:, :, 1], top[:, :, 0], ALU.subtract).then_inc(gate_go, 1)
                for t in range(NT):
                    step.add(v.max_index(at[:, t, :], top[:, t, :], key[:, t, :]))
                step.wait()
                step.link(v.tensor_copy(at_f[:, :, :], at[:, :, 0:K]))
                shape = [P, NT, K, E]
                step.add(v.tensor_tensor(hot[:, :, :, :], c.const[:, IOTA_AT:IOTA_AT + E].unsqueeze(1).unsqueeze(1).to_broadcast(shape),
                                         at_f[:, :, :].unsqueeze(3).to_broadcast(shape), ALU.is_equal))
                if layer == 1:
                    step.link(v.tensor_scalar(gate[:, :, 0], at_f[:, :, 0], float(m.last) + 0.5, 2.0, ALU.is_lt, ALU.mult))
                    step.link(v.tensor_tensor(gate[:, :, 0], gate[:, :, 0], top[:, :, 0], ALU.mult))
                elif layer == 2:
                    dve.wait_ge(key_done, 1)
                    step.link(v.tensor_scalar(small[:, 1, :], gate[:, :, 1], 1.0, None, ALU.add))
                    step.link(v.reciprocal(gate[:, :, 0], small[:, 1, :]))
                    step.link(v.tensor_tensor(gate[:, :, 1], gate[:, :, 1], gate[:, :, 0], ALU.mult))
                else:
                    step.link(v.tensor_copy(gate[:, :, :], top[:, :, 0:K]))
                with nc.allow_low_precision("counts up to 16 are exact"):
                    step.link(v.tensor_reduce(chosen[:, :, :], hot[:, :, :, :].rearrange("p t k e -> p t e k"), AX.X, ALU.add))
                    step.link(v.tensor_copy(sums[:, 0, 1:, :], chosen[:, :, :]))
                    for n, d in enumerate((1, 2, 4, 8)):
                        src, dst = sums[:, n % 2], sums[:, 1 - n % 2]
                        step.add(v.tensor_copy(dst[:, 1:1 + d, :], src[:, 1:1 + d, :]))
                        last = v.tensor_tensor(dst[:, 1 + d:, :], src[:, 1 + d:, :], src[:, 1:NT + 1 - d, :], ALU.add)
                        step.link(last)
                    dve.sem_inc(sums_done, 1)
                dve.wait_ge(counted, 1)
                step.link(v.tensor_scalar(tiles_i[:, :], c.bank[4][:, 0:E], float(P - 1), None, ALU.add))
                step.link(v.tensor_scalar(tiles_i[:, :], tiles_i[:, :], 7, None, ALU.logical_shift_right))
                step.link(v.tensor_copy(cum[:, 0, :], tiles_i[:, :]))
                now, d = 0, 1
                while d < E:
                    step.add(v.tensor_copy(cum[:, 1 - now, 0:d], cum[:, now, 0:d]))
                    step.link(v.tensor_tensor(cum[:, 1 - now, d:], cum[:, now, d:], cum[:, now, 0:E - d], ALU.add))
                    now, d = 1 - now, 2 * d
                step.add(v.tensor_scalar(cum[:, 1 - now, :], cum[:, now, :], c.const[:, PART_AT:PART_AT + 1], None, ALU.is_le))
                step.link(v.tensor_tensor(cum[:, 2, :], cum[:, now, :], tiles_i[:, :], ALU.subtract))
                step.link(v.tensor_reduce(owner_f[:, 0:1], cum[:, 1 - now, :], AX.X, ALU.add))
                v.tensor_scalar(owner_i[:, :], owner_f[:, 0:1], float(m.last), None, ALU.min).then_inc(owner_done, 1)
                step.link(v.tensor_scalar(cum[:, 2, :], cum[:, 2, :], float(P), None, ALU.mult))
                per = NT // max(1, NT * E // 512)
                for b in range(NT // per):
                    step.add(v.tensor_tensor(place[:, per * b:per * b + per, :], c.bank[2 + b][:, 0:per * E].rearrange("p (t e) -> p t e", t=per),
                                             cum[:, 2:3, :].to_broadcast([P, per, E]), ALU.add))
                step.wait()
                step.link(v.tensor_tensor(spread, hot[:, :, :, :], place[:, :, :].unsqueeze(2).to_broadcast(shape), ALU.mult))
                step.link(v.tensor_reduce(pos_f[:, :].rearrange("p (t k) -> p t k", t=NT), spread, AX.X, ALU.add))
                v.tensor_copy(pos[:, :], pos_f[:, :]).then_inc(pos_done, 1)

                def keep_x(g, k):
                    s = 4 * g + k
                    dve.wait_ge(turned_x, s + 1)
                    need(dve, up_done, s - 1)
                    v.tensor_copy(xT[:, k % 2, :], x_bank[:, 0:W]).then_inc(xT_ready, 1)

                def multiply(g, k):
                    s = 4 * g + k
                    dve.wait_ge(silu_done, s + 1)
                    dve.wait_ge(up_done, s + 1)
                    need(dve, turned_h, s - 1)
                    v.tensor_tensor(h[:, k % 2, :], silu[:, k % 2, :], c.bank[2 + k % 2][:, :], ALU.mult).then_inc(h_done, 1)

                def keep_y(g, k):
                    s = 4 * g + k
                    dve.wait_ge(down_done, s + 1)
                    need(dve, stored[k % 4], 16 * (g + k // 4))
                    v.tensor_copy(y[:, k % 4, :], y_bank[k % 2][:, 0:W]).then_inc(y_ready, 1)

                def slot(g, k):
                    if alive(g, k, 1):
                        keep_x(g, k + 1)
                    if m.gated and alive(g, k):
                        multiply(g, k)
                    if alive(g, k, -2):
                        keep_y(g, k - 2)

                keep_x(0, 0)
                in_slots(dve, T, slot)
                for n in range(NT * K):
                    dve.wait_ge(c.back_in[n % 8], 16 * ((m.before + n) // 8 + 1))
                    xs_t = c.x[:, TPB + n // K, :]
                    if n % K:
                        dve.wait_ge(back_used, n)
                    v.scalar_tensor_tensor(out=xs_t, in0=back[:, n % 8, :], scalar=gate[:, n // K, n % K:n % K + 1], in1=xs_t,
                                           op0=ALU.mult, op1=ALU.add).then_inc(back_used, 1)


def layer1_ffn(c, arg):
    layer1_shared(c, arg)
    experts_phase(c, 1, arg)


def layer2_ffn(c, arg):
    experts_phase(c, 2, arg)


def layer3_ffn(c, arg):
    experts_phase(c, 3, arg)


def layer0_attention(c, arg):
    attention_phase(c, 0, arg)


def layer2_attention(c, arg):
    attention_phase(c, 2, arg)


ALL_PHASES = (layer0_attention, layer0_ffn, layer1_attention, layer1_ffn,
              layer2_attention, layer2_ffn, layer3_attention, layer3_ffn)


def end_phase(c, out):
    nc = c.nc
    stored = c.sem("x_stored")
    with nc.Block() as block:
        @block.sync
        def _(sp):
            sp.dma_start(out.rearrange("b (t p) d -> p (b t) d", p=P), c.x[:, TPB:, :]).then_inc(stored, 16)
            sp.wait_ge(stored, 16)


def build(nc, arg, out, phases=ALL_PHASES):
    with ExitStack() as ctx:
        c = Core(nc, ctx)
        start_phase(c, arg)
        for n, phase in enumerate(phases):
            norm_phase(c, f"n{n}")
            phase(c, arg)
        end_phase(c, out)


def hid_major(w):
    return w.reshape(-1, P, w.shape[-1]).transpose(1, 0, 2).reshape(P, -1)


def gated(gate, up, down):
    return np.concatenate([np.concatenate([gate[e], up[e], hid_major(down[e])], axis=1) for e in range(len(gate))], axis=1)


def laid_out(inputs):
    a = {k: np.asarray(v) for k, v in inputs.items()}
    perm = np.arange(P).reshape(J, 2, D).transpose(1, 2, 0).reshape(P)
    o = {"x": a["x"], "ctxT": a["ctx_1024"].transpose(2, 0, 1), "mask": a["mask_1x1xSxS2_ff0"][0, 0],
         "maskT": a["mask_1x1xSxS2_ff0"][0, 0].T,
         "a0_wq": a["L0_xattn_Wq"][:, perm], "a0_wk": a["L0_xattn_Wk"][:, perm], "a0_wv": a["L0_xattn_Wv"], "a0_wo": a["L0_xattn_Wo"]}
    wf = a["L2_xattn_Wf"].T
    o["a2_wq"], o["a2_wk"], o["a2_wv"], o["a2_wp"] = a["L2_xattn_Wq"].T[:, perm], wf[:, :P][:, perm], wf[:, P:], a["L2_xattn_Wp"].T
    o["a2_bias_qk"] = np.stack([a["L2_xattn_bq"][perm], a["L2_xattn_bf"][:P][perm]], axis=1)
    o["a2_bias_row"] = np.stack([a["L2_xattn_bf"][P:], a["L2_xattn_bp"]])[None]
    o["a2_lora_a"] = np.stack([a["L2_xattn_Aq"], a["L2_xattn_Af"], a["L2_xattn_Ap"]], axis=1)
    bf = a["L2_xattn_Bf"].T
    o["a2_lora_b"] = np.stack([a["L2_xattn_Bq"].T[:, perm], bf[:, :P][:, perm], bf[:, P:], a["L2_xattn_Bp"].T], axis=1)
    f0_up = np.concatenate([a["L0_ffn_up_w"].reshape(-1, P), a["L0_ffn_shared_up"]]).T
    f0_down = np.concatenate([a["L0_ffn_down_w"].transpose(0, 2, 1).reshape(-1, P), a["L0_ffn_shared_down"].T])
    o["f0_w"] = np.concatenate([f0_up, hid_major(f0_down), a["L0_ffn_gate_w"].T], axis=1)
    o["f0_bias"] = np.tile(a["L0_ffn_bias_e"], (P, 1))
    o["const"] = np.concatenate([np.tile(np.arange(64), (P, 1)), np.triu(np.ones((P, P)), 1), np.arange(P)[:, None],
                                 np.tile(np.tril(np.ones((4, 4)), -1).reshape(16), (P, 1))], axis=1).astype(np.float32)
    o["f1_w"] = gated(*(np.concatenate([a["L1_ffn_w_" + n], a["L1_ffn_ws_" + n][None]]) for n in ("gate", "up", "down")))
    o["f2_w"] = gated(a["L2_ffn_experts_w1"], a["L2_ffn_experts_w3"], a["L2_ffn_experts_w2"])
    o["f3_w"] = np.concatenate([a["L3_ffn_keys"], a["L3_ffn_values"]], axis=2).transpose(1, 0, 2).reshape(P, -1)
    o["e1_router"], o["e2_router"], o["e3_router"] = a["L1_ffn_w_router"], a["L2_ffn_gate"], a["L3_ffn_expert_sel"].T
    o["a1_w"] = np.stack([a["L1_xattn_W"][:, :P].T, a["L1_xattn_W"][:, P:].T])
    o["a1_bias"] = a["L1_xattn_b"][None]
    o["one_hot8"] = np.repeat(np.eye(B, dtype=np.float32)[:, :, None], P, axis=2)
    for n in ("q", "k", "v", "o"):
        o["a3_w" + n] = a["L3_xattn_W" + n]
    o["a3_bias_qk"] = np.stack([a["L3_xattn_bq"], a["L3_xattn_bk"]], axis=1)
    o["a3_bias_vo"] = np.tile(np.stack([a["L3_xattn_bv"], a["L3_xattn_bo"]]), (P, 1, 1))
    expert = np.arange(8 * P) // 64
    o["spread0"] = np.tile(expert[None, :] == np.arange(16)[:, None], (PARTS, 1)).astype(np.float32)
    return {k: np.ascontiguousarray(v) for k, v in o.items()}


def kernel(**inputs):
    import concourse.bacc as bacc
    from concourse.bass_utils import run_bass_kernel_spmd

    nc = bacc.Bacc("TRN2", target_bir_lowering=False, num_devices=1)
    arrays = laid_out(inputs)
    arg = {k: nc.dram_tensor("in_" + k, v.shape, mybir.dt.from_np(v.dtype), kind="ExternalInput").ap() for k, v in arrays.items()}
    out = nc.dram_tensor("out", (B, TOK, P), F32, kind="ExternalOutput").ap()
    build(nc, arg, out)
    result = run_bass_kernel_spmd(nc, [{"in_" + k: v for k, v in arrays.items()}], core_ids=[0])
    return result.results[0]["out"]
```

```python
from contextlib import ExitStack

import numpy as np
import concourse.bass as bass
from concourse import mybir

F32 = mybir.dt.float32
BF16 = mybir.dt.bfloat16
F16 = mybir.dt.float16
I32 = mybir.dt.int32
U32 = mybir.dt.uint32
ACT = mybir.ActivationFunctionType
ALU = mybir.AluOpType
AX = mybir.AxisListType
ds = bass.ds

P = 128
B = 8
TOK = 256
N = B * TOK
NT = N // P
TPB = TOK // P
CTX = 512
H = 16
D = P // H
J = H // 2
EBUFS = 4
PARTS = 3
SLOTS = 6
QROWS = SLOTS * D
AUG = QROWS + PARTS
PVC = PARTS * (D + 1)
EPS = 1e-5
E_GATED = 8
HID = 512
GATED_COLS = 2 * HID + 4 * P
E3 = 64
TABLE = 128 * P
ROUTED_SCALE = 2.5
L0_AT = E_GATED * GATED_COLS
ZERO_AT = L0_AT + 2 * 10 * P + 16
IOTA_AT, TRI_AT, PART_AT, BEFORE_AT, CONSTS = 0, 64, 192, 193, 209


class Count:

    def __init__(self, eng, sem, base=0):
        self.eng, self.sem, self.base, self.n = eng, sem, base, 0

    def add(self, ins):
        ins.then_inc(self.sem, 1)
        self.n += 1

    def wait(self):
        self.eng.wait_ge(self.sem, self.base + self.n)

    def link(self, ins):
        self.add(ins)
        self.wait()


class Core:

    def __init__(self, nc, ctx):
        self.nc, self.ctx = nc, ctx
        self.x = self.sb("x", [P, NT + TPB, P], F32)
        self.xn = self.sb("xn", [P, NT, P], F32)
        self.xnT = self.sb("xnT", [P, N], F32)
        self.wa = self.sb("wa", [P, 64 * 256], F32)
        self.wb = self.sb("wb", [P, 8 * 1536], F32)
        self.ident = self.sb("ident", [P, P], F32)
        self.ident_bf = self.sb("ident_bf", [P, P], BF16)
        self.ones = self.sb("ones", [P, P], F32)
        self.stats = self.sb("stats", [P, NT, 6], F32)
        self.mean_var = self.sb("mean_var", [P, NT, 2], F32)
        self.std = self.sb("std", [P, NT], F32)
        self.rstd = self.sb("rstd", [P, NT], F32)
        self.ctx_sum = self.sb("ctx_sum", [P, B], F32)
        self.const = self.sb("const", [P, CONSTS], F32)
        self.w0_in, self.w1_in, self.w2_in, self.w3_in = (self.sem(f"w{n}_in") for n in range(4))
        self.rows_zero = self.sem("rows_zero")
        self.scattered, self.back_in = self.sem("scattered"), [self.sem(f"back_in{k}") for k in range(8)]
        self.rows_in = nc.dram_tensor("rows_in", [TABLE, P], F32)
        self.bank = [ctx.enter_context(nc.psum_tensor(f"bank{i}", [P, 512], F32)) for i in range(8)]

    def sb(self, name, shape, dt):
        return self.ctx.enter_context(self.nc.sbuf_tensor(name, shape, dt))

    def sem(self, name):
        return self.ctx.enter_context(self.nc.semaphore(name))


class Phase:

    def __init__(self, c, tag):
        self.c, self.tag, self.ctx, self.sems = c, tag, ExitStack(), []

    def __enter__(self):
        self.ctx.__enter__()
        return self

    def sb(self, name, shape, dt):
        return self.ctx.enter_context(self.c.nc.sbuf_tensor(self.tag + name, shape, dt))

    def sem(self, name):
        s = self.ctx.enter_context(self.c.nc.semaphore(self.tag + name))
        self.sems.append(s)
        return s

    def __exit__(self, *error):
        if error[0] is None:
            with self.c.nc.Block() as block:
                @block.sync
                def _(sp):
                    numbers = sorted(s.num for s in self.sems)
                    while numbers:
                        first = last = numbers.pop(0)
                        while numbers and numbers[0] == last + 1:
                            last = numbers.pop(0)
                        sp.sem_clear(range(first, last + 1))
        return self.ctx.__exit__(*error)


def need(eng, sem, n):
    if not isinstance(n, int) or n > 0:
        eng.wait_ge(sem, n)


def start_phase(c, arg):
    nc = c.nc
    loaded, const, moved = c.sem("x_loaded"), c.sem("const_ready"), c.sem("const_copied")
    with nc.Block() as block:
        @block.sync
        def _(sp):
            sp.dma_start(c.x[:, TPB:, :], arg["x"].rearrange("b (t p) d -> p (b t) d", p=P)).then_inc(loaded, 16)
            sp.dma_start(c.const[:, :], arg["const"]).then_inc(loaded, 16)
            sp.dma_start(c.wa[:, L0_AT:ZERO_AT], arg["f0_w"]).then_inc(c.w0_in, 16)
            sp.wait_ge(loaded, 32)

        @block.gpsimd
        def _(pool):
            nc.gpsimd.memset(c.ident[:, :], 0.0).then_inc(const, 1)
            pool.wait_ge(const, 1)
            nc.gpsimd.affine_select(out=c.ident[:, :], in_=c.ident[:, :], compare_op=ALU.not_equal, fill=1.0,
                                    base=0, pattern=[[-1, P]], channel_multiplier=1).then_inc(const, 1)

        @block.vector
        def _(dve):
            nc.vector.memset(c.ones[:, :], 1.0)
            nc.vector.memset(c.x[:, 0:TPB, :], 0.0)
            nc.vector.memset(c.wa[:, ZERO_AT:ZERO_AT + 1024], 0.0)
            dve.wait_ge(const, 2)
            nc.vector.tensor_copy(c.ident_bf[:, :], c.ident[:, :]).then_inc(moved, 1)


def norm_phase(c, tag):
    nc = c.nc
    with Phase(c, tag) as ph:
        stat, var, std, xn_ready, turned, kept = (ph.sem(n) for n in ("_stats", "_var", "_std", "_xn", "_turned", "_kept"))
        norm_block(c, stat, var, std, xn_ready, turned, kept)


def norm_block(c, stat, var, std, xn_ready, turned, kept):
    nc = c.nc
    with nc.Block() as block:
        @block.vector
        def _(dve):
            for t in range(NT):
                nc.vector.bn_stats(c.stats[:, t, :], c.x[:, TPB + t, :]).then_inc(stat, 1)
            for t in range(NT):
                dve.wait_ge(stat, t + 1)
                nc.vector.bn_aggr(c.mean_var[:, t, :], c.stats[:, t, :]).then_inc(stat, 1)
            dve.wait_ge(stat, 2 * NT)
            nc.vector.tensor_scalar(c.rstd[:, :], c.mean_var[:, :, 1], EPS, None, ALU.add).then_inc(var, 1)
            dve.wait_ge(std, 1)
            nc.vector.reciprocal(c.rstd[:, :], c.std[:, :]).then_inc(var, 1)
            dve.wait_ge(var, 2)
            for t in range(NT):
                nc.vector.tensor_scalar(c.xn[:, t, :], c.x[:, TPB + t, :], c.mean_var[:, t, 0:1],
                                        c.rstd[:, t:t + 1], ALU.subtract, ALU.mult).then_inc(xn_ready, 1)

        @block.scalar
        def _(act):
            act.wait_ge(var, 1)
            nc.scalar.activation(c.std[:, :], c.rstd[:, :], ACT.Sqrt).then_inc(std, 1)
            for q in range(NT // 4):
                act.wait_ge(turned, q + 1)
                nc.scalar.copy(c.xnT[:, 512 * q:512 * q + 512], c.bank[q % 4][:, :]).then_inc(kept, 1)

        @block.tensor
        def _(pe):
            for t in range(NT):
                pe.wait_ge(xn_ready, t + 1)
                last = nc.tensor.transpose(c.bank[t // 4][:, P * (t % 4):P * (t % 4) + P], c.xn[:, t, :], c.ident[:, :])
                if t % 4 == 3:
                    last.then_inc(turned, 1)


def background(c, layer, arg, sp, i):
    if layer == 0:
        cols, rows = L0_AT // 8, TABLE // 8
        sp.dma_start(c.wa[:, ds(cols * i, cols)], arg["f1_w"][:, ds(cols * i, cols)]).then_inc(c.w1_in, 16)
        zeros = c.wa[:, ZERO_AT:ZERO_AT + 1024].unsqueeze(1).to_broadcast([P, rows // 1024, 1024])
        sp.dma_start(c.rows_in[ds(rows * i, rows), :].rearrange("(p n r) d -> p n (r d)", p=P, r=8), zeros).then_inc(c.rows_zero, 16)
    else:
        cols = 2 * P * E3 // 8
        sp.dma_start(c.wa[:, ds(cols * i, cols)], arg["f3_w"][:, ds(cols * i, cols)]).then_inc(c.w3_in, 16)


def attention_phase(c, layer, arg):
    nc = c.nc
    causal = layer == 2
    keys = 2 * P if causal else CTX
    kt_n = keys // P
    NA = NB = 1 if causal else 2
    SPAN = 384 if causal else 1024
    SHARE = SPAN // 4
    scale = float(D) ** -0.5
    tag = f"a{layer}_"
    with Phase(c, tag) as ph:
        sb, sem = ph.sb, ph.sem
        w = sb("w", [P, 4, P], F32)
        ctxT = sb("ctxT", [P, 2, CTX], F32)
        k_full = sb("k_full", [P, keys], F32)
        q_full = sb("q_full", [P, TOK], F32)
        v_full = sb("v_full", [P, kt_n, P], F32)
        k_part = sb("k_part", [P, PARTS, keys], BF16)
        q_part = sb("q_part", [P, PARTS, TOK], BF16)
        KS = sb("KS", [P, 2, J, keys], BF16)
        QS = sb("QS", [P, 2, J, TOK], BF16)
        V = sb("V", [P, 2, kt_n, H, PVC], BF16)
        neg_max = sb("neg_max", [P, 2, TPB, H // 2], F32)
        m_part = sb("m_part", [P, 2, TPB, 2, PARTS, 4], BF16)
        m_rest = sb("m_rest", [P, 2, TPB, 8], F32)
        m_rows = sb("m_rows", [2 * PARTS * 4, 2, TOK], BF16)
        E2 = sb("E2", [P, EBUFS, SPAN], F16)
        heads = sb("heads", [P, TPB, H, D + 1], F32)
        rsum = sb("rsum", [P, TPB, H], F32)
        attn = sb("attn", [P, TPB, P], F32)
        attnT = sb("attnT", [P, TOK], F32)
        k_dram = nc.dram_tensor(tag + "k_dram", [2, SLOTS, P, keys], BF16)
        q_dram = nc.dram_tensor(tag + "q_dram", [2, SLOTS, P, TOK], BF16)
        a_bank, b_bank, o_bank, misc, m_bank = c.bank[0:2], c.bank[2:4], c.bank[4:6], c.bank[6], c.bank[7]
        bfview = c.wb[:, :].bitcast(BF16)
        if causal:
            E = sb("E", [P, EBUFS, SPAN], F32)
            E1 = sb("E1", [P, EBUFS, SPAN], F16)
            bias_qk = sb("bias_qk", [P, 2], F32)
            bias_q = sb("bias_q", [P, 1], F32)
            bias_row = sb("bias_row", [1, 2, P], F32)
            lora_a = sb("lora_a", [16, 3, P], F32)
            lora_b = sb("lora_b", [16, 4, P], F32)
            tri = sb("tri", [P, 2, P], BF16)
            tri_f = sb("tri_f", [P, 2, P], F32)
        else:
            mask_q = bfview[:, 0:3072].rearrange("p (m t k) -> p m t k", m=PARTS, t=TPB)
            mask_k = bfview[:, 3072:6144].rearrange("p (m t k) -> p m t k", m=PARTS, t=kt_n)
            mask_f = c.wb[:, 6144:8192].rearrange("p (m k) -> p m k", m=2)
            E1 = c.wb[:, 3072:3072 + EBUFS * SPAN // 2].bitcast(F16).rearrange("p (b n) -> p b n", b=EBUFS)
            E = c.wb[:, 8192:8192 + EBUFS * SPAN].rearrange("p (b n) -> p b n", b=EBUFS)
            any_mask = sb("any_mask", [P, 4], F32)
            any_mask_i = sb("any_mask_i", [P, 1], I32)

        LOADS = 16 * (8 if causal else 6)
        SETUP = 6 if causal else 7
        ANY_MASK = 6
        bias_scaled = sem("bias_scaled")
        loaded = sem("loaded")
        ctx_in = [sem(f"ctx_in{p}") for p in range(2)]
        setup, setup_pool = sem("setup"), sem("setup_pool")
        rows_of_ones = sem("rows_of_ones")
        mask_step, mask_ready = sem("mask_step"), sem("mask_ready")
        lora_done = sem("lora_done")
        proj_k, proj_q, proj_v = sem("proj_k"), sem("proj_q"), sem("proj_v")
        full_k, full_q, full_v = sem("full_k"), sem("full_q"), sem("full_v")
        parts_k, parts_q, parts_v = sem("parts_k"), sem("parts_q"), sem("parts_v")
        pool_step = sem("pool_step")
        out_k, out_q = sem("out_k"), sem("out_q")
        stack = [sem(f"stack{p}") for p in range(2)]
        logits_a, max_done = sem("logits_a"), sem("max_done")
        parts_m, turned_m, rows_m = sem("parts_m"), sem("turned_m"), sem("rows_m")
        aug = [[sem(f"aug{p}{g}") for g in range(2)] for p in range(2)]
        logits_b, exp_done = sem("logits_b"), sem("exp_done")
        e1_done, e2_done, pv_done = sem("e1_done"), sem("e2_done"), sem("pv_done")
        e2_share = sem("e2_share")
        norm_step, o_free, norm_done = sem("norm_step"), sem("o_free"), sem("norm_done")
        turned_o, kept_o, out_o, x_done = sem("turned_o"), sem("kept_o"), sem("out_o"), sem("x_done")
        summed = sem("summed")

        START = {max_done: 3, parts_m: 2, turned_m: 2, rows_m: 2, exp_done: 2, e1_done: 2, e2_done: 4, e2_share: 4, pv_done: 17,
                 o_free: 2, norm_done: 1, parts_k: 1, parts_q: 1, parts_v: 1, turned_o: 1, out_o: 1, out_k: 16, out_q: 16,
                 aug[0][0]: 16, aug[0][1]: 16, aug[1][0]: 16, aug[1][1]: 16}

        def reach(eng, s, n):
            eng.wait_ge(s, START.get(s, 0) + n)

        def head(h):
            return h // 2, h % 2, 64 * (h % 2)

        def logits_slot(bb, p, h):
            if h < LAG:
                return bb, p, H - LAG + h
            return bb + p, 1 - p, h - LAG

        LAG = 2
        STEP_LINKS = 3 * 2 + 2 * 3
        FIRST_LINKS = 2 * 5 + 3

        def v_parts(p):
            return [V[:, p, :, :, (D + 1) * m:(D + 1) * m + D] for m in range(PARTS)]

        with nc.Block() as block:
            @block.sync
            def _(sp):
                def load_ctx(bb, p):
                    sp.dma_start(ctxT[:, p, :], arg["ctxT"][:, ds(2 * bb + p, 1), :].rearrange("d o k -> d (o k)")).then_inc(ctx_in[p], 16)

                def parts_out(bb, p, stacked=None):
                    b = 2 * bb + p
                    reach(sp, parts_k, b + 1)
                    if stacked is not None:
                        sp.wait_ge(stack[p], stacked)
                    for first, n, part in ((0, 3, 0), (3, 2, 1), (5, 1, 2)):
                        sp.dma_start(k_dram[p, first:first + n].rearrange("s r k -> r s k"),
                                     k_part[:, part:part + 1, :].to_broadcast([P, n, keys])).then_inc(out_k, 16)
                    reach(sp, parts_q, b + 1)
                    for first, n in ((0, 3), (3, 2), (5, 1)):
                        sp.dma_start(q_dram[p, first:first + n].rearrange("s r k -> r s k"),
                                     q_part[:, 0:n, :]).then_inc(out_q, 16)

                def stack_in(bb, p):
                    b = 2 * bb + p
                    reach(sp, out_k, 48 * (b + 1))
                    reach(sp, out_q, 48 * (b + 1))
                    for par in range(2):
                        rows = slice(64 * par, 64 * par + 64)
                        dst = slice(64 * par, 64 * par + QROWS)
                        sp.dma_start(KS[dst, p, :, :], k_dram[p, :, rows, :].rearrange("s (d j) k -> s d (j k)", d=D)).then_inc(stack[p], 16)
                        sp.dma_start(QS[dst, p, :, :], q_dram[p, :, rows, :].rearrange("s (d j) k -> s d (j k)", d=D)).then_inc(stack[p], 16)

                def aug_in(bb, p, g):
                    reach(sp, rows_m, 2 * (2 * bb + p) + g + 1)
                    for par in range(2):
                        sp.dma_start(QS[64 * par + QROWS:64 * par + AUG, p, 4 * g:4 * g + 4, :],
                                     m_rows[12 * par:12 * par + 12, g, :]).then_inc(aug[p][g], 16)

                if causal:
                    for n, name in enumerate(("wq", "wk", "wv", "wp")):
                        sp.dma_start(w[:, n, :], arg["a2_" + name]).then_inc(loaded, 16)
                    sp.dma_start(bias_qk[:, :], arg["a2_bias_qk"]).then_inc(loaded, 16)
                    sp.dma_start(bias_row[:, :, :], arg["a2_bias_row"]).then_inc(loaded, 16)
                    sp.dma_start(lora_a[:, :, :], arg["a2_lora_a"]).then_inc(loaded, 16)
                    sp.dma_start(lora_b[:, :, :], arg["a2_lora_b"]).then_inc(loaded, 16)
                else:
                    for n, name in enumerate(("wq", "wk", "wv", "wo")):
                        sp.dma_start(w[:, n, :], arg["a0_" + name]).then_inc(loaded, 16)
                    sp.dma_start(mask_f[:, 0, :].rearrange("q (t k) -> q t k", t=TPB), arg["mask"].rearrange("(t q) k -> q t k", t=TPB)).then_inc(loaded, 16)
                    sp.dma_start(mask_f[:, 1, :].rearrange("k (t q) -> k t q", t=kt_n), arg["maskT"].rearrange("(t k) q -> k t q", t=kt_n)).then_inc(loaded, 16)
                load_ctx(0, 0)
                load_ctx(0, 1)
                for p in range(2):
                    parts_out(0, p)
                    if p == 0:
                        sp.wait_ge(rows_of_ones, 1)
                    stack_in(0, p)
                aug_in(0, 0, 0)

                def step(bb, p, more=True, last=False):
                    i = 2 * bb + p
                    if more:
                        reach(sp, proj_v, i + 1)
                        if not causal:
                            reach(sp, summed, i + 1)
                        load_ctx(bb + 1, p)
                    aug_in(bb, p, 1)
                    if more:
                        parts_out(bb + 1, p, stacked=64 * bb + 64)
                    if not last:
                        aug_in(bb + p, 1 - p, 0)
                    if more:
                        reach(sp, logits_b, NB * H * (i + 1))
                        stack_in(bb + 1, p)
                    background(c, layer, arg, sp, i)

                with sp.Fori(0, 3) as bb:
                    for p in range(2):
                        step(bb, p)
                step(3, 0, more=False)
                step(3, 1, more=False, last=True)

            @block.gpsimd
            def _(pool):
                def one(like):
                    ap = c.ones[:, 0:1]
                    for _ in range(len(like.shape) - 2):
                        ap = ap.unsqueeze(2)
                    return ap.to_broadcast(list(like.shape))

                def split(chain, full, parts, done, ready):
                    def rest():
                        ready()
                        chain.add(nc.gpsimd.tensor_tensor(full, full, parts[0], ALU.subtract))

                    def second():
                        chain.wait()
                        chain.add(nc.gpsimd.tensor_tensor(parts[1], full, one(full), ALU.mult))

                    def third():
                        chain.wait()
                        nc.gpsimd.tensor_tensor(parts[2], full, parts[1], ALU.subtract).then_inc(done, 1)

                    return rest, second, third

                def split_k(chain, b):
                    return split(chain, k_full[:, :], [k_part[:, m, :] for m in range(PARTS)], parts_k,
                                 lambda: reach(pool, full_k, b + 1))

                def split_q(chain, b):
                    return split(chain, q_full[:, :], [q_part[:, m, :] for m in range(PARTS)], parts_q,
                                 lambda: reach(pool, full_q, b + 1))

                def split_v(chain, b, p):
                    full = v_full[:, :, :].rearrange("k t (h d) -> k t h d", h=H)
                    return split(chain, full, v_parts(p), parts_v, lambda: reach(pool, full_v, b + 1))

                def split_max(chain, b, g):
                    reach(pool, max_done, 2 * (H * b + 8 * g + 8))
                    reach(pool, turned_m, 2 * (b - 1) + g + 1)
                    parts = [m_part[:, g, :, :, m, :] for m in range(PARTS)]
                    neg = neg_max[:, g, :, :].rearrange("q t (r j) -> q t r j", r=2)
                    rest = m_rest[:, g, :, :].rearrange("q t (r j) -> q t r j", r=2)
                    chain.link(nc.gpsimd.tensor_tensor(parts[0], neg, one(neg), ALU.mult))
                    chain.link(nc.gpsimd.tensor_tensor(rest, neg, parts[0], ALU.subtract))
                    chain.link(nc.gpsimd.tensor_tensor(parts[1], rest, one(rest), ALU.mult))
                    nc.gpsimd.tensor_tensor(parts[2], rest, parts[1], ALU.subtract).then_inc(parts_m, 1)

                def residual(b, h):
                    n = H * b + h
                    reach(pool, e1_done, n + 1)
                    reach(pool, pv_done, n - 3)
                    e = h % EBUFS
                    nc.gpsimd.tensor_tensor(E2[:, e, SHARE:], E[:, e, SHARE:], E1[:, e, SHARE:], ALU.subtract).then_inc(e2_done, 1)

                nc.gpsimd.memset(KS[:, :, :, :], 1.0).then_inc(rows_of_ones, 1)
                if causal:
                    nc.gpsimd.memset(tri_f[:, :, :], 0.0).then_inc(setup_pool, 1)
                    pool.wait_ge(setup_pool, 1)
                    nc.gpsimd.affine_select(out=tri_f[:, 0, :], in_=tri_f[:, 0, :], compare_op=ALU.is_ge, fill=-1e30,
                                            base=0, pattern=[[-1, P]], channel_multiplier=1).then_inc(setup_pool, 1)
                    nc.gpsimd.affine_select(out=tri_f[:, 1, :], in_=tri_f[:, 1, :], compare_op=ALU.is_ge, fill=-1e30,
                                            base=0, pattern=[[1, P]], channel_multiplier=-1).then_inc(setup_pool, 1)
                else:
                    pool.wait_ge(setup, ANY_MASK)
                    nc.gpsimd.partition_all_reduce(any_mask[:, 2:3], any_mask[:, 1:2], P, bass.bass_isa.ReduceOp.max).then_inc(setup_pool, 1)
                chain = Count(pool, pool_step)
                for b in range(2):
                    for op in split_k(chain, b) + split_q(chain, b):
                        op()
                for op in split_v(chain, 0, 0):
                    op()
                split_max(chain, 0, 0)
                residual(0, 0)
                assert chain.n == FIRST_LINKS

                def step(bb, p, more=True, last=False):
                    i = 2 * bb + p
                    chain = Count(pool, pool_step, FIRST_LINKS + STEP_LINKS * i)
                    if not more and p:
                        chain.base -= 4
                    splits = dict(zip((7, 8, 9, 10, 11, 12), split_k(chain, i + 2) + split_q(chain, i + 2))) if more else {}
                    if not last:
                        splits.update(zip((13, 14, 15), split_v(chain, i + 1, 1 - p)))
                    for h in range(1, H + 1):
                        if h < H:
                            residual(i, h)
                        elif not last:
                            residual(i + 1, 0)
                        if h == LAG - 1:
                            split_max(chain, i, 1)
                        if h in splits:
                            splits[h]()
                        if h == LAG + 7 and not last:
                            split_max(chain, i + 1, 0)
                    assert chain.n == (STEP_LINKS if more else 3 if last else 8)

                with pool.Fori(0, 3) as bb:
                    for p in range(2):
                        step(bb, p)
                step(3, 0, more=False)
                step(3, 1, more=False, last=True)

            @block.vector
            def _(dve):
                for s, n in START.items():
                    dve.sem_inc(s, n)
                for m in range(PARTS):
                    at = (D + 1) * m + D
                    nc.vector.memset(V[:, :, :, :, at:at + 1], 1.0 if m == 0 else 0.0).then_inc(setup, 1)
                nc.vector.memset(attn[:, :, :], 0.0).then_inc(setup, 1)
                dve.wait_ge(loaded, LOADS)
                if causal:
                    dve.wait_ge(setup_pool, 3)
                    nc.vector.tensor_copy(tri[:, :, :], tri_f[:, :, :]).then_inc(setup, 1)
                    dve.wait_ge(lora_done, 1)
                    nc.vector.scalar_tensor_tensor(out=w[:, :, :], in0=misc[:, :].rearrange("p (n k) -> p n k", n=4), scalar=1.0 / 16.0,
                                                   in1=w[:, :, :], op0=ALU.mult, op1=ALU.add).then_inc(setup, 1)
                else:
                    nc.vector.tensor_scalar(E[:, 0:2, :], mask_f[:, :, :], 0.0, None, ALU.not_equal).then_inc(setup, 1)
                    dve.wait_ge(setup, 5)
                    nc.vector.tensor_reduce(any_mask[:, 1:2], E[:, 0:2, :], AX.XY, ALU.max).then_inc(setup, 1)
                    assert ANY_MASK == 6
                    dve.wait_ge(setup_pool, 1)
                    nc.vector.tensor_copy(any_mask_i[:, :], any_mask[:, 2:3]).then_inc(setup, 1)
                    dve.wait_ge(setup, SETUP)
                    any_here = dve.value_load(any_mask_i[0:1, 0:1], min_val=0, max_val=1)
                    with dve.If(any_here > 0):
                        chain = Count(dve, mask_step)
                        parts = [bfview[:, 0:6144].rearrange("p (l m k) -> p l m k", l=2, m=PARTS)[:, :, m, :] for m in range(PARTS)]
                        full = mask_f[:, :, :]
                        chain.link(nc.vector.tensor_copy(parts[0], full))
                        chain.link(nc.vector.tensor_tensor(full, full, parts[0], ALU.subtract))
                        chain.link(nc.vector.tensor_copy(parts[1], full))
                        nc.vector.tensor_tensor(parts[2], full, parts[1], ALU.subtract).then_inc(mask_ready, 1)

                def maximum(b, h):
                    n = H * b + h
                    j, par, _ = head(h)
                    g, col = j // 4, 4 * par + j % 4
                    if h % 8 == 0:
                        reach(dve, parts_m, 2 * (b - 1) + g + 1)
                    for t in range(TPB):
                        if causal:
                            reach(dve, logits_a, n + 1)
                            src = a_bank[h % 2][:, 0:P] if t == 0 else a_bank[h % 2][:, P:3 * P]
                        else:
                            reach(dve, logits_a, 2 * n + t + 1)
                            src = a_bank[t][:, :]
                        nc.vector.tensor_reduce(neg_max[:, g, t, col:col + 1], src, AX.X, ALU.max, negate=True).then_inc(max_done, 1)

                def first_part(b, h):
                    n = H * b + h
                    reach(dve, exp_done, NB * (n + 1))
                    reach(dve, pv_done, n - 3)
                    nc.vector.tensor_copy(E1[:, h % EBUFS, :], E[:, h % EBUFS, :]).then_inc(e1_done, 1)

                def residual(b, h):
                    n = H * b + h
                    reach(dve, e1_done, n + 1)
                    e = h % EBUFS
                    nc.vector.tensor_tensor(E2[:, e, 0:SHARE], E[:, e, 0:SHARE], E1[:, e, 0:SHARE], ALU.subtract).then_inc(e2_share, 1)

                def normalise(b):
                    reach(dve, pv_done, H * (b + 1))
                    for t in range(TPB):
                        nc.vector.tensor_reduce(heads[:, t, :, :], o_bank[t][:, 0:H * PVC].rearrange("q (h m c) -> q h c m", h=H, m=PARTS),
                                                AX.X, ALU.add).then_inc(o_free, 1)
                    reach(dve, o_free, 2 * (b + 1))
                    nc.vector.reciprocal(rsum[:, :, :], heads[:, :, :, D]).then_inc(norm_step, 1)
                    reach(dve, norm_step, b + 1)
                    reach(dve, turned_o, b + 1)
                    nc.vector.tensor_tensor(attn[:, :, :].rearrange("q t (h d) -> q t h d", h=H), heads[:, :, :, 0:D],
                                            rsum[:, :, :].unsqueeze(3).to_broadcast([P, TPB, H, D]), ALU.mult).then_inc(norm_done, 1)

                def add_to_x(b1):
                    reach(dve, out_o, b1 + 1)
                    xs = c.x[:, ds(TPB * b1, TPB), :]
                    nc.vector.tensor_tensor(xs, xs, misc[:, 0:TOK].rearrange("q (t d) -> q t d", t=TPB), ALU.add).then_inc(x_done, 1)

                def sum_ctx(bb, p):
                    dve.wait_ge(ctx_in[p], 16 * (bb + 1))
                    nc.vector.tensor_reduce(c.ctx_sum[:, ds(2 * bb + p, 1)], ctxT[:, p, :], AX.X, ALU.add).then_inc(summed, 1)

                if not causal:
                    sum_ctx(0, 0)
                    sum_ctx(0, 1)
                for h in range(H - LAG + 1):
                    maximum(0, h)
                first_part(0, 0)

                def step(bb, p, more=True, last=False):
                    i = 2 * bb + p
                    for h in range(1, H + 1):
                        if h < H:
                            if h < LAG or not last:
                                _, _, ah = logits_slot(bb, p, h)
                                maximum(i if h < LAG else i + 1, ah)
                            residual(i, h - 1)
                            first_part(i, h)
                        else:
                            residual(i, h - 1)
                            if not last:
                                maximum(i + 1, H - LAG)
                                first_part(i + 1, 0)
                            normalise(i)
                        if h == 3:
                            add_to_x(i)
                        if h == 8 and more and not causal:
                            sum_ctx(bb + 1, p)

                with dve.Fori(0, 3) as bb:
                    for p in range(2):
                        step(bb, p)
                step(3, 0, more=False)
                step(3, 1, more=False, last=True)
                add_to_x(B)

            @block.scalar
            def _(act):
                def exps(b, h):
                    n = H * b + h
                    for u in range(NB):
                        reach(act, logits_b, NB * n + u + 1)
                        if u == 0:
                            reach(act, e2_done, n - 3)
                            reach(act, e2_share, n - 3)
                        if causal:
                            nc.scalar.activation(E[:, h % EBUFS, :], b_bank[h % 2][:, 0:SPAN], ACT.Exp).then_inc(exp_done, 1)
                        else:
                            nc.scalar.activation(E[:, h % EBUFS, 512 * u:512 * u + 512], b_bank[u][:, :], ACT.Exp).then_inc(exp_done, 1)

                def keep_k(b):
                    reach(act, proj_k, b + 1)
                    reach(act, parts_k, b)
                    reach(act, out_k, 48 * b)
                    bias = bias_qk[:, 1:2] if causal else 0.0
                    nc.scalar.activation(k_part[:, 0, :], misc[:, 0:keys], ACT.Identity, bias=bias)
                    nc.scalar.activation(k_full[:, :], misc[:, 0:keys], ACT.Identity, bias=bias).then_inc(full_k, 1)

                def keep_q(b):
                    reach(act, proj_q, b + 1)
                    reach(act, parts_q, b)
                    reach(act, out_q, 48 * b)
                    bias = bias_q[:, :] if causal else 0.0
                    nc.scalar.activation(q_part[:, 0, :], misc[:, 0:TOK], ACT.Identity, bias=bias, scale=scale)
                    nc.scalar.activation(q_full[:, :], misc[:, 0:TOK], ACT.Identity, bias=bias, scale=scale).then_inc(full_q, 1)

                def keep_v(b, p):
                    reach(act, proj_v, b + 1)
                    reach(act, parts_v, b)
                    reach(act, pv_done, H * (b - 1))
                    nc.scalar.activation(v_parts(p)[0], misc[:, 0:keys].rearrange("k (t h d) -> k t h d", t=kt_n, h=H), ACT.Identity)
                    nc.scalar.copy(v_full[:, :, :], misc[:, 0:keys].rearrange("k (t c) -> k t c", t=kt_n)).then_inc(full_v, 1)

                def keep_max(b, g, other, count):
                    reach(act, turned_m, 2 * b + g + 1)
                    reach(act, aug[other][g], 32 * count)
                    nc.scalar.copy(m_rows[:, g, :], m_bank[:, :].bitcast(BF16)[0:2 * PARTS * 4, TOK * g:TOK * g + TOK]).then_inc(rows_m, 1)

                def keep_o(b1):
                    reach(act, turned_o, b1 + 1)
                    reach(act, out_o, b1)
                    nc.scalar.copy(attnT[:, :], misc[:, 0:TOK]).then_inc(kept_o, 1)

                if causal:
                    act.wait_ge(loaded, LOADS)
                    nc.scalar.mul(bias_q[:, :], bias_qk[:, 0:1], scale).then_inc(bias_scaled, 1)
                    act.wait_ge(bias_scaled, 1)
                for b in range(2):
                    keep_k(b)
                    keep_q(b)
                act.wait_ge(setup, 4)
                keep_v(0, 0)
                keep_max(0, 0, 1, 0)
                exps(0, 0)

                def step(bb, p, more=True, last=False):
                    i = 2 * bb + p
                    for h in range(1, H + 1):
                        if h < H:
                            exps(i, h)
                        elif not last:
                            exps(i + 1, 0)
                        if h == 2:
                            keep_o(i)
                        if h == LAG + 1:
                            keep_max(i, 1, 1 - p, bb + p)
                        if h == 6 and more:
                            keep_k(i + 2)
                        if h == 7 and more:
                            keep_q(i + 2)
                        if h == 9 and not last:
                            keep_v(i + 1, 1 - p)
                        if h == LAG + 9 and not last:
                            keep_max(i + 1, 0, p, bb + 1)

                with act.Fori(0, 3) as bb:
                    for p in range(2):
                        step(bb, p)
                step(3, 0, more=False)
                step(3, 1, more=False, last=True)
                keep_o(B)

            @block.tensor
            def _(pe):
                def project_k(bb, p):
                    pe.wait_ge(ctx_in[p], 16 * (bb + 1))
                    nc.tensor.matmul(misc[:, 0:keys], w[:, 1, :], ctxT[:, p, 0:keys], start=True, stop=True).then_inc(proj_k, 1)

                def project_q(b):
                    nc.tensor.matmul(misc[:, 0:TOK], w[:, 0, :], c.xnT[:, ds(TOK * b, TOK)], start=True, stop=True).then_inc(proj_q, 1)

                def project_v(p):
                    for t in range(kt_n):
                        out = misc[:, P * t:P * t + P]
                        last = nc.tensor.matmul(out, ctxT[:, p, P * t:P * t + P], w[:, 2, :], start=True, stop=not causal)
                        if causal:
                            last = nc.tensor.matmul(out, c.ones[0:1, :], bias_row[0:1, 0, :], start=False, stop=True)
                    last.then_inc(proj_v, 1)

                def logits_qk(masked, b, p, h, t):
                    n = H * b + h
                    j, _, row = head(h)
                    rows = slice(row, row + QROWS)
                    if causal:
                        reach(pe, max_done, 2 * n - 2)
                        for t in range(TPB):
                            out = a_bank[h % 2][:, P * t:P * t + P * (t + 1)]
                            nc.tensor.matmul(out, QS[rows, p, j, P * t:P * t + P], KS[rows, p, j, 0:P * (t + 1)], start=True, stop=True)
                            last = nc.tensor.matmul(a_bank[h % 2][:, 2 * P * t:2 * P * t + P], c.ident_bf[:, :], tri[:, 0, :],
                                                    start=False, stop=True, skip_group_check=True)
                        last.then_inc(logits_a, 1)
                        return
                    reach(pe, max_done, 2 * n + t - 1)
                    last = nc.tensor.matmul(a_bank[t][:, :], QS[rows, p, j, P * t:P * t + P], KS[rows, p, j, :], start=True, stop=True)
                    for m in range(PARTS if masked else 0):
                        last = nc.tensor.matmul(a_bank[t][:, :], c.ident_bf[:, :], mask_q[:, m, t, :], start=False, stop=True,
                                                skip_group_check=True)
                    last.then_inc(logits_a, 1)

                def logits_kq(masked, b, p, h, u):
                    n = NB * (H * b + h) + u
                    j, _, row = head(h)
                    rows = slice(row, row + AUG)
                    reach(pe, exp_done, n - 1)
                    if causal:
                        out = b_bank[h % 2]
                        for t in range(TPB):
                            nc.tensor.matmul(out[:, 2 * P * t:2 * P + P * t], KS[rows, p, j, P * t:P * t + P], QS[rows, p, j, P * t:TOK],
                                             start=True, stop=True)
                            last = nc.tensor.matmul(out[:, 2 * P * t:2 * P * t + P], c.ident_bf[:, :], tri[:, 1, :], start=False, stop=True,
                                                    skip_group_check=True)
                        last.then_inc(logits_b, 1)
                        return
                    for t in (2 * u, 2 * u + 1):
                        out = b_bank[u][:, TOK * (t % 2):TOK * (t % 2) + TOK]
                        last = nc.tensor.matmul(out, KS[rows, p, j, P * t:P * t + P], QS[rows, p, j, :], start=True, stop=True)
                        for m in range(PARTS if masked else 0):
                            last = nc.tensor.matmul(out, c.ident_bf[:, :], mask_k[:, m, t, :], start=False, stop=True,
                                                    skip_group_check=True)
                    last.then_inc(logits_b, 1)

                def weigh_v(b, p, h):
                    n = H * b + h
                    reach(pe, e2_done, n + 1)
                    reach(pe, e2_share, n + 1)
                    if h == 0:
                        reach(pe, o_free, 2 * b)
                        reach(pe, parts_v, b + 1)
                    for t in range(TPB):
                        key_tiles = range(t + 1) if causal else range(kt_n)
                        for k in key_tiles:
                            at = P * (t + k) if causal else TOK * k + P * t
                            for e in (E1, E2):
                                last = nc.tensor.matmul(o_bank[t][:, PVC * h:PVC * h + PVC], e[:, h % EBUFS, at:at + P], V[:, p, k, h, :],
                                                        start=(k == 0 and e is E1), stop=(k == key_tiles[-1] and e is E2))
                    last.then_inc(pv_done, 1)

                def turn_max(b, g):
                    reach(pe, parts_m, 2 * b + g + 1)
                    reach(pe, rows_m, 2 * (b - 1) + g + 1)
                    out = m_bank[:, :].bitcast(BF16)
                    for t in range(TPB):
                        last = nc.tensor.transpose(out[0:2 * PARTS * 4, TOK * g + P * t:TOK * g + P * t + P],
                                                   m_part[:, g, t, :, :, :].rearrange("q r m j -> q (r m j)"), c.ident_bf[:, :])
                    last.then_inc(turned_m, 1)

                def turn_o(b1):
                    reach(pe, norm_done, b1)
                    for t in range(TPB):
                        last = nc.tensor.transpose(misc[:, P * t:P * t + P], attn[:, t, :], c.ident[:, :])
                    last.then_inc(turned_o, 1)

                def project_o(b1):
                    reach(pe, kept_o, b1 + 1)
                    for t in range(TPB):
                        out = misc[:, P * t:P * t + P]
                        last = nc.tensor.matmul(out, attnT[:, P * t:P * t + P], w[:, 3, :], start=True, stop=not causal)
                        if causal:
                            last = nc.tensor.matmul(out, c.ones[0:1, :], bias_row[0:1, 1, :], start=False, stop=True)
                    last.then_inc(out_o, 1)

                def heads_together(masked, b, p, h, ab, ap, ah):
                    for u in range(2):
                        if u < NB and b is not None:
                            logits_kq(masked, b, p, h, u)
                        if u < NA and ab is not None:
                            logits_qk(masked, ab, ap, ah, u)

                def program(masked):
                    if masked:
                        pe.wait_ge(mask_ready, 1)
                    pe.wait_ge(stack[0], 64)
                    for h in range(H - LAG):
                        heads_together(masked, None, None, None, 0, 0, h)
                        if h == 8:
                            turn_max(0, 0)
                    reach(pe, aug[0][0], 32)
                    heads_together(masked, 0, 0, 0, 0, 0, H - LAG)

                    def step(bb, p, more=True, last=False):
                        i = 2 * bb + p
                        for h in range(1, H + 1):
                            if h == LAG and not last:
                                pe.wait_ge(stack[1 - p], 64 * (bb + p + 1))
                            if h == 8:
                                reach(pe, aug[p][1], 32 * (bb + 1))
                            if h < H:
                                with_a = h < LAG or not last
                                _, ap, ah = logits_slot(bb, p, h)
                                heads_together(masked, i, p, h, (i if h < LAG else i + 1) if with_a else None, ap, ah)
                            elif not last:
                                reach(pe, aug[1 - p][0], 32 * (bb + p + 1))
                                heads_together(masked, i + 1, 1 - p, 0, i + 1, 1 - p, H - LAG)
                            if h >= 2:
                                weigh_v(i, p, h - 2)
                            if h == H:
                                weigh_v(i, p, h - 1)
                            if h == 2:
                                reach(pe, full_v, i + 1)
                                turn_o(i)
                            if h == 3:
                                project_o(i)
                            if h == LAG + 1:
                                turn_max(i, 1)
                            if h == 6 and more:
                                reach(pe, x_done, i + 1)
                                project_k(bb + 1, p)
                            if h == 7 and more:
                                reach(pe, full_k, i + 3)
                                project_q(i + 2)
                            if h == 9 and not last:
                                if more:
                                    reach(pe, full_q, i + 3)
                                else:
                                    reach(pe, x_done, i + 1)
                                project_v(1 - p)
                            if h == LAG + 9 and not last:
                                turn_max(i + 1, 0)

                    with pe.Fori(0, 3) as bb:
                        for p in range(2):
                            step(bb, p)
                    step(3, 0, more=False)
                    step(3, 1, more=False, last=True)
                    reach(pe, x_done, B)
                    turn_o(B)
                    project_o(B)

                pe.wait_ge(loaded, LOADS)
                if causal:
                    for n, (a, b) in enumerate(((0, 0), (1, 1), (1, 2), (2, 3))):
                        last = nc.tensor.matmul(misc[:, P * n:P * n + P], lora_a[:, a, :], lora_b[:, b, :], start=True, stop=True)
                    last.then_inc(lora_done, 1)
                if causal:
                    pe.wait_ge(setup, SETUP)
                for p in range(2):
                    project_k(0, p)
                    reach(pe, full_k, p + 1)
                    project_q(p)
                    reach(pe, full_q, p + 1)
                project_v(0)
                pe.wait_ge(setup, SETUP)
                if causal:
                    program(False)
                else:
                    masked = pe.value_load(any_mask_i[0:1, 0:1], min_val=0, max_val=1)
                    with pe.If(masked > 0):
                        program(True)
                    with pe.Else():
                        program(False)


CHUNK = 512
NC = N // CHUNK
TPC = CHUNK // P
E0 = 16
HID0 = 8 + 2


def dense_block(c, ph, up, gate, down, weighted, router, hidden):
    nc = c.nc
    tiles = len(up)
    order = list(range(weighted, tiles)) + list(range(weighted))
    r = ph.sb("relu", [P, 3, CHUNK], F32)
    prod = ph.sb("prod", [P, 2, CHUNK], F32)
    hT = hidden[:, 0:2 * tiles * CHUNK].rearrange("p (b i t) -> p b i t", b=2, i=tiles)
    up_bank, side_bank, down_bank = c.bank[0:2], c.bank[2:4], c.bank[4:6]
    sides = tiles if gate else weighted
    up_done, side_done, act_done, prod_done, h_done = (ph.sem(n) for n in ("up_done", "side_done", "act_done", "prod_done", "h_done"))
    down_done, x_done = ph.sem("down_done"), ph.sem("x_done")
    if gate:
        h_done = prod_done
    X_AT = 4

    def side_number(q, k):
        if gate:
            return tiles * q + k
        return None if order[k] >= weighted else weighted * q + k - (tiles - weighted)

    with nc.Block() as block:
        @block.sync
        def _(sp):
            router.loads(sp)

        @block.tensor
        def _(pe):
            def up_product(q, k):
                n, i, m = tiles * q + k, order[k], side_number(q, k)
                need(pe, act_done if not gate else prod_done, n - 1)
                rhs = c.xnT[:, CHUNK * q:CHUNK * q + CHUNK]
                nc.tensor.matmul(up_bank[n % 2][:, :], up[i], rhs, start=True, stop=True).then_inc(up_done, 1)
                if m is None:
                    return
                need(pe, act_done if gate else prod_done, m - 1)
                if gate:
                    nc.tensor.matmul(side_bank[m % 2][:, :], gate[i], rhs, start=True, stop=True).then_inc(side_done, 1)
                else:
                    lhsT, rows = router.scale_rows(i, q)
                    nc.tensor.matmul(side_bank[m % 2][:, :], lhsT, rows, start=True, stop=True).then_inc(side_done, 1)

            def down_product(q):
                pe.wait_ge(h_done, tiles * (q + 1))
                need(pe, x_done, q - 1)
                for t in range(TPC):
                    for i in range(tiles):
                        last = nc.tensor.matmul(down_bank[q % 2][:, P * t:P * t + P], hT[:, q % 2, i, P * t:P * t + P], down[i],
                                                start=(i == 0), stop=(i == tiles - 1))
                last.then_inc(down_done, 1)

            router.pe(pe)
            for q in range(NC):
                for k in range(tiles):
                    if q == 0 and k == tiles - weighted and not gate:
                        router.pe_weights(pe)
                    up_product(q, k)
                    if k == 1 and q:
                        down_product(q - 1)
            down_product(NC - 1)

        @block.scalar
        def _(act):
            router.act(act)
            for q in range(NC):
                for k in range(tiles):
                    n = tiles * q + k
                    if q == 0 and k == tiles - weighted and not gate:
                        router.act_weights(act)
                    if gate:
                        act.wait_ge(side_done, n + 1)
                        need(act, h_done, n - 2)
                        nc.scalar.activation(r[:, n % 3, :], side_bank[n % 2][:, :], ACT.Silu).then_inc(act_done, 1)
                    else:
                        act.wait_ge(up_done, n + 1)
                        need(act, h_done, n - 2)
                        nc.scalar.activation(r[:, n % 3, :], up_bank[n % 2][:, :], ACT.Relu).then_inc(act_done, 1)

        @block.vector
        def _(dve):
            def add_to_x(q):
                dve.wait_ge(down_done, q + 1)
                xs = c.x[:, TPB + TPC * q:TPB + TPC * (q + 1), :]
                nc.vector.tensor_tensor(xs, xs, down_bank[q % 2][:, :].rearrange("p (t d) -> p t d", t=TPC), ALU.add).then_inc(x_done, 1)

            router.dve(dve)
            for q in range(NC):
                for k in range(tiles):
                    n, m = tiles * q + k, side_number(q, k)
                    if k == min(X_AT, tiles - 1) and q:
                        add_to_x(q - 1)
                    if m is None:
                        continue
                    dve.wait_ge(act_done, n + 1)
                    if gate:
                        dve.wait_ge(up_done, n + 1)
                        need(dve, down_done, q - 1)
                        nc.vector.tensor_tensor(hT[:, q % 2, k, :], r[:, n % 3, :], up_bank[n % 2][:, :], ALU.mult).then_inc(prod_done, 1)
                    else:
                        dve.wait_ge(side_done, m + 1)
                        need(dve, h_done, n - 1)
                        nc.vector.tensor_tensor(prod[:, m % 2, :], r[:, n % 3, :], side_bank[m % 2][:, :], ALU.mult).then_inc(prod_done, 1)
            add_to_x(NC - 1)

        @block.gpsimd
        def _(pool):
            router.pool(pool)
            if not gate:
                for q in range(NC):
                    for k in range(tiles):
                        n, m = tiles * q + k, side_number(q, k)
                        need(pool, down_done, q - 1)
                        if m is None:
                            pool.wait_ge(act_done, n + 1)
                            first = r[:, n % 3, :]
                        else:
                            pool.wait_ge(prod_done, m + 1)
                            first = prod[:, m % 2, :]
                        nc.gpsimd.tensor_tensor(hT[:, q % 2, order[k], :], first, r[:, n % 3, :], ALU.mult).then_inc(h_done, 1)


class Router0:

    def __init__(self, c, ph, arg):
        self.c, self.arg = c, arg
        self.w = c.wa[:, L0_AT + 2 * HID0 * P:L0_AT + 2 * HID0 * P + E0]
        sb = ph.sb
        self.bias = sb("bias", [P, E0], F32)
        self.spread_f = sb("spread_f", [PARTS * E0, 8 * P], F32)
        self.spread = sb("spread", [PARTS * E0, 8 * P], BF16)
        self.scores = sb("scores", [P, NT, E0], F32)
        self.sc = sb("sc", [P, NT, E0], F32)
        self.pair = sb("pair", [P, 6, NT * 4], F32)
        self.group = sb("group", [P, NT, 4], F32)
        self.beats = sb("beats", [P, 2, NT, 4, 4], F32)
        self.rank = sb("rank", [P, NT, 4], F32)
        self.masked = sb("masked", [P, NT, E0], F32)
        self.top = sb("top", [P, NT, 8], F32)
        self.at = sb("at", [P, NT, 8], U32)
        self.at_f = sb("at_f", [P, NT, 4], F32)
        self.hot = sb("hot", [P, NT, 4, E0], F32)
        self.weight = sb("weight", [P, NT, E0], F32)
        self.den = sb("den", [P, NT], F32)
        self.part = sb("part", [P, NT, PARTS, E0], BF16)
        self.partT = sb("partT", [PARTS * E0, N], BF16)
        self.loaded, self.logits, self.scored = ph.sem("r_loaded"), ph.sem("r_logits"), ph.sem("r_scored")
        self.step, self.ready = ph.sem("r_step"), ph.sem("r_ready")
        self.turned, self.kept, self.copied = ph.sem("r_turned"), ph.sem("r_kept"), ph.sem("r_copied")

    def loads(self, sp):
        sp.dma_start(self.bias[:, :], self.arg["f0_bias"]).then_inc(self.loaded, 16)
        sp.dma_start(self.spread_f[:, :], self.arg["spread0"]).then_inc(self.loaded, 16)

    def pe(self, pe):
        nc, c = self.c.nc, self.c
        pe.wait_ge(c.w0_in, 16)
        for t in range(NT):
            last = nc.tensor.matmul(c.bank[7][:, E0 * t:E0 * t + E0], c.xnT[:, P * t:P * t + P], self.w, start=True, stop=True)
        last.then_inc(self.logits, 1)

    def pe_weights(self, pe):
        nc, c = self.c.nc, self.c
        pe.wait_ge(self.ready, 1)
        for t in range(NT):
            out = c.bank[6 + t // 8][:, :].bitcast(BF16)[0:PARTS * E0, P * (t % 8):P * (t % 8) + P]
            last = nc.tensor.transpose(out, self.part[:, t, :, :].rearrange("p m e -> p (m e)"), c.ident_bf[:, :])
            if t % 8 == 7:
                last.then_inc(self.turned, 1)
        pe.wait_ge(self.kept, 2)
        pe.wait_ge(self.copied, 1)

    def scale_rows(self, i, q):
        return self.spread[:, P * i:P * i + P], self.partT[:, CHUNK * q:CHUNK * q + CHUNK]

    def act(self, act):
        nc, c = self.c.nc, self.c
        act.wait_ge(self.logits, 1)
        nc.scalar.activation(self.scores[:, :, :], c.bank[7][:, 0:NT * E0].rearrange("p (t e) -> p t e", t=NT), ACT.Sigmoid).then_inc(self.scored, 1)

    def act_weights(self, act):
        nc, c = self.c.nc, self.c
        for half in range(2):
            act.wait_ge(self.turned, half + 1)
            nc.scalar.copy(self.partT[:, 1024 * half:1024 * half + 1024],
                           c.bank[6 + half][:, :].bitcast(BF16)[0:PARTS * E0, :]).then_inc(self.kept, 1)

    def pool(self, pool):
        pool.wait_ge(self.loaded, 32)
        self.c.nc.gpsimd.tensor_copy(self.spread[:, :], self.spread_f[:, :]).then_inc(self.copied, 1)

    def dve(self, dve):
        nc, c = self.c.nc, self.c
        v = nc.vector
        step = Count(dve, self.step)
        dve.wait_ge(self.loaded, 32)
        dve.wait_ge(self.scored, 1)
        step.link(v.tensor_tensor(self.sc[:, :, :], self.scores[:, :, :], self.bias[:, :].unsqueeze(1).to_broadcast([P, NT, E0]), ALU.add))
        a, b, cc, d = (self.sc[:, :, :].rearrange("p t (g m) -> p (t g) m", g=4)[:, :, m] for m in range(4))
        hi1, lo1, hi2, lo2, both, rest = (self.pair[:, m, :] for m in range(6))
        step.add(v.tensor_tensor(hi1, a, b, ALU.max))
        step.add(v.tensor_tensor(lo1, a, b, ALU.min))
        step.add(v.tensor_tensor(hi2, cc, d, ALU.max))
        step.link(v.tensor_tensor(lo2, cc, d, ALU.min))
        step.add(v.tensor_tensor(both, hi1, hi2, ALU.min))
        step.add(v.tensor_tensor(rest, lo1, lo2, ALU.max))
        step.link(v.tensor_tensor(hi1, hi1, hi2, ALU.max))
        step.link(v.tensor_tensor(both, both, rest, ALU.max))
        group = self.group[:, :, :]
        step.link(v.tensor_tensor(group.rearrange("p t g -> p (t g)"), hi1, both, ALU.add))
        mine = group.unsqueeze(3).to_broadcast([P, NT, 4, 4])
        other = group.unsqueeze(2).to_broadcast([P, NT, 4, 4])
        more, same = self.beats[:, 0, :, :, :], self.beats[:, 1, :, :, :]
        before = c.const[:, BEFORE_AT:BEFORE_AT + 16].rearrange("p (g h) -> p g h", g=4).unsqueeze(1).to_broadcast([P, NT, 4, 4])
        step.add(v.tensor_tensor(more, other, mine, ALU.is_gt))
        step.link(v.tensor_tensor(same, other, mine, ALU.is_ge))
        step.link(v.tensor_tensor(same, same, before, ALU.mult))
        step.link(v.tensor_tensor(more, more, same, ALU.max))
        step.link(v.tensor_reduce(self.rank[:, :, :], more, AX.X, ALU.add))
        step.link(v.tensor_scalar(self.rank[:, :, :], self.rank[:, :, :], 1.5, None, ALU.is_lt))
        step.link(v.tensor_tensor(self.masked[:, :, :].rearrange("p t (g m) -> p t g m", g=4), self.sc[:, :, :].rearrange("p t (g m) -> p t g m", g=4),
                                  self.rank[:, :, :].unsqueeze(3).to_broadcast([P, NT, 4, 4]), ALU.mult))
        for t in range(NT):
            step.add(v.max(self.top[:, t, :], self.masked[:, t, :]))
        step.wait()
        for t in range(NT):
            step.add(v.max_index(self.at[:, t, :], self.top[:, t, :], self.masked[:, t, :]))
        step.wait()
        step.link(v.tensor_copy(self.at_f[:, :, :], self.at[:, :, 0:4]))
        step.link(v.tensor_tensor(self.hot[:, :, :, :], c.const[:, IOTA_AT:IOTA_AT + E0].unsqueeze(1).unsqueeze(1).to_broadcast([P, NT, 4, E0]),
                                  self.at_f[:, :, :].unsqueeze(3).to_broadcast([P, NT, 4, E0]), ALU.is_equal))
        step.link(v.tensor_reduce(self.weight[:, :, :], self.hot[:, :, :, :].rearrange("p t k e -> p t e k"), AX.X, ALU.add))
        weight = self.weight[:, :, :]
        step.link(v.tensor_tensor(weight, weight, self.scores[:, :, :], ALU.mult))
        step.link(v.tensor_reduce(self.den[:, :], weight, AX.X, ALU.add))
        step.link(v.tensor_scalar(self.den[:, :], self.den[:, :], 1e-20, None, ALU.add))
        step.link(v.reciprocal(self.den[:, :], self.den[:, :]))
        step.link(v.scalar_tensor_tensor(out=weight, in0=weight, scalar=ROUTED_SCALE, in1=self.den[:, :].unsqueeze(2).to_broadcast([P, NT, E0]),
                                         op0=ALU.mult, op1=ALU.mult))
        part = [self.part[:, :, m, :] for m in range(PARTS)]
        step.link(v.tensor_copy(part[0], weight))
        step.link(v.tensor_tensor(weight, weight, part[0], ALU.subtract))
        step.link(v.tensor_copy(part[1], weight))
        v.tensor_tensor(part[2], weight, part[1], ALU.subtract).then_inc(self.ready, 1)


def layer0_ffn(c, arg):
    with Phase(c, "f0_") as ph:
        router = Router0(c, ph, arg)
        up = [c.wa[:, L0_AT + P * i:L0_AT + P * i + P] for i in range(HID0)]
        down = [c.wa[:, L0_AT + P * (HID0 + i):L0_AT + P * (HID0 + i) + P] for i in range(HID0)]
        dense_block(c, ph, up, None, down, 8, router, c.wb)


def layer1_attention(c, arg):
    nc = c.nc
    with Phase(c, "a1_") as ph:
        w = ph.sb("w", [P, 2, P], F32)
        bias = ph.sb("bias", [1, P], F32)
        one_hot = ph.sb("one_hot", [B, B, P], F32)
        mean = ph.sb("mean", [P, B], F32)
        rows = ph.sb("rows", [B, P], F32)
        loaded, mean_ready, rows_out, rows_ready, out_done = (ph.sem(n) for n in ("loaded", "mean", "rows_out", "rows_ready", "out_done"))
        with nc.Block() as block:
            @block.sync
            def _(sp):
                sp.dma_start(w[:, :, :], arg["a1_w"].rearrange("n p d -> p n d")).then_inc(loaded, 16)
                sp.dma_start(bias[:, :], arg["a1_bias"]).then_inc(loaded, 16)
                sp.dma_start(one_hot[:, :, :], arg["one_hot8"]).then_inc(loaded, 16)
                cols = E_GATED * GATED_COLS // 8
                for n in range(8):
                    sp.dma_start(c.wb[:, cols * n:cols * n + cols], arg["f2_w"][:, cols * n:cols * n + cols]).then_inc(c.w2_in, 16)

            @block.tensor
            def _(pe):
                pe.wait_ge(loaded, 48)
                pe.wait_ge(mean_ready, 1)
                nc.tensor.matmul(c.bank[7][0:B, 0:P], mean[:, :], w[:, 1, :], start=True, stop=False)
                nc.tensor.matmul(c.bank[7][0:B, 0:P], c.ones[0:1, 0:B], bias[:, :], start=False, stop=True).then_inc(rows_out, 1)
                pe.wait_ge(rows_ready, 1)
                for t in range(NT):
                    out = c.bank[t // 4][:, P * (t % 4):P * (t % 4) + P]
                    nc.tensor.matmul(out, c.xnT[:, P * t:P * t + P], w[:, 0, :], start=True, stop=False)
                    nc.tensor.matmul(out, one_hot[:, t // TPB, :], rows[:, :], start=False, stop=True).then_inc(out_done, 1)

            @block.scalar
            def _(act):
                nc.scalar.mul(mean[:, :], c.ctx_sum[:, :], 1.0 / CTX).then_inc(mean_ready, 1)
                act.wait_ge(rows_out, 1)
                nc.scalar.copy(rows[:, :], c.bank[7][0:B, 0:P]).then_inc(rows_ready, 1)

            @block.vector
            def _(dve):
                for q in range(NT // 4):
                    dve.wait_ge(out_done, 4 * (q + 1))
                    xs = c.x[:, TPB + 4 * q:TPB + 4 * q + 4, :]
                    nc.vector.tensor_tensor(xs, xs, c.bank[q][:, :].rearrange("p (t d) -> p t d", t=4), ALU.add)


class NoRouter:

    def __init__(self, c):
        self.c = c

    def pe(self, pe):
        pe.wait_ge(self.c.w1_in, 16 * 8)

    def loads(self, sp): pass
    def act(self, act): pass
    def dve(self, dve): pass
    def pool(self, pool): pass


def layer1_shared(c, arg):
    with Phase(c, "s1_") as ph:
        at = (E_GATED - 1) * GATED_COLS
        gate, up, down = ([c.wa[:, at + first + P * i:at + first + P * i + P] for i in range(4)] for first in (0, HID, 2 * HID))
        dense_block(c, ph, up, gate, down, 0, NoRouter(c), c.wa[:, L0_AT:])


def layer3_attention(c, arg):
    nc = c.nc
    KT = CTX // P
    with Phase(c, "a3_") as ph:
        sb, sem = ph.sb, ph.sem
        w = sb("w", [P, 4, P], F32)
        bias_qk = sb("bias_qk", [P, 2], F32)
        bias_q = sb("bias_q", [P, 1], F32)
        bias_vo = sb("bias_vo", [P, 2, P], F32)
        ctxT = sb("ctxT", [P, 2, CTX], F32)
        qT = sb("qT", [P, 2, TOK], F32)
        kT = sb("kT", [P, 2, CTX], F32)
        v = sb("v", [P, 2, KT, P], F32)
        neg_max = sb("neg_max", [P, 2, TPB], F32)
        total = sb("total", [P, 2, TPB], F32)
        inverse = sb("inverse", [P, 2, TPB], F32)
        prob = sb("prob", [P, 2, TPB, CTX], F32)
        probT = sb("probT", [P, KT, TOK], F32)
        headT = sb("headT", [P, TOK], F32)
        loaded, biased = sem("loaded"), sem("biased")
        ctx_in = [sem(f"ctx_in{p}") for p in range(2)]
        proj_q, proj_k, proj_v = sem("proj_q"), sem("proj_k"), sem("proj_v")
        full_q, full_k, full_v = sem("full_q"), sem("full_k"), sem("full_v")
        logits, max_done, exp_done = sem("logits"), sem("max_done"), sem("exp_done")
        turned, kept = sem("turned"), sem("kept")
        head_out, head_kept, out_done = sem("head_out"), sem("head_kept"), sem("out_done")
        inv_done, x_done, bias_added = sem("inv_done"), sem("x_done"), sem("bias_added")
        k_bank, q_bank, v_bank, l_bank, p_bank, o_bank = c.bank[0], c.bank[1], c.bank[2], c.bank[3:5], c.bank[5:7], c.bank[7]
        scale = float(P) ** -0.5

        def slots(eng, first, step, last):
            for b in first:
                step(b, b % 2, b // 2)
            with eng.Fori(1, 3) as g:
                for p in range(2):
                    step(2 * g + p, p, g)
            for b in last:
                step(b, b % 2, b // 2)

        with nc.Block() as block:
            @block.sync
            def _(sp):
                for n, name in enumerate(("wq", "wk", "wv", "wo")):
                    sp.dma_start(w[:, n, :], arg["a3_" + name]).then_inc(loaded, 16)
                sp.dma_start(bias_qk[:, :], arg["a3_bias_qk"]).then_inc(loaded, 16)
                sp.dma_start(bias_vo[:, :, :], arg["a3_bias_vo"]).then_inc(loaded, 16)

                def step(b, p, g):
                    need(sp, proj_k, b - 1)
                    need(sp, proj_v, b - 1)
                    sp.dma_start(ctxT[:, p, :], arg["ctxT"][:, ds(b, 1), :].rearrange("d o k -> d (o k)")).then_inc(ctx_in[p], 16)

                slots(sp, (0, 1), step, (6, 7))

            @block.tensor
            def _(pe):
                def project(b, p, g):
                    pe.wait_ge(ctx_in[p], 16 * g + 16)
                    need(pe, full_k, b)
                    nc.tensor.matmul(k_bank[:, :], w[:, 1, :], ctxT[:, p, :], start=True, stop=True).then_inc(proj_k, 1)
                    need(pe, full_q, b)
                    nc.tensor.matmul(q_bank[:, 0:TOK], w[:, 0, :], c.xnT[:, ds(TOK * b, TOK)], start=True, stop=True).then_inc(proj_q, 1)
                    need(pe, full_v, b)
                    for t in range(KT):
                        last = nc.tensor.matmul(v_bank[:, P * t:P * t + P], ctxT[:, p, P * t:P * t + P], w[:, 2, :], start=True, stop=True)
                    last.then_inc(proj_v, 1)

                def find_logits(b, p, g):
                    pe.wait_ge(full_q, b + 1)
                    pe.wait_ge(full_k, b + 1)
                    for t in range(TPB):
                        need(pe, exp_done, 2 * b + t - 1)
                        nc.tensor.matmul(l_bank[t][:, :], qT[:, p, P * t:P * t + P], kT[:, p, :], start=True, stop=True).then_inc(logits, 1)

                def turn(b, p, g):
                    for t in range(TPB):
                        pe.wait_ge(exp_done, 2 * b + t + 1)
                        need(pe, kept, 2 * b + t - 1)
                        for k in range(KT):
                            last = nc.tensor.transpose(p_bank[t][:, P * k:P * k + P], prob[:, p, t, P * k:P * k + P], c.ident[:, :])
                        last.then_inc(turned, 1)

                def weigh(b, p, g):
                    pe.wait_ge(kept, 2 * b + 2)
                    pe.wait_ge(full_v, b + 1)
                    need(pe, x_done, b)
                    for k in range(KT):
                        last = nc.tensor.matmul(o_bank[:, 0:TOK], v[:, p, k, :], probT[:, k, :], start=(k == 0), stop=(k == KT - 1))
                    last.then_inc(head_out, 1)

                def project_out(b, p, g):
                    pe.wait_ge(head_kept, b + 1)
                    for t in range(TPB):
                        last = nc.tensor.matmul(o_bank[:, TOK + P * t:TOK + P * t + P], headT[:, P * t:P * t + P], w[:, 3, :],
                                                start=True, stop=True)
                    last.then_inc(out_done, 1)

                def step(b, p, g):
                    turn(b, p, g)
                    if not isinstance(b, int) or b < B - 1:
                        project(b + 1, 1 - p, g + p)
                    weigh(b, p, g)
                    if not isinstance(b, int) or b < B - 1:
                        find_logits(b + 1, 1 - p, g + p)
                    project_out(b, p, g)

                pe.wait_ge(loaded, 96)
                project(0, 0, 0)
                find_logits(0, 0, 0)
                slots(pe, (0, 1), step, (6, 7))

            @block.scalar
            def _(act):
                def project(b, p, g):
                    act.wait_ge(proj_k, b + 1)
                    need(act, logits, 2 * b - 2)
                    nc.scalar.activation(kT[:, p, :], k_bank[:, :], ACT.Identity, bias=bias_qk[:, 1:2]).then_inc(full_k, 1)
                    act.wait_ge(proj_q, b + 1)
                    nc.scalar.activation(qT[:, p, :], q_bank[:, 0:TOK], ACT.Identity, bias=bias_q[:, :], scale=scale).then_inc(full_q, 1)

                def exps(b, p, g):
                    for t in range(TPB):
                        act.wait_ge(max_done, 2 * b + t + 1)
                        need(act, turned, 2 * b - 3 + t)
                        need(act, inv_done, b - 1)
                        nc.scalar.activation(prob[:, p, t, :], l_bank[t][:, :], ACT.Exp, bias=neg_max[:, p, t:t + 1],
                                             accum_out=total[:, p, t:t + 1]).then_inc(exp_done, 1)

                def step(b, p, g):
                    more = not isinstance(b, int) or b < B - 1
                    if more:
                        project(b + 1, 1 - p, g + p)
                    act.wait_ge(head_out, b + 1)
                    need(act, out_done, b)
                    nc.scalar.copy(headT[:, :], o_bank[:, 0:TOK]).then_inc(head_kept, 1)
                    if more:
                        exps(b + 1, 1 - p, g + p)

                act.wait_ge(loaded, 96)
                nc.scalar.mul(bias_q[:, :], bias_qk[:, 0:1], scale).then_inc(biased, 1)
                act.wait_ge(biased, 1)
                project(0, 0, 0)
                exps(0, 0, 0)
                slots(act, (0, 1), step, (6, 7))

            @block.vector
            def _(dve):
                def keep_v(b, p, g):
                    dve.wait_ge(proj_v, b + 1)
                    need(dve, head_out, b - 1)
                    nc.vector.tensor_tensor(v[:, p, :, :], v_bank[:, :].rearrange("p (t d) -> p t d", t=KT),
                                            bias_vo[:, 0:1, :].to_broadcast([P, KT, P]), ALU.add).then_inc(full_v, 1)

                def maxima(b, p, g):
                    for t in range(TPB):
                        dve.wait_ge(logits, 2 * b + t + 1)
                        nc.vector.tensor_reduce(neg_max[:, p, t:t + 1], l_bank[t][:, :], AX.X, ALU.max, negate=True).then_inc(max_done, 1)

                def step(b, p, g):
                    more = not isinstance(b, int) or b < B - 1
                    for t in range(TPB):
                        dve.wait_ge(turned, 2 * b + t + 1)
                        need(dve, head_out, b)
                        nc.vector.tensor_copy(probT[:, :, P * t:P * t + P], p_bank[t][:, :].rearrange("p (k q) -> p k q", k=KT)).then_inc(kept, 1)
                    nc.vector.reciprocal(inverse[:, p, :], total[:, p, :]).then_inc(inv_done, 1)
                    if more:
                        keep_v(b + 1, 1 - p, g + p)
                        maxima(b + 1, 1 - p, g + p)
                    dve.wait_ge(out_done, b + 1)
                    dve.wait_ge(inv_done, b + 1)
                    dve.wait_ge(bias_added, 1)
                    for t in range(TPB):
                        xs = c.x[:, ds(TPB * b + TPB + t, 1), :].rearrange("p o d -> p (o d)")
                        last = nc.vector.scalar_tensor_tensor(out=xs, in0=o_bank[:, TOK + P * t:TOK + P * t + P], scalar=inverse[:, p, t:t + 1],
                                                              in1=xs, op0=ALU.mult, op1=ALU.add)
                    last.then_inc(x_done, 1)

                dve.wait_ge(loaded, 96)
                keep_v(0, 0, 0)
                maxima(0, 0, 0)
                slots(dve, (0, 1), step, (6, 7))

            @block.gpsimd
            def _(pool):
                pool.wait_ge(loaded, 96)
                xs = c.x[:, TPB:, :]
                nc.gpsimd.tensor_tensor(xs, xs, bias_vo[:, 1:2, :].to_broadcast([P, NT, P]), ALU.add).then_inc(bias_added, 1)


class Experts:

    def __init__(self, layer):
        self.layer = layer
        self.gated = layer != 3
        self.E = E3 if layer == 3 else E_GATED
        self.K = {1: 1, 2: 2, 3: 4}[layer]
        self.last = self.E - 2 if layer == 1 else self.E - 1
        self.before = {1: 0, 2: NT, 3: 3 * NT}[layer]
        self.cols = GATED_COLS if self.gated else 2 * P
        self.tiles = N * self.K // P + self.E
        self.per_step = 1 if self.gated else 4
        self.steps = self.tiles // self.per_step
        assert self.steps % 4 == 0 and self.tiles * P <= TABLE and self.tiles <= P


def in_slots(nc, eng, T, slot):
    for k in range(6):
        slot(0, k)
    with eng.Fori(4, T - 4, 4) as s:
        s = nc.s_assert_within(s, 4, T - 8, skip_runtime_bounds_check_because="the loop goes by fours")
        for k in range(2, 6):
            slot(s, k)
    for k in range(2, 6):
        slot(T - 4, k)


def experts_phase(c, layer, arg):
    nc = c.nc
    m = Experts(layer)
    E, K, T, W = m.E, m.K, m.steps, m.per_step * P
    weights, weights_in = (c.wb, c.w2_in) if layer == 2 else (c.wa, c.w1_in if layer == 1 else c.w3_in)
    with Phase(c, f"e{layer}_") as ph:
        sb, sem = ph.sb, ph.sem
        w_router = sb("w_router", [P, E], F32)
        key = sb("key", [P, NT, E], F32)
        top = sb("top", [P, NT, 8], F32)
        at = sb("at", [P, NT, 8], U32)
        at_f = sb("at_f", [P, NT, K], F32)
        gate = sb("gate", [P, NT, K], F32)
        small = sb("small", [P, 2, NT], F32)
        hot = sb("hot", [P, NT, K, E], BF16)
        chosen = sb("chosen", [P, NT, E], BF16)
        sums = sb("sums", [P, 2, NT + 1, E], BF16)
        tri = sb("tri", [P, P], BF16)
        ones_bf = sb("ones_bf", [P, P], BF16)
        tiles_i = sb("tiles_i", [P, E], I32)
        cum = sb("cum", [P, 3, E], F32)
        place = sb("place", [P, NT, E], F32)
        if layer == 3:
            spread = c.wb[:, 0:NT * K * E].rearrange("p (t k e) -> p t k e", t=NT, k=K)
        else:
            spread = sb("spread", [P, NT, K, E], F32)[:, :, :, :]
        pos_f = sb("pos_f", [P, NT * K], F32)
        pos = sb("pos", [P, NT * K], I32)
        owner_f = sb("owner_f", [P, 2], F32)
        owner_i = sb("owner_i", [P, 1], I32)
        owner = sb("owner", [1, P], I32)
        xs = sb("xs", [P, 4, W], F32)
        xT = sb("xT", [P, 2, W], F32)
        silu = sb("silu", [P, 2, HID], F32) if m.gated else None
        h = sb("h", [P, 2, HID], F32)
        hT = sb("hT", [P, 2, HID], F32)
        y = sb("y", [P, 4, W], F32)
        back = sb("back", [P, 8, P], F32)

        rows_out = nc.dram_tensor(f"rows_out{layer}", [m.tiles * P, P], F32)

        loaded, logits_done, key_done, step_done = sem("loaded"), sem("logits_done"), sem("key_done"), sem("step_done")
        const_bf, sums_done, counted, pos_done = sem("const_bf"), sem("sums_done"), sem("counted"), sem("pos_done")
        silu_go, gate_go = sem("silu_go"), sem("gate_go")
        owner_done, owner_in = sem("owner_done"), sem("owner_in")
        x_in = [sem(f"x_in{k}") for k in range(4)]
        turned_x, xT_ready, up_done, silu_done, h_done = (sem(n) for n in ("turned_x", "xT_ready", "up_done", "silu_done", "h_done"))
        turned_h, hT_ready, down_done, y_ready = (sem(n) for n in ("turned_h", "hT_ready", "down_done", "y_ready"))
        stored = [sem(f"stored{k}") for k in range(4)]
        back_used = sem("back_used")
        x_bank, h_bank, y_bank = c.bank[4], c.bank[6], (c.bank[5], c.bank[7])

        def rows_of(table, s):
            rows = table[ds(W * s, W), :]
            return rows.rearrange("(j p) d -> p j d", p=P)

        def columns(buffer, k):
            return buffer[:, k % 4, :].rearrange("p (j d) -> p j d", d=P)

        def alive(s, k, d=0):
            return not isinstance(s, int) or 0 <= s + k + d < T

        with nc.Block() as block:
            @block.sync
            def _(sp):
                sp.dma_start(w_router[:, :], arg[f"e{layer}_router"]).then_inc(loaded, 16)
                sp.wait_ge(owner_done, 1)
                sp.dma_start(owner[:, :], owner_i[:, :]).then_inc(owner_in, 16)

                def load(s, k):
                    need(sp, turned_x, s + k - 3)
                    sp.dma_start(columns(xs, k), rows_of(c.rows_in, s + k)).then_inc(x_in[k % 4], 16)

                def store(s, k):
                    sp.wait_ge(y_ready, s + k + 1)
                    sp.dma_start(rows_of(rows_out, s + k), columns(y, k)).then_inc(stored[k % 4], 16)

                def slot(s, k):
                    if alive(s, k, 2):
                        load(s, k + 2)
                    if alive(s, k, -2):
                        store(s, k - 2)

                sp.wait_ge(c.scattered, 16 * (m.before + NT * K))
                for k in range(2):
                    load(0, k)
                in_slots(nc, sp, T, slot)

            @block.gpsimd
            def _(pool):
                pool.wait_ge(pos_done, 1)
                pool.wait_ge(c.rows_zero, 16 * 8)
                for t in range(NT):
                    for j in range(K):
                        pool.indirect_dma_start(out=c.rows_in[:, :], out_offset=bass.IndirectOffsetOnAxis(ap=pos[:, K * t + j:K * t + j + 1], axis=0),
                                                in_=c.xn[:, t, :], in_offset=None).then_inc(c.scattered, 16)
                for k in range(4):
                    pool.wait_ge(stored[k], 16 * T // 4)
                for n in range(NT * K):
                    need(pool, back_used, n - 7)
                    pool.indirect_dma_start(out=back[:, n % 8, :], out_offset=None, in_=rows_out[:, :],
                                            in_offset=bass.IndirectOffsetOnAxis(ap=pos[:, n:n + 1], axis=0)).then_inc(c.back_in[n % 8], 16)

            @block.tensor
            def _(pe):
                pe.wait_ge(loaded, 16)
                for t in range(NT):
                    out = c.bank[t * E // 512][:, E * t % 512:E * t % 512 + E]
                    last = nc.tensor.matmul(out, c.xnT[:, P * t:P * t + P], w_router[:, :], start=True, stop=True)
                last.then_inc(logits_done, 1)
                pe.wait_ge(const_bf, 2)
                pe.wait_ge(sums_done, 1)
                half = max(1, NT * E // 512)
                per = NT // half
                for b in range(half):
                    out = c.bank[2 + b][:, 0:per * E]
                    nc.tensor.matmul(out, tri[:, :], chosen[:, per * b:per * b + per, :].rearrange("p t e -> p (t e)"), start=True, stop=False)
                    nc.tensor.matmul(out, ones_bf[:, :], sums[:, 0, per * b:per * b + per, :].rearrange("p t e -> p (t e)"), start=False, stop=True)
                nc.tensor.matmul(c.bank[4][:, 0:E], ones_bf[:, :], sums[:, 0, NT, :], start=True, stop=True).then_inc(counted, 1)

                def expert(s, k, j):
                    n = m.per_step * s + (m.per_step * k + j)
                    at = pe.value_load(owner[0:1, ds(n, 1)] if not isinstance(n, int) else owner[0:1, n:n + 1])
                    return nc.s_assert_within(at, 0, m.last * m.cols, skip_runtime_bounds_check_because="entries are clipped to the last expert")

                def turn_x(s, k):
                    pe.wait_ge(x_in[k % 4], 4 * s + 16 * (k // 4 + 1))
                    need(pe, xT_ready, s + k)
                    for j in range(m.per_step):
                        last = nc.tensor.transpose(x_bank[:, P * j:P * j + P], xs[:, k % 4, P * j:P * j + P], c.ident[:, :])
                    last.then_inc(turned_x, 1)

                def up(s, k):
                    e_s = [expert(s, k, j) for j in range(m.per_step)]
                    pe.wait_ge(xT_ready, s + (k + 1))
                    need(pe, h_done, s + (k - 1))
                    if m.gated:
                        e = e_s[0]
                        nc.tensor.matmul(c.bank[k % 2][:, :], xT[:, k % 2, :], weights[:, ds(e, HID)], start=True, stop=True).then_inc(silu_go, 1)
                        nc.tensor.matmul(c.bank[2 + k % 2][:, :], xT[:, k % 2, :], weights[:, ds(e + HID, HID)],
                                         start=True, stop=True).then_inc(up_done, 1)
                        return
                    for j, e in enumerate(e_s):
                        last = nc.tensor.matmul(c.bank[k % 2][:, P * j:P * j + P], xT[:, k % 2, P * j:P * j + P], weights[:, ds(e, P)],
                                                start=True, stop=True)
                    last.then_inc(up_done, 1)

                def turn_h(s, k):
                    pe.wait_ge(h_done, s + (k + 1))
                    need(pe, hT_ready, s + k)
                    for j in range(4):
                        last = nc.tensor.transpose(h_bank[:, P * j:P * j + P], h[:, k % 2, P * j:P * j + P], c.ident[:, :])
                    last.then_inc(turned_h, 1)

                def down(s, k):
                    e_s = [expert(s, k, j) for j in range(m.per_step)]
                    pe.wait_ge(hT_ready, s + (k + 1))
                    need(pe, y_ready, s + (k - 1))
                    e = e_s[0]
                    for j in range(4):
                        lhsT = hT[:, k % 2, P * j:P * j + P]
                        if m.gated:
                            last = nc.tensor.matmul(y_bank[k % 2][:, 0:P], lhsT, weights[:, ds(e + (2 * HID + P * j), P)],
                                                    start=(j == 0), stop=(j == 3))
                        else:
                            e = e_s[j]
                            last = nc.tensor.matmul(y_bank[k % 2][:, P * j:P * j + P], lhsT, weights[:, ds(e + P, P)], start=True, stop=True)
                    last.then_inc(down_done, 1)

                def slot(s, k):
                    if alive(s, k, 1):
                        turn_x(s, k + 1)
                    if alive(s, k):
                        up(s, k)
                    if alive(s, k, -1):
                        turn_h(s, k - 1)
                    if alive(s, k, -2):
                        down(s, k - 2)

                pe.wait_ge(owner_in, 16)
                pe.wait_ge(pos_done, 1)
                pe.wait_ge(weights_in, 16 * 8)
                turn_x(0, 0)
                in_slots(nc, pe, T, slot)

            @block.scalar
            def _(act):
                act.wait_ge(logits_done, 1)
                if layer == 1:
                    act.wait_ge(step_done, 3)
                    nc.scalar.activation(key[:, :, :], key[:, :, :], ACT.Exp).then_inc(key_done, 1)
                if layer == 2:
                    act.wait_ge(gate_go, 1)
                    nc.scalar.activation(gate[:, :, 1], small[:, 0, :], ACT.Exp).then_inc(key_done, 1)
                if layer == 3:
                    for b in range(2):
                        nc.scalar.activation(key[:, 8 * b:8 * b + 8, :], c.bank[b][:, :].rearrange("p (t e) -> p t e", t=8), ACT.Sigmoid).then_inc(key_done, 1)

                def activate(s, k):
                    if m.gated:
                        act.wait_ge(silu_go, s + (k + 1))
                        need(act, h_done, s + (k - 1))
                        nc.scalar.activation(silu[:, k % 2, :], c.bank[k % 2][:, :], ACT.Silu).then_inc(silu_done, 1)
                    else:
                        act.wait_ge(up_done, s + (k + 1))
                        need(act, turned_h, s + (k - 1))
                        nc.scalar.activation(h[:, k % 2, :], c.bank[k % 2][:, :], ACT.Relu).then_inc(h_done, 1)

                def keep_h(s, k):
                    act.wait_ge(turned_h, s + (k + 1))
                    need(act, down_done, s + (k - 1))
                    nc.scalar.copy(hT[:, k % 2, :], h_bank[:, :]).then_inc(hT_ready, 1)

                def slot(s, k):
                    if alive(s, k):
                        activate(s, k)
                    if alive(s, k, -1):
                        keep_h(s, k - 1)

                in_slots(nc, act, T, slot)

            @block.vector
            def _(dve):
                v = nc.vector
                step = Count(dve, step_done)
                v.tensor_copy(tri[:, :], c.const[:, TRI_AT:TRI_AT + P]).then_inc(const_bf, 1)
                v.memset(ones_bf[:, :], 1.0).then_inc(const_bf, 1)
                step.link(v.memset(sums[:, :, 0:1, :], 0.0))
                dve.wait_ge(logits_done, 1)
                if layer == 1:
                    logits = c.bank[0][:, 0:NT * E].rearrange("p (t e) -> p t e", t=NT)
                    wide = [P, NT, E]
                    step.link(v.tensor_reduce(small[:, 0, :], logits, AX.X, ALU.max))
                    step.add(v.tensor_tensor(key[:, :, :], logits, small[:, 0, :].unsqueeze(2).to_broadcast(wide), ALU.subtract))
                    dve.wait_ge(key_done, 1)
                    step.link(v.tensor_reduce(small[:, 0, :], key[:, :, :], AX.X, ALU.add))
                    step.link(v.reciprocal(small[:, 1, :], small[:, 0, :]))
                    step.link(v.tensor_tensor(key[:, :, :], key[:, :, :], small[:, 1, :].unsqueeze(2).to_broadcast(wide), ALU.mult))
                elif layer == 2:
                    step.link(v.tensor_copy(key[:, :, :], c.bank[0][:, 0:NT * E].rearrange("p (t e) -> p t e", t=NT)))
                else:
                    dve.wait_ge(key_done, 2)
                for t in range(NT):
                    step.add(v.max(top[:, t, :], key[:, t, :]))
                step.wait()
                if layer == 2:
                    v.tensor_tensor(small[:, 0, :], top[:, :, 1], top[:, :, 0], ALU.subtract).then_inc(gate_go, 1)
                for t in range(NT):
                    step.add(v.max_index(at[:, t, :], top[:, t, :], key[:, t, :]))
                step.wait()
                step.link(v.tensor_copy(at_f[:, :, :], at[:, :, 0:K]))
                shape = [P, NT, K, E]
                step.add(v.tensor_tensor(hot[:, :, :, :], c.const[:, IOTA_AT:IOTA_AT + E].unsqueeze(1).unsqueeze(1).to_broadcast(shape),
                                         at_f[:, :, :].unsqueeze(3).to_broadcast(shape), ALU.is_equal))
                if layer == 1:
                    step.link(v.tensor_scalar(gate[:, :, 0], at_f[:, :, 0], float(m.last) + 0.5, 2.0, ALU.is_lt, ALU.mult))
                    step.link(v.tensor_tensor(gate[:, :, 0], gate[:, :, 0], top[:, :, 0], ALU.mult))
                elif layer == 2:
                    dve.wait_ge(key_done, 1)
                    step.link(v.tensor_scalar(small[:, 1, :], gate[:, :, 1], 1.0, None, ALU.add))
                    step.link(v.reciprocal(gate[:, :, 0], small[:, 1, :]))
                    step.link(v.tensor_tensor(gate[:, :, 1], gate[:, :, 1], gate[:, :, 0], ALU.mult))
                else:
                    step.link(v.tensor_copy(gate[:, :, :], top[:, :, 0:K]))
                with nc.allow_low_precision("counts up to 16 are exact"):
                    step.link(v.tensor_reduce(chosen[:, :, :], hot[:, :, :, :].rearrange("p t k e -> p t e k"), AX.X, ALU.add))
                    step.link(v.tensor_copy(sums[:, 0, 1:, :], chosen[:, :, :]))
                    for n, d in enumerate((1, 2, 4, 8)):
                        src, dst = sums[:, n % 2], sums[:, 1 - n % 2]
                        step.add(v.tensor_copy(dst[:, 1:1 + d, :], src[:, 1:1 + d, :]))
                        last = v.tensor_tensor(dst[:, 1 + d:, :], src[:, 1 + d:, :], src[:, 1:NT + 1 - d, :], ALU.add)
                        step.link(last)
                    dve.sem_inc(sums_done, 1)
                dve.wait_ge(counted, 1)
                step.link(v.tensor_scalar(tiles_i[:, :], c.bank[4][:, 0:E], float(P - 1), None, ALU.add))
                step.link(v.tensor_scalar(tiles_i[:, :], tiles_i[:, :], 7, None, ALU.logical_shift_right))
                step.link(v.tensor_copy(cum[:, 0, :], tiles_i[:, :]))
                now, d = 0, 1
                while d < E:
                    step.add(v.tensor_copy(cum[:, 1 - now, 0:d], cum[:, now, 0:d]))
                    step.link(v.tensor_tensor(cum[:, 1 - now, d:], cum[:, now, d:], cum[:, now, 0:E - d], ALU.add))
                    now, d = 1 - now, 2 * d
                step.add(v.tensor_scalar(cum[:, 1 - now, :], cum[:, now, :], c.const[:, PART_AT:PART_AT + 1], None, ALU.is_le))
                step.link(v.tensor_tensor(cum[:, 2, :], cum[:, now, :], tiles_i[:, :], ALU.subtract))
                step.link(v.tensor_reduce(owner_f[:, 0:1], cum[:, 1 - now, :], AX.X, ALU.add))
                v.tensor_scalar(owner_i[:, :], owner_f[:, 0:1], float(m.last), float(m.cols), ALU.min, ALU.mult).then_inc(owner_done, 1)
                step.link(v.tensor_scalar(cum[:, 2, :], cum[:, 2, :], float(P), None, ALU.mult))
                per = NT // max(1, NT * E // 512)
                for b in range(NT // per):
                    step.add(v.tensor_tensor(place[:, per * b:per * b + per, :], c.bank[2 + b][:, 0:per * E].rearrange("p (t e) -> p t e", t=per),
                                             cum[:, 2:3, :].to_broadcast([P, per, E]), ALU.add))
                step.wait()
                step.link(v.tensor_tensor(spread, hot[:, :, :, :], place[:, :, :].unsqueeze(2).to_broadcast(shape), ALU.mult))
                step.link(v.tensor_reduce(pos_f[:, :].rearrange("p (t k) -> p t k", t=NT), spread, AX.X, ALU.add))
                v.tensor_copy(pos[:, :], pos_f[:, :]).then_inc(pos_done, 1)

                def keep_x(s, k):
                    dve.wait_ge(turned_x, s + (k + 1))
                    need(dve, up_done, s + (k - 1))
                    v.tensor_copy(xT[:, k % 2, :], x_bank[:, 0:W]).then_inc(xT_ready, 1)

                def multiply(s, k):
                    dve.wait_ge(silu_done, s + (k + 1))
                    dve.wait_ge(up_done, s + (k + 1))
                    need(dve, turned_h, s + (k - 1))
                    v.tensor_tensor(h[:, k % 2, :], silu[:, k % 2, :], c.bank[2 + k % 2][:, :], ALU.mult).then_inc(h_done, 1)

                def keep_y(s, k):
                    dve.wait_ge(down_done, s + (k + 1))
                    need(dve, stored[k % 4], 4 * s + 16 * (k // 4))
                    v.tensor_copy(y[:, k % 4, :], y_bank[k % 2][:, 0:W]).then_inc(y_ready, 1)

                def slot(s, k):
                    if alive(s, k, 1):
                        keep_x(s, k + 1)
                    if m.gated and alive(s, k):
                        multiply(s, k)
                    if alive(s, k, -2):
                        keep_y(s, k - 2)

                keep_x(0, 0)
                in_slots(nc, dve, T, slot)
                for n in range(NT * K):
                    dve.wait_ge(c.back_in[n % 8], 16 * ((m.before + n) // 8 + 1))
                    xs_t = c.x[:, TPB + n // K, :]
                    if n % K:
                        dve.wait_ge(back_used, n)
                    v.scalar_tensor_tensor(out=xs_t, in0=back[:, n % 8, :], scalar=gate[:, n // K, n % K:n % K + 1], in1=xs_t,
                                           op0=ALU.mult, op1=ALU.add).then_inc(back_used, 1)


def layer1_ffn(c, arg):
    layer1_shared(c, arg)
    experts_phase(c, 1, arg)


def layer2_ffn(c, arg):
    experts_phase(c, 2, arg)


def layer3_ffn(c, arg):
    experts_phase(c, 3, arg)


def layer0_attention(c, arg):
    attention_phase(c, 0, arg)


def layer2_attention(c, arg):
    attention_phase(c, 2, arg)


ALL_PHASES = (layer0_attention, layer0_ffn, layer1_attention, layer1_ffn,
              layer2_attention, layer2_ffn, layer3_attention, layer3_ffn)


def end_phase(c, out):
    nc = c.nc
    stored = c.sem("x_stored")
    with nc.Block() as block:
        @block.sync
        def _(sp):
            sp.dma_start(out.rearrange("b (t p) d -> p (b t) d", p=P), c.x[:, TPB:, :]).then_inc(stored, 16)
            sp.wait_ge(stored, 16)


def build(nc, arg, out, phases=ALL_PHASES):
    with ExitStack() as ctx:
        c = Core(nc, ctx)
        start_phase(c, arg)
        for n, phase in enumerate(phases):
            norm_phase(c, f"n{n}")
            phase(c, arg)
        end_phase(c, out)


def hid_major(w):
    return w.reshape(-1, P, w.shape[-1]).transpose(1, 0, 2).reshape(P, -1)


def gated(gate, up, down):
    return np.concatenate([np.concatenate([gate[e], up[e], hid_major(down[e])], axis=1) for e in range(len(gate))], axis=1)


def laid_out(inputs):
    a = {k: np.asarray(v) for k, v in inputs.items()}
    perm = np.arange(P).reshape(J, 2, D).transpose(1, 2, 0).reshape(P)
    o = {"x": a["x"], "ctxT": a["ctx_1024"].transpose(2, 0, 1), "mask": a["mask_1x1xSxS2_ff0"][0, 0],
         "maskT": a["mask_1x1xSxS2_ff0"][0, 0].T,
         "a0_wq": a["L0_xattn_Wq"][:, perm], "a0_wk": a["L0_xattn_Wk"][:, perm], "a0_wv": a["L0_xattn_Wv"], "a0_wo": a["L0_xattn_Wo"]}
    wf = a["L2_xattn_Wf"].T
    o["a2_wq"], o["a2_wk"], o["a2_wv"], o["a2_wp"] = a["L2_xattn_Wq"].T[:, perm], wf[:, :P][:, perm], wf[:, P:], a["L2_xattn_Wp"].T
    o["a2_bias_qk"] = np.stack([a["L2_xattn_bq"][perm], a["L2_xattn_bf"][:P][perm]], axis=1)
    o["a2_bias_row"] = np.stack([a["L2_xattn_bf"][P:], a["L2_xattn_bp"]])[None]
    o["a2_lora_a"] = np.stack([a["L2_xattn_Aq"], a["L2_xattn_Af"], a["L2_xattn_Ap"]], axis=1)
    bf = a["L2_xattn_Bf"].T
    o["a2_lora_b"] = np.stack([a["L2_xattn_Bq"].T[:, perm], bf[:, :P][:, perm], bf[:, P:], a["L2_xattn_Bp"].T], axis=1)
    f0_up = np.concatenate([a["L0_ffn_up_w"].reshape(-1, P), a["L0_ffn_shared_up"]]).T
    f0_down = np.concatenate([a["L0_ffn_down_w"].transpose(0, 2, 1).reshape(-1, P), a["L0_ffn_shared_down"].T])
    o["f0_w"] = np.concatenate([f0_up, hid_major(f0_down), a["L0_ffn_gate_w"].T], axis=1)
    o["f0_bias"] = np.tile(a["L0_ffn_bias_e"], (P, 1))
    o["const"] = np.concatenate([np.tile(np.arange(64), (P, 1)), np.triu(np.ones((P, P)), 1), np.arange(P)[:, None],
                                 np.tile(np.tril(np.ones((4, 4)), -1).reshape(16), (P, 1))], axis=1).astype(np.float32)
    o["f1_w"] = gated(*(np.concatenate([a["L1_ffn_w_" + n], a["L1_ffn_ws_" + n][None]]) for n in ("gate", "up", "down")))
    o["f2_w"] = gated(a["L2_ffn_experts_w1"], a["L2_ffn_experts_w3"], a["L2_ffn_experts_w2"])
    o["f3_w"] = np.concatenate([a["L3_ffn_keys"], a["L3_ffn_values"]], axis=2).transpose(1, 0, 2).reshape(P, -1)
    o["e1_router"], o["e2_router"], o["e3_router"] = a["L1_ffn_w_router"], a["L2_ffn_gate"], a["L3_ffn_expert_sel"].T
    o["a1_w"] = np.stack([a["L1_xattn_W"][:, :P].T, a["L1_xattn_W"][:, P:].T])
    o["a1_bias"] = a["L1_xattn_b"][None]
    o["one_hot8"] = np.repeat(np.eye(B, dtype=np.float32)[:, :, None], P, axis=2)
    for n in ("q", "k", "v", "o"):
        o["a3_w" + n] = a["L3_xattn_W" + n]
    o["a3_bias_qk"] = np.stack([a["L3_xattn_bq"], a["L3_xattn_bk"]], axis=1)
    o["a3_bias_vo"] = np.tile(np.stack([a["L3_xattn_bv"], a["L3_xattn_bo"]]), (P, 1, 1))
    expert = np.arange(8 * P) // 64
    o["spread0"] = np.tile(expert[None, :] == np.arange(16)[:, None], (PARTS, 1)).astype(np.float32)
    return {k: np.ascontiguousarray(v) for k, v in o.items()}


def kernel(**inputs):
    import concourse.bacc as bacc
    from concourse.bass_utils import run_bass_kernel_spmd

    nc = bacc.Bacc("TRN2", target_bir_lowering=False, num_devices=1)
    arrays = laid_out(inputs)
    arg = {k: nc.dram_tensor("in_" + k, v.shape, mybir.dt.from_np(v.dtype), kind="ExternalInput").ap() for k, v in arrays.items()}
    out = nc.dram_tensor("out", (B, TOK, P), F32, kind="ExternalOutput").ap()
    build(nc, arg, out)
    result = run_bass_kernel_spmd(nc, [{"in_" + k: v for k, v in arrays.items()}], core_ids=[0])
    return result.results[0]["out"]
```

```python
from contextlib import ExitStack

import numpy as np
import concourse.bass as bass
from concourse import mybir

F32 = mybir.dt.float32
BF16 = mybir.dt.bfloat16
F16 = mybir.dt.float16
I32 = mybir.dt.int32
U32 = mybir.dt.uint32
ACT = mybir.ActivationFunctionType
ALU = mybir.AluOpType
AX = mybir.AxisListType
ds = bass.ds

P = 128
B = 8
TOK = 256
N = B * TOK
NT = N // P
TPB = TOK // P
CTX = 512
H = 16
D = P // H
J = H // 2
EBUFS = 4
PARTS = 3
SLOTS = 6
QROWS = SLOTS * D
AUG = QROWS + PARTS
PVC = PARTS * (D + 1)
EPS = 1e-5
E_GATED = 8
HID = 512
GATED_COLS = 2 * HID + 4 * P
E3 = 64
TABLE = 128 * P
ROUTED_SCALE = 2.5
L0_AT = E_GATED * GATED_COLS
ZERO_AT = L0_AT + 2 * 10 * P + 16
IOTA_AT, TRI_AT, PART_AT, BEFORE_AT, FIELD_AT, CONSTS = 0, 64, 192, 193, 209, 213


class Count:

    def __init__(self, eng, sem, base=0):
        self.eng, self.sem, self.base, self.n = eng, sem, base, 0

    def add(self, ins):
        ins.then_inc(self.sem, 1)
        self.n += 1

    def wait(self):
        self.eng.wait_ge(self.sem, self.base + self.n)

    def link(self, ins):
        self.add(ins)
        self.wait()


class Core:

    def __init__(self, nc, ctx):
        self.nc, self.ctx = nc, ctx
        self.used = []
        self.x = self.sb("x", [P, NT + TPB, P], F32)
        self.xn = self.sb("xn", [P, NT, P], F32)
        self.xnT = self.sb("xnT", [P, N], F32)
        self.wa = self.sb("wa", [P, 64 * 256], F32)
        self.wb = self.sb("wb", [P, 8 * 1536], F32)
        self.ident = self.sb("ident", [P, P], F32)
        self.ident_bf = self.sb("ident_bf", [P, P], BF16)
        self.ones = self.sb("ones", [P, P], F32)
        self.stats = self.sb("stats", [P, NT + TPB, 6], F32)
        self.mean_var = self.sb("mean_var", [P, NT, 2], F32)
        self.std = self.sb("std", [P, NT], F32)
        self.rstd = self.sb("rstd", [P, NT], F32)
        self.shift = self.sb("shift", [P, NT], F32)
        self.ctx_sum = self.sb("ctx_sum", [P, B], F32)
        self.const = self.sb("const", [P, CONSTS], F32)
        self.w0_in, self.w1_in, self.w2_in, self.w3_in = (self.sem(f"w{n}_in") for n in range(4))
        self.rows_zero = self.sem("rows_zero")
        self.norm = {n: self.sem("norm_" + n) for n in ("stats", "var", "std", "by_dve", "by_act", "turned", "kept")}
        self.scattered, self.back_in = self.sem("scattered"), [self.sem(f"back_in{k}") for k in range(8)]
        self.rows_in = nc.dram_tensor("rows_in", [TABLE, P], F32)
        self.bank = [ctx.enter_context(nc.psum_tensor(f"bank{i}", [P, 512], F32)) for i in range(8)]

    def take_stats(self, tile):
        at = slice(tile, tile + 1) if isinstance(tile, int) else ds(tile, 1)
        self.nc.vector.bn_stats(self.stats[:, at, :].rearrange("p o s -> p (o s)"), self.x[:, at, :].rearrange("p o d -> p (o d)"))

    def sb(self, name, shape, dt):
        return self.ctx.enter_context(self.nc.sbuf_tensor(name, shape, dt))

    def sem(self, name):
        return self.ctx.enter_context(self.nc.semaphore(name))


class Phase:

    def __init__(self, c, tag):
        self.c, self.tag, self.buffers, self.signals, self.sems = c, tag, ExitStack(), ExitStack(), []

    def __enter__(self):
        return self

    def sb(self, name, shape, dt):
        return self.buffers.enter_context(self.c.nc.sbuf_tensor(self.tag + name, shape, dt))

    def sem(self, name):
        s = self.signals.enter_context(self.c.nc.semaphore(self.tag + name))
        self.sems.append(s)
        return s

    def __exit__(self, *error):
        self.c.used.append(self)
        return self.buffers.__exit__(*error)


def zero_used(c, sp):
    numbers = sorted(s.num for phase in c.used for s in phase.sems)
    while numbers:
        first = last = numbers.pop(0)
        while numbers and numbers[0] == last + 1:
            last = numbers.pop(0)
        sp.sem_clear(range(first, last + 1))


def release_used(c):
    for phase in c.used:
        phase.signals.close()
    c.used = []


def need(eng, sem, n):
    if not isinstance(n, int) or n > 0:
        eng.wait_ge(sem, n)


def start_phase(c, arg):
    nc = c.nc
    loaded, const, moved = c.sem("x_loaded"), c.sem("const_ready"), c.sem("const_copied")
    with nc.Block() as block:
        @block.sync
        def _(sp):
            sp.dma_start(c.x[:, TPB:, :], arg["x"].rearrange("b (t p) d -> p (b t) d", p=P)).then_inc(loaded, 16)
            sp.dma_start(c.const[:, :], arg["const"]).then_inc(loaded, 16)
            sp.dma_start(c.wa[:, L0_AT:ZERO_AT], arg["f0_w"]).then_inc(c.w0_in, 16)
            sp.wait_ge(loaded, 32)

        @block.gpsimd
        def _(pool):
            nc.gpsimd.memset(c.ident[:, :], 0.0).then_inc(const, 1)
            pool.wait_ge(const, 1)
            nc.gpsimd.affine_select(out=c.ident[:, :], in_=c.ident[:, :], compare_op=ALU.not_equal, fill=1.0,
                                    base=0, pattern=[[-1, P]], channel_multiplier=1).then_inc(const, 1)

        @block.vector
        def _(dve):
            nc.vector.memset(c.ones[:, :], 1.0)
            nc.vector.memset(c.x[:, 0:TPB, :], 0.0)
            nc.vector.memset(c.wa[:, ZERO_AT:ZERO_AT + 1024], 0.0)
            dve.wait_ge(const, 2)
            nc.vector.tensor_copy(c.ident_bf[:, :], c.ident[:, :]).then_inc(moved, 1)
            dve.wait_ge(loaded, 32)
            for t in range(NT):
                c.take_stats(TPB + t)


def norm_phase(c, n):
    nc = c.nc
    stat, var, std, turned, kept = c.norm["stats"], c.norm["var"], c.norm["std"], c.norm["turned"], c.norm["kept"]
    QUADS = NT // 4
    by = {0: ("by_dve", 3), 1: ("by_dve", 3), 2: ("by_dve", 3), 3: ("by_act", 1)}

    def tiles_of(name):
        return [t for t in range(NT) if by[t % 4][0] == name]

    with nc.Block() as block:
        @block.sync
        def _(sp):
            zero_used(c, sp)

        @block.vector
        def _(dve):
            for t in range(NT):
                nc.vector.bn_aggr(c.mean_var[:, t, :], c.stats[:, TPB + t, :]).then_inc(stat, 1)
            dve.wait_ge(stat, NT * (n + 1))
            nc.vector.tensor_scalar(c.rstd[:, :], c.mean_var[:, :, 1], EPS, None, ALU.add).then_inc(var, 1)
            dve.wait_ge(std, n + 1)
            nc.vector.reciprocal(c.rstd[:, :], c.std[:, :]).then_inc(var, 1)
            dve.wait_ge(var, 3 * n + 2)
            nc.vector.scalar_tensor_tensor(out=c.shift[:, :], in0=c.mean_var[:, :, 0], scalar=-1.0, in1=c.rstd[:, :],
                                           op0=ALU.mult, op1=ALU.mult).then_inc(var, 1)
            for t in tiles_of("by_dve"):
                nc.vector.tensor_scalar(c.xn[:, t, :], c.x[:, TPB + t, :], c.mean_var[:, t, 0:1],
                                        c.rstd[:, t:t + 1], ALU.subtract, ALU.mult).then_inc(c.norm["by_dve"], 1)

        @block.scalar
        def _(act):
            act.wait_ge(var, 3 * n + 1)
            nc.scalar.activation(c.std[:, :], c.rstd[:, :], ACT.Sqrt).then_inc(std, 1)
            act.wait_ge(var, 3 * n + 3)
            for t in tiles_of("by_act"):
                nc.scalar.activation(c.xn[:, t, :], c.x[:, TPB + t, :], ACT.Identity, bias=c.shift[:, t:t + 1],
                                     scale=c.rstd[:, t:t + 1]).then_inc(c.norm["by_act"], 1)
            for q in range(QUADS):
                act.wait_ge(turned, QUADS * n + q + 1)
                nc.scalar.copy(c.xnT[:, 512 * q:512 * q + 512], c.bank[q][:, :]).then_inc(kept, 1)

        @block.tensor
        def _(pe):
            for t in range(NT):
                name, share = by[t % 4]
                pe.wait_ge(c.norm[name], share * (QUADS * n + t // 4) + (t % 4 if share == 3 else 0) + 1)
                last = nc.tensor.transpose(c.bank[t // 4][:, P * (t % 4):P * (t % 4) + P], c.xn[:, t, :], c.ident[:, :])
                if t % 4 == 3:
                    last.then_inc(turned, 1)

    release_used(c)


def background(c, layer, arg, sp, i):
    if layer == 0:
        cols, rows = L0_AT // 8, TABLE // 8
        sp.dma_start(c.wa[:, ds(cols * i, cols)], arg["f1_w"][:, ds(cols * i, cols)]).then_inc(c.w1_in, 16)
        zeros = c.wa[:, ZERO_AT:ZERO_AT + 1024].unsqueeze(1).to_broadcast([P, rows // 1024, 1024])
        sp.dma_start(c.rows_in[ds(rows * i, rows), :].rearrange("(p n r) d -> p n (r d)", p=P, r=8), zeros).then_inc(c.rows_zero, 16)
    else:
        cols = 2 * P * E3 // 8
        sp.dma_start(c.wa[:, ds(cols * i, cols)], arg["f3_w"][:, ds(cols * i, cols)]).then_inc(c.w3_in, 16)


def attention_phase(c, layer, arg):
    nc = c.nc
    causal = layer == 2
    keys = 2 * P if causal else CTX
    kt_n = keys // P
    NA = NB = 1 if causal else 2
    SPAN = 384 if causal else 1024
    SHARE = SPAN // 4
    scale = float(D) ** -0.5
    tag = f"a{layer}_"
    with Phase(c, tag) as ph:
        sb, sem = ph.sb, ph.sem
        w = sb("w", [P, 4, P], F32)
        ctxT = sb("ctxT", [P, 2, CTX], F32)
        k_full = sb("k_full", [P, keys], F32)
        q_full = sb("q_full", [P, TOK], F32)
        v_full = sb("v_full", [P, kt_n, P], F32)
        k_part = sb("k_part", [P, PARTS, keys], BF16)
        q_part = sb("q_part", [P, PARTS, TOK], BF16)
        KS = sb("KS", [P, 2, J, keys], BF16)
        QS = sb("QS", [P, 2, J, TOK], BF16)
        V = sb("V", [P, 2, kt_n, H, PVC], BF16)
        neg_max = sb("neg_max", [P, 2, TPB, H // 2], F32)
        m_part = sb("m_part", [P, 2, TPB, 2, PARTS, 4], BF16)
        m_rest = sb("m_rest", [P, 2, TPB, 8], F32)
        m_rows = sb("m_rows", [2 * PARTS * 4, 2, TOK], BF16)
        E2 = sb("E2", [P, EBUFS, SPAN], F16)
        heads = sb("heads", [P, TPB, H, D + 1], F32)
        rsum = sb("rsum", [P, TPB, H], F32)
        attn = sb("attn", [P, TPB, P], F32)
        attnT = sb("attnT", [P, TOK], F32)
        k_dram = nc.dram_tensor(tag + "k_dram", [2, SLOTS, P, keys], BF16)
        q_dram = nc.dram_tensor(tag + "q_dram", [2, SLOTS, P, TOK], BF16)
        a_bank, b_bank, o_bank, misc, m_bank = c.bank[0:2], c.bank[2:4], c.bank[4:6], c.bank[6], c.bank[7]
        bfview = c.wb[:, :].bitcast(BF16)
        if causal:
            E = sb("E", [P, EBUFS, SPAN], F32)
            E1 = sb("E1", [P, EBUFS, SPAN], F16)
            bias_qk = sb("bias_qk", [P, 2], F32)
            bias_q = sb("bias_q", [P, 1], F32)
            bias_row = sb("bias_row", [1, 2, P], F32)
            lora_a = sb("lora_a", [16, 3, P], F32)
            lora_b = sb("lora_b", [16, 4, P], F32)
            tri = sb("tri", [P, 2, P], BF16)
            tri_f = sb("tri_f", [P, 2, P], F32)
        else:
            mask_q = bfview[:, 0:3072].rearrange("p (m t k) -> p m t k", m=PARTS, t=TPB)
            mask_k = bfview[:, 3072:6144].rearrange("p (m t k) -> p m t k", m=PARTS, t=kt_n)
            mask_f = c.wb[:, 6144:8192].rearrange("p (m k) -> p m k", m=2)
            E1 = c.wb[:, 3072:3072 + EBUFS * SPAN // 2].bitcast(F16).rearrange("p (b n) -> p b n", b=EBUFS)
            E = c.wb[:, 8192:8192 + EBUFS * SPAN].rearrange("p (b n) -> p b n", b=EBUFS)
            any_mask = sb("any_mask", [P, 4], F32)
            any_mask_i = sb("any_mask_i", [P, 1], I32)

        LOADS = 16 * (5 if causal else 1)
        SETUP = 6 if causal else 7
        ANY_MASK = 6
        bias_scaled = sem("bias_scaled")
        loaded, mask_in = sem("loaded"), sem("mask_in")
        ctx_in = [sem(f"ctx_in{p}") for p in range(2)]
        setup, setup_pool = sem("setup"), sem("setup_pool")
        rows_of_ones = sem("rows_of_ones")
        mask_step, mask_ready = sem("mask_step"), sem("mask_ready")
        lora_done = sem("lora_done")
        proj_k, proj_q, proj_v = sem("proj_k"), sem("proj_q"), sem("proj_v")
        full_k, full_q, full_v = sem("full_k"), sem("full_q"), sem("full_v")
        parts_k, parts_q, parts_v = sem("parts_k"), sem("parts_q"), sem("parts_v")
        pool_step = sem("pool_step")
        out_k, out_q = sem("out_k"), sem("out_q")
        stack = [[sem(f"stack{p}{g}") for g in range(2)] for p in range(2)]
        logits_a, max_done = sem("logits_a"), sem("max_done")
        parts_m, turned_m, rows_m = sem("parts_m"), sem("turned_m"), sem("rows_m")
        aug = [[sem(f"aug{p}{g}") for g in range(2)] for p in range(2)]
        logits_b, exp_done = sem("logits_b"), sem("exp_done")
        e1_done, e2_done, pv_done = sem("e1_done"), sem("e2_done"), sem("pv_done")
        e2_share = sem("e2_share")
        norm_step, o_free, norm_done = sem("norm_step"), sem("o_free"), sem("norm_done")
        turned_o, kept_o, out_o, x_done = sem("turned_o"), sem("kept_o"), sem("out_o"), sem("x_done")
        summed = sem("summed")

        START = {max_done: 3, parts_m: 2, turned_m: 2, rows_m: 2, exp_done: 2, e1_done: 2, e2_done: 4, e2_share: 4, pv_done: 17,
                 o_free: 2, norm_done: 1, parts_k: 1, parts_q: 1, parts_v: 1, turned_o: 1, out_o: 1, out_k: 16, out_q: 16,
                 aug[0][0]: 16, aug[0][1]: 16, aug[1][0]: 16, aug[1][1]: 16}

        def reach(eng, s, n):
            eng.wait_ge(s, START.get(s, 0) + n)

        def head(h):
            return h // 2, h % 2, 64 * (h % 2)

        def logits_slot(bb, p, h):
            if h < LAG:
                return bb, p, H - LAG + h
            return bb + p, 1 - p, h - LAG

        LAG = 3
        STEP_LINKS = 3 * 2 + 2 * 3
        FIRST_LINKS = 2 * 5 + 3

        def v_parts(p):
            return [V[:, p, :, :, (D + 1) * m:(D + 1) * m + D] for m in range(PARTS)]

        with nc.Block() as block:
            @block.sync
            def _(sp):
                def load_ctx(bb, p):
                    sp.dma_start(ctxT[:, p, :], arg["ctxT"][:, ds(2 * bb + p, 1), :].rearrange("d o k -> d (o k)")).then_inc(ctx_in[p], 16)

                def parts_out(bb, p, stacked=None):
                    b = 2 * bb + p
                    reach(sp, parts_k, b + 1)
                    if stacked is not None:
                        for g in range(2):
                            sp.wait_ge(stack[p][g], stacked)
                    for first, n, part in ((0, 3, 0), (3, 2, 1), (5, 1, 2)):
                        sp.dma_start(k_dram[p, first:first + n].rearrange("s r k -> r s k"),
                                     k_part[:, part:part + 1, :].to_broadcast([P, n, keys])).then_inc(out_k, 16)
                    reach(sp, parts_q, b + 1)
                    for first, n in ((0, 3), (3, 2), (5, 1)):
                        sp.dma_start(q_dram[p, first:first + n].rearrange("s r k -> r s k"),
                                     q_part[:, 0:n, :]).then_inc(out_q, 16)

                def stack_in(bb, p, g):
                    b = 2 * bb + p
                    reach(sp, out_k, 48 * (b + 1))
                    reach(sp, out_q, 48 * (b + 1))
                    for par in range(2):
                        rows = slice(64 * par, 64 * par + 64)
                        dst = slice(64 * par, 64 * par + QROWS)
                        for stack_of, dram in ((KS, k_dram), (QS, q_dram)):
                            slots = dram[p, :, rows, :].rearrange("s (d j) k -> s d j k", d=D)[:, :, 4 * g:4 * g + 4, :]
                            sp.dma_start(stack_of[dst, p, 4 * g:4 * g + 4, :], slots).then_inc(stack[p][g], 16)

                def aug_in(bb, p, g):
                    reach(sp, rows_m, 2 * (2 * bb + p) + g + 1)
                    for par in range(2):
                        sp.dma_start(QS[64 * par + QROWS:64 * par + AUG, p, 4 * g:4 * g + 4, :],
                                     m_rows[12 * par:12 * par + 12, g, :]).then_inc(aug[p][g], 16)

                if causal:
                    sp.dma_start(w[:, :, :], arg["a2_w"]).then_inc(loaded, 16)
                    sp.dma_start(bias_qk[:, :], arg["a2_bias_qk"]).then_inc(loaded, 16)
                    sp.dma_start(bias_row[:, :, :], arg["a2_bias_row"]).then_inc(loaded, 16)
                    sp.dma_start(lora_a[:, :, :], arg["a2_lora_a"]).then_inc(loaded, 16)
                    sp.dma_start(lora_b[:, :, :], arg["a2_lora_b"]).then_inc(loaded, 16)
                else:
                    sp.dma_start(w[:, :, :], arg["a0_w"]).then_inc(loaded, 16)
                load_ctx(0, 0)
                load_ctx(0, 1)
                if not causal:
                    sp.dma_start(mask_f[:, 0, :].rearrange("q (t k) -> q t k", t=TPB), arg["mask"].rearrange("(t q) k -> q t k", t=TPB)).then_inc(mask_in, 16)
                    sp.dma_start(mask_f[:, 1, :].rearrange("k (t q) -> k t q", t=kt_n), arg["maskT"].rearrange("(t k) q -> k t q", t=kt_n)).then_inc(mask_in, 16)
                for p in range(2):
                    parts_out(0, p)
                    if p == 0:
                        sp.wait_ge(rows_of_ones, 1)
                    stack_in(0, p, 0)
                    stack_in(0, p, 1)
                aug_in(0, 0, 0)

                def step(bb, p, more=True, last=False):
                    i = 2 * bb + p
                    if more:
                        reach(sp, proj_v, i + 1)
                        if not causal:
                            reach(sp, summed, i + 1)
                        load_ctx(bb + 1, p)
                    aug_in(bb, p, 1)
                    if not last:
                        aug_in(bb + p, 1 - p, 0)
                    if more:
                        parts_out(bb + 1, p, stacked=64 * bb + 64)
                        reach(sp, logits_b, NB * (H * i + H // 2))
                        stack_in(bb + 1, p, 0)
                    if more:
                        reach(sp, logits_b, NB * H * (i + 1))
                        stack_in(bb + 1, p, 1)
                    background(c, layer, arg, sp, i)

                step(0, 0)
                step(0, 1)
                with sp.Fori(1, 3) as bb:
                    for p in range(2):
                        step(bb, p)
                step(3, 0, more=False)
                step(3, 1, more=False, last=True)

            @block.gpsimd
            def _(pool):
                def one(like):
                    ap = c.ones[:, 0:1]
                    for _ in range(len(like.shape) - 2):
                        ap = ap.unsqueeze(2)
                    return ap.to_broadcast(list(like.shape))

                def split(chain, full, parts, done, ready):
                    def rest():
                        ready()
                        chain.add(nc.gpsimd.tensor_tensor(full, full, parts[0], ALU.subtract))

                    def second():
                        chain.wait()
                        chain.add(nc.gpsimd.tensor_tensor(parts[1], full, one(full), ALU.mult))

                    def third():
                        chain.wait()
                        nc.gpsimd.tensor_tensor(parts[2], full, parts[1], ALU.subtract).then_inc(done, 1)

                    return rest, second, third

                def split_k(chain, b):
                    return split(chain, k_full[:, :], [k_part[:, m, :] for m in range(PARTS)], parts_k,
                                 lambda: reach(pool, full_k, b + 1))

                def split_q(chain, b):
                    return split(chain, q_full[:, :], [q_part[:, m, :] for m in range(PARTS)], parts_q,
                                 lambda: reach(pool, full_q, b + 1))

                def split_v(chain, b, p):
                    full = v_full[:, :, :].rearrange("k t (h d) -> k t h d", h=H)
                    return split(chain, full, v_parts(p), parts_v, lambda: reach(pool, full_v, b + 1))

                def split_max(chain, b, g):
                    reach(pool, max_done, 2 * (H * b + 8 * g + 8))
                    reach(pool, turned_m, 2 * (b - 1) + g + 1)
                    parts = [m_part[:, g, :, :, m, :] for m in range(PARTS)]
                    neg = neg_max[:, g, :, :].rearrange("q t (r j) -> q t r j", r=2)
                    rest = m_rest[:, g, :, :].rearrange("q t (r j) -> q t r j", r=2)
                    chain.link(nc.gpsimd.tensor_tensor(parts[0], neg, one(neg), ALU.mult))
                    chain.link(nc.gpsimd.tensor_tensor(rest, neg, parts[0], ALU.subtract))
                    chain.link(nc.gpsimd.tensor_tensor(parts[1], rest, one(rest), ALU.mult))
                    nc.gpsimd.tensor_tensor(parts[2], rest, parts[1], ALU.subtract).then_inc(parts_m, 1)

                def residual(b, h):
                    n = H * b + h
                    reach(pool, e1_done, n + 1)
                    reach(pool, pv_done, n - 3)
                    e = h % EBUFS
                    nc.gpsimd.tensor_tensor(E2[:, e, SHARE:], E[:, e, SHARE:], E1[:, e, SHARE:], ALU.subtract).then_inc(e2_done, 1)

                if causal:
                    nc.gpsimd.memset(tri_f[:, :, :], 0.0).then_inc(setup_pool, 1)
                    pool.wait_ge(setup_pool, 1)
                    nc.gpsimd.affine_select(out=tri_f[:, 0, :], in_=tri_f[:, 0, :], compare_op=ALU.is_ge, fill=-1e30,
                                            base=0, pattern=[[-1, P]], channel_multiplier=1).then_inc(setup_pool, 1)
                    nc.gpsimd.affine_select(out=tri_f[:, 1, :], in_=tri_f[:, 1, :], compare_op=ALU.is_ge, fill=-1e30,
                                            base=0, pattern=[[1, P]], channel_multiplier=-1).then_inc(setup_pool, 1)
                chain = Count(pool, pool_step)
                for b in range(2):
                    for op in split_k(chain, b) + split_q(chain, b):
                        op()
                    if b == 0 and not causal:
                        pool.wait_ge(setup, ANY_MASK)
                        nc.gpsimd.partition_all_reduce(any_mask[:, 2:3], any_mask[:, 1:2], P, bass.bass_isa.ReduceOp.max).then_inc(setup_pool, 1)
                for op in split_v(chain, 0, 0):
                    op()
                split_max(chain, 0, 0)
                residual(0, 0)
                assert chain.n == FIRST_LINKS

                def step(bb, p, more=True, last=False):
                    i = 2 * bb + p
                    chain = Count(pool, pool_step, FIRST_LINKS + STEP_LINKS * i)
                    if not more and p:
                        chain.base -= 4
                    splits = []
                    if more:
                        splits += zip((8, 9, 10, 11, 11, 12) if causal else (8, 9, 10, 11, 12, 13), split_k(chain, i + 2) + split_q(chain, i + 2))
                    if not last:
                        splits += zip((12, 13, 14) if causal else (14, 15, 16), split_v(chain, i + 1, 1 - p))
                    for h in range(1, H + 1):
                        if h < H:
                            residual(i, h)
                        elif not last:
                            residual(i + 1, 0)
                        if h == LAG - 1:
                            split_max(chain, i, 1)
                        for slot, op in splits:
                            if slot == h:
                                op()
                        if h == LAG + 7 and not last:
                            split_max(chain, i + 1, 0)
                    assert chain.n == (STEP_LINKS if more else 3 if last else 8)

                step(0, 0)
                step(0, 1)
                with pool.Fori(1, 3) as bb:
                    for p in range(2):
                        step(bb, p)
                step(3, 0, more=False)
                step(3, 1, more=False, last=True)

            @block.vector
            def _(dve):
                for s, n in START.items():
                    dve.sem_inc(s, n)
                for m in range(PARTS):
                    at = (D + 1) * m + D
                    nc.vector.memset(V[:, :, :, :, at:at + 1], 1.0 if m == 0 else 0.0).then_inc(setup, 1)
                nc.vector.memset(attn[:, :, :], 0.0).then_inc(setup, 1)
                nc.vector.memset(KS[:, :, :, :], 1.0).then_inc(rows_of_ones, 1)
                if causal:
                    dve.wait_ge(loaded, LOADS)
                    dve.wait_ge(setup_pool, 3)
                    nc.vector.tensor_copy(tri[:, :, :], tri_f[:, :, :]).then_inc(setup, 1)
                    dve.wait_ge(lora_done, 1)
                    nc.vector.scalar_tensor_tensor(out=w[:, :, :], in0=misc[:, :].rearrange("p (n k) -> p n k", n=4), scalar=1.0 / 16.0,
                                                   in1=w[:, :, :], op0=ALU.mult, op1=ALU.add).then_inc(setup, 1)
                else:
                    dve.wait_ge(mask_in, 32)
                    nc.vector.tensor_scalar(E[:, 0:2, :], mask_f[:, :, :], 0.0, None, ALU.not_equal).then_inc(setup, 1)
                    dve.wait_ge(setup, 5)
                    nc.vector.tensor_reduce(any_mask[:, 1:2], E[:, 0:2, :], AX.XY, ALU.max).then_inc(setup, 1)
                    assert ANY_MASK == 6
                    dve.wait_ge(setup_pool, 1)
                    nc.vector.tensor_copy(any_mask_i[:, :], any_mask[:, 2:3]).then_inc(setup, 1)
                    dve.wait_ge(setup, SETUP)
                    any_here = dve.value_load(any_mask_i[0:1, 0:1], min_val=0, max_val=1)
                    with dve.If(any_here > 0):
                        chain = Count(dve, mask_step)
                        parts = [bfview[:, 0:6144].rearrange("p (l m k) -> p l m k", l=2, m=PARTS)[:, :, m, :] for m in range(PARTS)]
                        full = mask_f[:, :, :]
                        chain.link(nc.vector.tensor_copy(parts[0], full))
                        chain.link(nc.vector.tensor_tensor(full, full, parts[0], ALU.subtract))
                        chain.link(nc.vector.tensor_copy(parts[1], full))
                        nc.vector.tensor_tensor(parts[2], full, parts[1], ALU.subtract).then_inc(mask_ready, 1)

                def maximum(b, h):
                    n = H * b + h
                    j, par, _ = head(h)
                    g, col = j // 4, 4 * par + j % 4
                    if h % 8 == 0:
                        reach(dve, parts_m, 2 * (b - 1) + g + 1)
                    for t in range(TPB):
                        if causal:
                            reach(dve, logits_a, n + 1)
                            src = a_bank[h % 2][:, 0:P] if t == 0 else a_bank[h % 2][:, P:3 * P]
                        else:
                            reach(dve, logits_a, 2 * n + t + 1)
                            src = a_bank[t][:, :]
                        nc.vector.tensor_reduce(neg_max[:, g, t, col:col + 1], src, AX.X, ALU.max, negate=True).then_inc(max_done, 1)

                def first_part(b, h):
                    n = H * b + h
                    reach(dve, exp_done, NB * (n + 1))
                    reach(dve, pv_done, n - 3)
                    nc.vector.tensor_copy(E1[:, h % EBUFS, :], E[:, h % EBUFS, :]).then_inc(e1_done, 1)

                def residual(b, h):
                    n = H * b + h
                    reach(dve, e1_done, n + 1)
                    e = h % EBUFS
                    nc.vector.tensor_tensor(E2[:, e, 0:SHARE], E[:, e, 0:SHARE], E1[:, e, 0:SHARE], ALU.subtract).then_inc(e2_share, 1)

                def normalise(b):
                    reach(dve, pv_done, H * (b + 1))
                    for t in range(TPB):
                        nc.vector.tensor_reduce(heads[:, t, :, :], o_bank[t][:, 0:H * PVC].rearrange("q (h m c) -> q h c m", h=H, m=PARTS),
                                                AX.X, ALU.add).then_inc(o_free, 1)
                    reach(dve, o_free, 2 * (b + 1))
                    nc.vector.reciprocal(rsum[:, :, :], heads[:, :, :, D]).then_inc(norm_step, 1)
                    reach(dve, norm_step, b + 1)
                    reach(dve, turned_o, b + 1)
                    nc.vector.tensor_tensor(attn[:, :, :].rearrange("q t (h d) -> q t h d", h=H), heads[:, :, :, 0:D],
                                            rsum[:, :, :].unsqueeze(3).to_broadcast([P, TPB, H, D]), ALU.mult).then_inc(norm_done, 1)

                def add_to_x(b1):
                    reach(dve, out_o, b1 + 1)
                    xs = c.x[:, ds(TPB * b1, TPB), :]
                    nc.vector.tensor_tensor(xs, xs, misc[:, 0:TOK].rearrange("q (t d) -> q t d", t=TPB), ALU.add).then_inc(x_done, 1)
                    reach(dve, x_done, b1 + 1)
                    for t in range(TPB):
                        c.take_stats(TPB * b1 + t)

                def sum_ctx(bb, p):
                    dve.wait_ge(ctx_in[p], 16 * (bb + 1))
                    nc.vector.tensor_reduce(c.ctx_sum[:, ds(2 * bb + p, 1)], ctxT[:, p, :], AX.X, ALU.add).then_inc(summed, 1)

                if not causal:
                    sum_ctx(0, 0)
                    sum_ctx(0, 1)
                for h in range(H - LAG + 1):
                    maximum(0, h)
                first_part(0, 0)

                def step(bb, p, more=True, last=False, first=False):
                    i = 2 * bb + p
                    for h in range(1, H + 1):
                        if h == 2 and not first:
                            normalise(i - 1)
                        if h < H:
                            if h < LAG or not last:
                                _, _, ah = logits_slot(bb, p, h)
                                maximum(i if h < LAG else i + 1, ah)
                            residual(i, h - 1)
                            first_part(i, h)
                        else:
                            residual(i, h - 1)
                            if not last:
                                maximum(i + 1, H - LAG)
                                first_part(i + 1, 0)
                        if h == 5:
                            add_to_x(i)
                        if h == 8 and more and not causal:
                            sum_ctx(bb + 1, p)

                step(0, 0, first=True)
                step(0, 1)
                with dve.Fori(1, 3) as bb:
                    for p in range(2):
                        step(bb, p)
                step(3, 0, more=False)
                step(3, 1, more=False, last=True)
                normalise(B - 1)
                add_to_x(B)

            @block.scalar
            def _(act):
                def exps(b, h):
                    n = H * b + h
                    for u in range(NB):
                        reach(act, logits_b, NB * n + u + 1)
                        if u == 0:
                            reach(act, e2_done, n - 3)
                            reach(act, e2_share, n - 3)
                        if causal:
                            nc.scalar.activation(E[:, h % EBUFS, :], b_bank[h % 2][:, 0:SPAN], ACT.Exp).then_inc(exp_done, 1)
                        else:
                            nc.scalar.activation(E[:, h % EBUFS, 512 * u:512 * u + 512], b_bank[u][:, :], ACT.Exp).then_inc(exp_done, 1)

                def keep_k(b):
                    reach(act, proj_k, b + 1)
                    reach(act, parts_k, b)
                    reach(act, out_k, 48 * b)
                    bias = bias_qk[:, 1:2] if causal else 0.0
                    nc.scalar.activation(k_part[:, 0, :], misc[:, 0:keys], ACT.Identity, bias=bias)
                    nc.scalar.activation(k_full[:, :], misc[:, 0:keys], ACT.Identity, bias=bias).then_inc(full_k, 1)

                def keep_q(b):
                    reach(act, proj_q, b + 1)
                    reach(act, parts_q, b)
                    reach(act, out_q, 48 * b)
                    bias = bias_q[:, :] if causal else 0.0
                    nc.scalar.activation(q_part[:, 0, :], misc[:, 0:TOK], ACT.Identity, bias=bias, scale=scale)
                    nc.scalar.activation(q_full[:, :], misc[:, 0:TOK], ACT.Identity, bias=bias, scale=scale).then_inc(full_q, 1)

                def keep_v(b, p):
                    reach(act, proj_v, b + 1)
                    reach(act, parts_v, b)
                    reach(act, pv_done, H * (b - 1))
                    nc.scalar.activation(v_parts(p)[0], misc[:, 0:keys].rearrange("k (t h d) -> k t h d", t=kt_n, h=H), ACT.Identity)
                    nc.scalar.copy(v_full[:, :, :], misc[:, 0:keys].rearrange("k (t c) -> k t c", t=kt_n)).then_inc(full_v, 1)

                def keep_max(b, g, other, count):
                    reach(act, turned_m, 2 * b + g + 1)
                    reach(act, aug[other][g], 32 * count)
                    nc.scalar.copy(m_rows[:, g, :], m_bank[:, :].bitcast(BF16)[0:2 * PARTS * 4, TOK * g:TOK * g + TOK]).then_inc(rows_m, 1)

                def keep_o(b1):
                    reach(act, turned_o, b1 + 1)
                    reach(act, out_o, b1)
                    nc.scalar.copy(attnT[:, :], misc[:, 0:TOK]).then_inc(kept_o, 1)

                if causal:
                    act.wait_ge(loaded, LOADS)
                    nc.scalar.mul(bias_q[:, :], bias_qk[:, 0:1], scale).then_inc(bias_scaled, 1)
                    act.wait_ge(bias_scaled, 1)
                for b in range(2):
                    keep_k(b)
                    keep_q(b)
                act.wait_ge(setup, 4)
                keep_v(0, 0)
                keep_max(0, 0, 1, 0)
                exps(0, 0)

                def step(bb, p, more=True, last=False):
                    i = 2 * bb + p
                    for h in range(1, H + 1):
                        if h < H:
                            exps(i, h)
                        elif not last:
                            exps(i + 1, 0)
                        if h == 4:
                            keep_o(i)
                        if h == LAG + 1:
                            keep_max(i, 1, 1 - p, bb + p)
                        if h == 7 and more:
                            keep_k(i + 2)
                        if h == 8 and more:
                            keep_q(i + 2)
                        if h == 10 and not last:
                            keep_v(i + 1, 1 - p)
                        if h == LAG + 9 and not last:
                            keep_max(i + 1, 0, p, bb + 1)

                step(0, 0)
                step(0, 1)
                with act.Fori(1, 3) as bb:
                    for p in range(2):
                        step(bb, p)
                step(3, 0, more=False)
                step(3, 1, more=False, last=True)
                keep_o(B)

            @block.tensor
            def _(pe):
                def project_k(bb, p):
                    pe.wait_ge(ctx_in[p], 16 * (bb + 1))
                    nc.tensor.matmul(misc[:, 0:keys], w[:, 1, :], ctxT[:, p, 0:keys], start=True, stop=True).then_inc(proj_k, 1)

                def project_q(b):
                    nc.tensor.matmul(misc[:, 0:TOK], w[:, 0, :], c.xnT[:, ds(TOK * b, TOK)], start=True, stop=True).then_inc(proj_q, 1)

                def project_v(p):
                    for t in range(kt_n):
                        out = misc[:, P * t:P * t + P]
                        last = nc.tensor.matmul(out, ctxT[:, p, P * t:P * t + P], w[:, 2, :], start=True, stop=not causal)
                        if causal:
                            last = nc.tensor.matmul(out, c.ones[0:1, :], bias_row[0:1, 0, :], start=False, stop=True)
                    last.then_inc(proj_v, 1)

                def logits_qk(masked, b, p, h, t):
                    n = H * b + h
                    j, _, row = head(h)
                    rows = slice(row, row + QROWS)
                    if causal:
                        reach(pe, max_done, 2 * n - 2)
                        for t in range(TPB):
                            out = a_bank[h % 2][:, P * t:P * t + P * (t + 1)]
                            nc.tensor.matmul(out, QS[rows, p, j, P * t:P * t + P], KS[rows, p, j, 0:P * (t + 1)], start=True, stop=True)
                            last = nc.tensor.matmul(a_bank[h % 2][:, 2 * P * t:2 * P * t + P], c.ident_bf[:, :], tri[:, 0, :],
                                                    start=False, stop=True, skip_group_check=True)
                        last.then_inc(logits_a, 1)
                        return
                    reach(pe, max_done, 2 * n + t - 1)
                    last = nc.tensor.matmul(a_bank[t][:, :], QS[rows, p, j, P * t:P * t + P], KS[rows, p, j, :], start=True, stop=True)
                    for m in range(PARTS if masked else 0):
                        last = nc.tensor.matmul(a_bank[t][:, :], c.ident_bf[:, :], mask_q[:, m, t, :], start=False, stop=True,
                                                skip_group_check=True)
                    last.then_inc(logits_a, 1)

                def logits_kq(masked, b, p, h, u):
                    n = NB * (H * b + h) + u
                    j, _, row = head(h)
                    rows = slice(row, row + AUG)
                    reach(pe, exp_done, n - 1)
                    if causal:
                        out = b_bank[h % 2]
                        for t in range(TPB):
                            nc.tensor.matmul(out[:, 2 * P * t:2 * P + P * t], KS[rows, p, j, P * t:P * t + P], QS[rows, p, j, P * t:TOK],
                                             start=True, stop=True)
                            last = nc.tensor.matmul(out[:, 2 * P * t:2 * P * t + P], c.ident_bf[:, :], tri[:, 1, :], start=False, stop=True,
                                                    skip_group_check=True)
                        last.then_inc(logits_b, 1)
                        return
                    for t in (2 * u, 2 * u + 1):
                        out = b_bank[u][:, TOK * (t % 2):TOK * (t % 2) + TOK]
                        last = nc.tensor.matmul(out, KS[rows, p, j, P * t:P * t + P], QS[rows, p, j, :], start=True, stop=True)
                        for m in range(PARTS if masked else 0):
                            last = nc.tensor.matmul(out, c.ident_bf[:, :], mask_k[:, m, t, :], start=False, stop=True,
                                                    skip_group_check=True)
                    last.then_inc(logits_b, 1)

                def weigh_v(b, p, h):
                    n = H * b + h
                    reach(pe, e2_done, n + 1)
                    reach(pe, e2_share, n + 1)
                    if h == 0:
                        reach(pe, o_free, 2 * b)
                        reach(pe, parts_v, b + 1)
                    for t in range(TPB):
                        key_tiles = range(t + 1) if causal else range(kt_n)
                        for k in key_tiles:
                            at = P * (t + k) if causal else TOK * k + P * t
                            for e in (E1, E2):
                                last = nc.tensor.matmul(o_bank[t][:, PVC * h:PVC * h + PVC], e[:, h % EBUFS, at:at + P], V[:, p, k, h, :],
                                                        start=(k == 0 and e is E1), stop=(k == key_tiles[-1] and e is E2))
                    last.then_inc(pv_done, 1)

                def turn_max(b, g):
                    reach(pe, parts_m, 2 * b + g + 1)
                    reach(pe, rows_m, 2 * (b - 1) + g + 1)
                    out = m_bank[:, :].bitcast(BF16)
                    for t in range(TPB):
                        last = nc.tensor.transpose(out[0:2 * PARTS * 4, TOK * g + P * t:TOK * g + P * t + P],
                                                   m_part[:, g, t, :, :, :].rearrange("q r m j -> q (r m j)"), c.ident_bf[:, :])
                    last.then_inc(turned_m, 1)

                def turn_o(b1):
                    reach(pe, norm_done, b1)
                    for t in range(TPB):
                        last = nc.tensor.transpose(misc[:, P * t:P * t + P], attn[:, t, :], c.ident[:, :])
                    last.then_inc(turned_o, 1)

                def project_o(b1):
                    reach(pe, kept_o, b1 + 1)
                    for t in range(TPB):
                        out = misc[:, P * t:P * t + P]
                        last = nc.tensor.matmul(out, attnT[:, P * t:P * t + P], w[:, 3, :], start=True, stop=not causal)
                        if causal:
                            last = nc.tensor.matmul(out, c.ones[0:1, :], bias_row[0:1, 1, :], start=False, stop=True)
                    last.then_inc(out_o, 1)

                def heads_together(masked, b, p, h, ab, ap, ah):
                    for u in range(2):
                        if u < NB and b is not None:
                            logits_kq(masked, b, p, h, u)
                        if u < NA and ab is not None:
                            logits_qk(masked, ab, ap, ah, u)

                def program(masked):
                    if masked:
                        pe.wait_ge(mask_ready, 1)
                    pe.wait_ge(stack[0][0], 64)
                    for h in range(H - LAG):
                        if h == H // 2:
                            pe.wait_ge(stack[0][1], 64)
                        heads_together(masked, None, None, None, 0, 0, h)
                        if h == 8:
                            turn_max(0, 0)
                    reach(pe, aug[0][0], 32)
                    heads_together(masked, 0, 0, 0, 0, 0, H - LAG)

                    def step(bb, p, more=True, last=False, first=False):
                        i = 2 * bb + p
                        for h in range(1, H + 1):
                            if h in (LAG, LAG + 8) and not last:
                                pe.wait_ge(stack[1 - p][(h - LAG) // 8], 64 * (bb + p + 1))
                            if h == 8:
                                reach(pe, aug[p][1], 32 * (bb + 1))
                            if h < H:
                                with_a = h < LAG or not last
                                _, ap, ah = logits_slot(bb, p, h)
                                heads_together(masked, i, p, h, (i if h < LAG else i + 1) if with_a else None, ap, ah)
                            elif not last:
                                reach(pe, aug[1 - p][0], 32 * (bb + p + 1))
                                heads_together(masked, i + 1, 1 - p, 0, i + 1, 1 - p, H - LAG)
                            if h >= 2:
                                weigh_v(i, p, h - 2)
                            elif not first:
                                weigh_v(i - 1, 1 - p, H - 1)
                            if h == 4:
                                reach(pe, full_v, i + 1)
                                turn_o(i)
                            if h == 5:
                                project_o(i)
                            if h == LAG + 1:
                                turn_max(i, 1)
                            if h == 7 and more:
                                reach(pe, x_done, i + 1)
                                project_k(bb + 1, p)
                            if h == 8 and more:
                                reach(pe, full_k, i + 3)
                                project_q(i + 2)
                            if h == 10 and not last:
                                if more:
                                    reach(pe, full_q, i + 3)
                                else:
                                    reach(pe, x_done, i + 1)
                                project_v(1 - p)
                            if h == LAG + 9 and not last:
                                turn_max(i + 1, 0)

                    step(0, 0, first=True)
                    step(0, 1)
                    with pe.Fori(1, 3) as bb:
                        for p in range(2):
                            step(bb, p)
                    step(3, 0, more=False)
                    step(3, 1, more=False, last=True)
                    weigh_v(B - 1, 1, H - 1)
                    reach(pe, x_done, B)
                    turn_o(B)
                    project_o(B)

                pe.wait_ge(loaded, LOADS)
                if causal:
                    for n, (a, b) in enumerate(((0, 0), (1, 1), (1, 2), (2, 3))):
                        last = nc.tensor.matmul(misc[:, P * n:P * n + P], lora_a[:, a, :], lora_b[:, b, :], start=True, stop=True)
                    last.then_inc(lora_done, 1)
                if causal:
                    pe.wait_ge(setup, SETUP)
                for p in range(2):
                    project_k(0, p)
                    reach(pe, full_k, p + 1)
                    project_q(p)
                    reach(pe, full_q, p + 1)
                project_v(0)
                pe.wait_ge(setup, SETUP)
                if causal:
                    program(False)
                else:
                    masked = pe.value_load(any_mask_i[0:1, 0:1], min_val=0, max_val=1)
                    with pe.If(masked > 0):
                        program(True)
                    with pe.Else():
                        program(False)


CHUNK = 512
NC = N // CHUNK
TPC = CHUNK // P
E0 = 16
HID0 = 8 + 2


def dense_block(c, ph, up, gate, down, weighted, router, hidden, first=0, chunks=NC):
    nc = c.nc
    tiles = len(up)
    order = list(range(weighted, tiles)) + list(range(weighted))
    RB = 3 if gate else 12
    r = ph.sb("relu", [P, RB, CHUNK], F32)
    prod = ph.sb("prod", [P, 2, CHUNK], F32)
    hT = hidden[:, 0:2 * tiles * CHUNK].rearrange("p (b i t) -> p b i t", b=2, i=tiles)
    up_bank, side_bank, down_bank = c.bank[0:2], c.bank[2:4], c.bank[4:6]
    sides = tiles if gate else weighted
    up_done, side_done, act_done, prod_done, h_done = (ph.sem(n) for n in ("up_done", "side_done", "act_done", "prod_done", "h_done"))
    down_done, x_done = ph.sem("down_done"), ph.sem("x_done")
    if gate:
        h_done = prod_done
    DOWN_AT = 1 if gate else 4
    X_AT = 3 if gate else 7

    def side_number(q, k):
        if gate:
            return tiles * q + k
        return None if order[k] >= weighted else weighted * q + k - (tiles - weighted)

    with nc.Block() as block:
        @block.sync
        def _(sp):
            router.loads(sp)

        @block.tensor
        def _(pe):
            def up_product(q, k):
                n, i = tiles * q + k, order[k]
                need(pe, act_done if not gate else prod_done, n - 1)
                rhs = c.xnT[:, CHUNK * (first + q):CHUNK * (first + q + 1)]
                nc.tensor.matmul(up_bank[n % 2][:, :], up[i], rhs, start=True, stop=True).then_inc(up_done, 1)

            def side_product(q, k):
                i, m = order[k], side_number(q, k)
                if m is None:
                    return
                rhs = c.xnT[:, CHUNK * (first + q):CHUNK * (first + q + 1)]
                need(pe, act_done if gate else prod_done, m - 1)
                if gate:
                    nc.tensor.matmul(side_bank[m % 2][:, :], gate[i], rhs, start=True, stop=True).then_inc(side_done, 1)
                else:
                    lhsT, rows = router.scale_rows(i, q)
                    nc.tensor.matmul(side_bank[m % 2][:, :], lhsT, rows, start=True, stop=True).then_inc(side_done, 1)

            def down_product(q):
                pe.wait_ge(h_done, tiles * (q + 1))
                need(pe, x_done, q - 1)
                for t in range(TPC):
                    for i in range(tiles):
                        last = nc.tensor.matmul(down_bank[q % 2][:, P * t:P * t + P], hT[:, q % 2, i, P * t:P * t + P], down[i],
                                                start=(i == 0), stop=(i == tiles - 1))
                last.then_inc(down_done, 1)

            router.pe(pe)
            for q in range(chunks):
                if q == 0 and not gate:
                    for k in range(tiles):
                        up_product(q, k)
                    router.pe_weights(pe)
                for k in range(tiles):
                    if q or gate:
                        up_product(q, k)
                    side_product(q, k)
                    if k == DOWN_AT and q:
                        down_product(q - 1)
            down_product(chunks - 1)

        @block.scalar
        def _(act):
            router.act(act)
            for q in range(chunks):
                for k in range(tiles):
                    n = tiles * q + k
                    if gate:
                        act.wait_ge(side_done, n + 1)
                        need(act, h_done, n + 1 - RB)
                        nc.scalar.activation(r[:, n % RB, :], side_bank[n % 2][:, :], ACT.Silu).then_inc(act_done, 1)
                    else:
                        act.wait_ge(up_done, n + 1)
                        need(act, h_done, n + 1 - RB)
                        nc.scalar.activation(r[:, n % RB, :], up_bank[n % 2][:, :], ACT.Relu).then_inc(act_done, 1)
                if q == 0 and not gate:
                    router.act_weights(act)

        @block.vector
        def _(dve):
            def add_to_x(q):
                dve.wait_ge(down_done, q + 1)
                xs = c.x[:, TPB + TPC * (first + q):TPB + TPC * (first + q + 1), :]
                nc.vector.tensor_tensor(xs, xs, down_bank[q % 2][:, :].rearrange("p (t d) -> p t d", t=TPC), ALU.add).then_inc(x_done, 1)
                if not gate:
                    dve.wait_ge(x_done, q + 1)
                    for t in range(TPC):
                        c.take_stats(TPB + TPC * (first + q) + t)

            router.dve(dve)
            for q in range(chunks):
                for k in range(tiles):
                    n, m = tiles * q + k, side_number(q, k)
                    if k == X_AT and q:
                        add_to_x(q - 1)
                    if m is None:
                        continue
                    dve.wait_ge(act_done, n + 1)
                    if gate:
                        dve.wait_ge(up_done, n + 1)
                        need(dve, down_done, q - 1)
                        nc.vector.tensor_tensor(hT[:, q % 2, k, :], r[:, n % RB, :], up_bank[n % 2][:, :], ALU.mult).then_inc(prod_done, 1)
                    else:
                        dve.wait_ge(side_done, m + 1)
                        need(dve, h_done, n - 1)
                        nc.vector.tensor_tensor(prod[:, m % 2, :], r[:, n % RB, :], side_bank[m % 2][:, :], ALU.mult).then_inc(prod_done, 1)
            add_to_x(chunks - 1)
            dve.wait_ge(x_done, chunks)
            router.dve_last(dve)

        @block.gpsimd
        def _(pool):
            router.pool(pool)
            if not gate:
                for q in range(chunks):
                    for k in range(tiles):
                        n, m = tiles * q + k, side_number(q, k)
                        need(pool, down_done, q - 1)
                        if m is None:
                            pool.wait_ge(act_done, n + 1)
                            first = r[:, n % RB, :]
                        else:
                            pool.wait_ge(prod_done, m + 1)
                            first = prod[:, m % 2, :]
                        nc.gpsimd.tensor_tensor(hT[:, q % 2, order[k], :], first, r[:, n % RB, :], ALU.mult).then_inc(h_done, 1)


class Router0:

    def __init__(self, c, ph, arg):
        self.c, self.arg = c, arg
        self.w = c.wa[:, L0_AT + 2 * HID0 * P:L0_AT + 2 * HID0 * P + E0]
        sb = ph.sb
        self.bias = sb("bias", [P, E0], F32)
        self.spread_f = sb("spread_f", [PARTS * E0, 8 * P], F32)
        self.spread = sb("spread", [PARTS * E0, 8 * P], BF16)
        self.scores = sb("scores", [P, NT, E0], F32)
        self.sc = sb("sc", [P, NT, E0], F32)
        self.pair = sb("pair", [P, 6, NT * 4], F32)
        self.group = sb("group", [P, NT, 4], F32)
        self.beats = sb("beats", [P, 2, NT, 4, 4], F32)
        self.rank = sb("rank", [P, NT, 4], F32)
        self.masked = sb("masked", [P, NT, E0], F32)
        self.top = sb("top", [P, NT, 8], F32)
        self.at = sb("at", [P, NT, 8], U32)
        self.at_f = sb("at_f", [P, NT, 4], F32)
        self.hot = sb("hot", [P, NT, 4, E0], F32)
        self.weight = sb("weight", [P, NT, E0], F32)
        self.den = sb("den", [P, NT], F32)
        self.part = sb("part", [P, NT, PARTS, E0], BF16)
        self.partT = sb("partT", [PARTS * E0, N], BF16)
        self.loaded, self.logits, self.scored = ph.sem("r_loaded"), ph.sem("r_logits"), ph.sem("r_scored")
        self.step, self.ready = ph.sem("r_step"), ph.sem("r_ready")
        self.turned, self.kept, self.copied = ph.sem("r_turned"), ph.sem("r_kept"), ph.sem("r_copied")

    def loads(self, sp):
        sp.dma_start(self.bias[:, :], self.arg["f0_bias"]).then_inc(self.loaded, 16)
        sp.dma_start(self.spread_f[:, :], self.arg["spread0"]).then_inc(self.loaded, 16)

    def pe(self, pe):
        nc, c = self.c.nc, self.c
        pe.wait_ge(c.w0_in, 16)
        for t in range(NT):
            last = nc.tensor.matmul(c.bank[7][:, E0 * t:E0 * t + E0], c.xnT[:, P * t:P * t + P], self.w, start=True, stop=True)
        last.then_inc(self.logits, 1)

    def pe_weights(self, pe):
        nc, c = self.c.nc, self.c
        pe.wait_ge(self.ready, 1)
        for t in range(NT):
            out = c.bank[6 + t // 8][:, :].bitcast(BF16)[0:PARTS * E0, P * (t % 8):P * (t % 8) + P]
            last = nc.tensor.transpose(out, self.part[:, t, :, :].rearrange("p m e -> p (m e)"), c.ident_bf[:, :])
            if t % 8 == 7:
                last.then_inc(self.turned, 1)
        pe.wait_ge(self.kept, 2)
        pe.wait_ge(self.copied, 1)

    def scale_rows(self, i, q):
        return self.spread[:, P * i:P * i + P], self.partT[:, CHUNK * q:CHUNK * q + CHUNK]

    def act(self, act):
        nc, c = self.c.nc, self.c
        act.wait_ge(self.logits, 1)
        nc.scalar.activation(self.scores[:, :, :], c.bank[7][:, 0:NT * E0].rearrange("p (t e) -> p t e", t=NT), ACT.Sigmoid).then_inc(self.scored, 1)

    def act_weights(self, act):
        nc, c = self.c.nc, self.c
        for half in range(2):
            act.wait_ge(self.turned, half + 1)
            nc.scalar.copy(self.partT[:, 1024 * half:1024 * half + 1024],
                           c.bank[6 + half][:, :].bitcast(BF16)[0:PARTS * E0, :]).then_inc(self.kept, 1)

    def dve_last(self, dve): pass

    def pool(self, pool):
        pool.wait_ge(self.loaded, 32)
        self.c.nc.gpsimd.tensor_copy(self.spread[:, :], self.spread_f[:, :]).then_inc(self.copied, 1)

    def dve(self, dve):
        nc, c = self.c.nc, self.c
        v = nc.vector
        step = Count(dve, self.step)
        dve.wait_ge(self.loaded, 32)
        dve.wait_ge(self.scored, 1)
        step.link(v.tensor_tensor(self.sc[:, :, :], self.scores[:, :, :], self.bias[:, :].unsqueeze(1).to_broadcast([P, NT, E0]), ALU.add))
        a, b, cc, d = (self.sc[:, :, :].rearrange("p t (g m) -> p (t g) m", g=4)[:, :, m] for m in range(4))
        hi1, lo1, hi2, lo2, both, rest = (self.pair[:, m, :] for m in range(6))
        step.add(v.tensor_tensor(hi1, a, b, ALU.max))
        step.add(v.tensor_tensor(lo1, a, b, ALU.min))
        step.add(v.tensor_tensor(hi2, cc, d, ALU.max))
        step.link(v.tensor_tensor(lo2, cc, d, ALU.min))
        step.add(v.tensor_tensor(both, hi1, hi2, ALU.min))
        step.add(v.tensor_tensor(rest, lo1, lo2, ALU.max))
        step.link(v.tensor_tensor(hi1, hi1, hi2, ALU.max))
        step.link(v.tensor_tensor(both, both, rest, ALU.max))
        group = self.group[:, :, :]
        step.link(v.tensor_tensor(group.rearrange("p t g -> p (t g)"), hi1, both, ALU.add))
        mine = group.unsqueeze(3).to_broadcast([P, NT, 4, 4])
        other = group.unsqueeze(2).to_broadcast([P, NT, 4, 4])
        more, same = self.beats[:, 0, :, :, :], self.beats[:, 1, :, :, :]
        before = c.const[:, BEFORE_AT:BEFORE_AT + 16].rearrange("p (g h) -> p g h", g=4).unsqueeze(1).to_broadcast([P, NT, 4, 4])
        step.add(v.tensor_tensor(more, other, mine, ALU.is_gt))
        step.link(v.tensor_tensor(same, other, mine, ALU.is_ge))
        step.link(v.tensor_tensor(same, same, before, ALU.mult))
        step.link(v.tensor_tensor(more, more, same, ALU.max))
        step.link(v.tensor_reduce(self.rank[:, :, :], more, AX.X, ALU.add))
        step.link(v.tensor_scalar(self.rank[:, :, :], self.rank[:, :, :], 1.5, None, ALU.is_lt))
        step.link(v.tensor_tensor(self.masked[:, :, :].rearrange("p t (g m) -> p t g m", g=4), self.sc[:, :, :].rearrange("p t (g m) -> p t g m", g=4),
                                  self.rank[:, :, :].unsqueeze(3).to_broadcast([P, NT, 4, 4]), ALU.mult))
        for t in range(NT):
            step.add(v.max(self.top[:, t, :], self.masked[:, t, :]))
        step.wait()
        for t in range(NT):
            step.add(v.max_index(self.at[:, t, :], self.top[:, t, :], self.masked[:, t, :]))
        step.wait()
        step.link(v.tensor_copy(self.at_f[:, :, :], self.at[:, :, 0:4]))
        step.link(v.tensor_tensor(self.hot[:, :, :, :], c.const[:, IOTA_AT:IOTA_AT + E0].unsqueeze(1).unsqueeze(1).to_broadcast([P, NT, 4, E0]),
                                  self.at_f[:, :, :].unsqueeze(3).to_broadcast([P, NT, 4, E0]), ALU.is_equal))
        step.link(v.tensor_reduce(self.weight[:, :, :], self.hot[:, :, :, :].rearrange("p t k e -> p t e k"), AX.X, ALU.add))
        weight = self.weight[:, :, :]
        step.link(v.tensor_tensor(weight, weight, self.scores[:, :, :], ALU.mult))
        step.link(v.tensor_reduce(self.den[:, :], weight, AX.X, ALU.add))
        step.link(v.tensor_scalar(self.den[:, :], self.den[:, :], 1e-20, None, ALU.add))
        step.link(v.reciprocal(self.den[:, :], self.den[:, :]))
        step.link(v.scalar_tensor_tensor(out=weight, in0=weight, scalar=ROUTED_SCALE, in1=self.den[:, :].unsqueeze(2).to_broadcast([P, NT, E0]),
                                         op0=ALU.mult, op1=ALU.mult))
        part = [self.part[:, :, m, :] for m in range(PARTS)]
        step.link(v.tensor_copy(part[0], weight))
        step.link(v.tensor_tensor(weight, weight, part[0], ALU.subtract))
        step.link(v.tensor_copy(part[1], weight))
        v.tensor_tensor(part[2], weight, part[1], ALU.subtract).then_inc(self.ready, 1)


def layer0_ffn(c, arg):
    with Phase(c, "f0_") as ph:
        router = Router0(c, ph, arg)
        up = [c.wa[:, L0_AT + P * i:L0_AT + P * i + P] for i in range(HID0)]
        down = [c.wa[:, L0_AT + P * (HID0 + i):L0_AT + P * (HID0 + i) + P] for i in range(HID0)]
        dense_block(c, ph, up, None, down, 8, router, c.wb)


def layer1_attention(c, arg):
    nc = c.nc
    with Phase(c, "a1_") as ph:
        w = ph.sb("w", [P, 2, P], F32)
        bias = ph.sb("bias", [1, P], F32)
        one_hot = ph.sb("one_hot", [B, B, P], F32)
        mean = ph.sb("mean", [P, B], F32)
        rows = ph.sb("rows", [B, P], F32)
        loaded, mean_ready, rows_out, rows_ready = (ph.sem(n) for n in ("loaded", "mean", "rows_out", "rows_ready"))
        out_done, added = ph.sem("out_done"), ph.sem("added")
        with nc.Block() as block:
            @block.sync
            def _(sp):
                sp.dma_start(w[:, :, :], arg["a1_w"].rearrange("n p d -> p n d")).then_inc(loaded, 16)
                sp.dma_start(bias[:, :], arg["a1_bias"]).then_inc(loaded, 16)
                sp.dma_start(one_hot[:, :, :], arg["one_hot8"]).then_inc(loaded, 16)
                cols = E_GATED * GATED_COLS // 8
                for n in range(8):
                    sp.dma_start(c.wb[:, cols * n:cols * n + cols], arg["f2_w"][:, cols * n:cols * n + cols]).then_inc(c.w2_in, 16)

            @block.tensor
            def _(pe):
                pe.wait_ge(loaded, 48)
                pe.wait_ge(mean_ready, 1)
                nc.tensor.matmul(c.bank[7][0:B, 0:P], mean[:, :], w[:, 1, :], start=True, stop=False)
                nc.tensor.matmul(c.bank[7][0:B, 0:P], c.ones[0:1, 0:B], bias[:, :], start=False, stop=True).then_inc(rows_out, 1)
                pe.wait_ge(rows_ready, 1)
                for t in range(NT):
                    out = c.bank[t // 4][:, P * (t % 4):P * (t % 4) + P]
                    nc.tensor.matmul(out, c.xnT[:, P * t:P * t + P], w[:, 0, :], start=True, stop=False)
                    nc.tensor.matmul(out, one_hot[:, t // TPB, :], rows[:, :], start=False, stop=True).then_inc(out_done, 1)

            @block.scalar
            def _(act):
                nc.scalar.mul(mean[:, :], c.ctx_sum[:, :], 1.0 / CTX).then_inc(mean_ready, 1)
                act.wait_ge(rows_out, 1)
                nc.scalar.copy(rows[:, :], c.bank[7][0:B, 0:P]).then_inc(rows_ready, 1)

            @block.vector
            def _(dve):
                for q in range(NT // 4):
                    dve.wait_ge(out_done, 4 * (q + 1))
                    xs = c.x[:, TPB + 4 * q:TPB + 4 * q + 4, :]
                    nc.vector.tensor_tensor(xs, xs, c.bank[q][:, :].rearrange("p (t d) -> p t d", t=4), ALU.add).then_inc(added, 1)
                    dve.wait_ge(added, q + 1)
                    for t in range(4):
                        c.take_stats(TPB + 4 * q + t)


class Beside:

    def __init__(self, c, pool, dve_last):
        self.c, self.pool, self.dve_last = c, pool, dve_last

    def pe(self, pe):
        pe.wait_ge(self.c.w1_in, 16 * 8)

    def loads(self, sp): pass
    def act(self, act): pass
    def dve(self, dve): pass


def layer1_shared(c, tag, first, chunks, pool, dve_last):
    with Phase(c, tag) as ph:
        at = (E_GATED - 1) * GATED_COLS
        gate, up, down = ([c.wa[:, at + skip + P * i:at + skip + P * i + P] for i in range(4)] for skip in (0, HID, 2 * HID))
        dense_block(c, ph, up, gate, down, 0, Beside(c, pool, dve_last), c.wa[:, L0_AT:], first, chunks)


def layer3_attention(c, arg):
    nc = c.nc
    KT = CTX // P
    with Phase(c, "a3_") as ph:
        sb, sem = ph.sb, ph.sem
        w = sb("w", [P, 4, P], F32)
        bias_qk = sb("bias_qk", [P, 2], F32)
        bias_q = sb("bias_q", [P, 1], F32)
        bias_vo = sb("bias_vo", [P, 2, P], F32)
        ctxT = sb("ctxT", [P, 2, CTX], F32)
        qT = sb("qT", [P, 2, TOK], F32)
        kT = sb("kT", [P, 2, CTX], F32)
        v = sb("v", [P, 2, KT, P], F32)
        neg_max = sb("neg_max", [P, 2, TPB], F32)
        total = sb("total", [P, 2, TPB], F32)
        inverse = sb("inverse", [P, 2, TPB], F32)
        prob = sb("prob", [P, 2, TPB, CTX], F32)
        probT = sb("probT", [P, KT, TOK], F32)
        headT = sb("headT", [P, TOK], F32)
        loaded, biased = sem("loaded"), sem("biased")
        ctx_in = [sem(f"ctx_in{p}") for p in range(2)]
        proj_q, proj_k, proj_v = sem("proj_q"), sem("proj_k"), sem("proj_v")
        full_q, full_k, full_v = sem("full_q"), sem("full_k"), sem("full_v")
        logits, max_done, exp_done = sem("logits"), sem("max_done"), sem("exp_done")
        turned, kept = sem("turned"), sem("kept")
        head_out, head_kept, out_done = sem("head_out"), sem("head_kept"), sem("out_done")
        inv_done, x_done, bias_added = sem("inv_done"), sem("x_done"), sem("bias_added")
        k_bank, q_bank, v_bank, l_bank, p_bank, o_bank = c.bank[0], c.bank[1], c.bank[2], c.bank[3:5], c.bank[5:7], c.bank[7]
        scale = float(P) ** -0.5

        def slots(eng, first, step, last):
            for b in first:
                step(b, b % 2, b // 2)
            with eng.Fori(1, 3) as g:
                for p in range(2):
                    step(2 * g + p, p, g)
            for b in last:
                step(b, b % 2, b // 2)

        with nc.Block() as block:
            @block.sync
            def _(sp):
                sp.dma_start(w[:, :, :], arg["a3_w"]).then_inc(loaded, 16)
                sp.dma_start(bias_qk[:, :], arg["a3_bias_qk"]).then_inc(loaded, 16)
                sp.dma_start(bias_vo[:, :, :], arg["a3_bias_vo"]).then_inc(loaded, 16)

                def step(b, p, g):
                    need(sp, proj_k, b - 1)
                    need(sp, proj_v, b - 1)
                    sp.dma_start(ctxT[:, p, :], arg["ctxT"][:, ds(b, 1), :].rearrange("d o k -> d (o k)")).then_inc(ctx_in[p], 16)

                slots(sp, (0, 1), step, (6, 7))

            @block.tensor
            def _(pe):
                def project(b, p, g):
                    pe.wait_ge(ctx_in[p], 16 * g + 16)
                    need(pe, full_k, b)
                    nc.tensor.matmul(k_bank[:, :], w[:, 1, :], ctxT[:, p, :], start=True, stop=True).then_inc(proj_k, 1)
                    need(pe, full_q, b)
                    nc.tensor.matmul(q_bank[:, 0:TOK], w[:, 0, :], c.xnT[:, ds(TOK * b, TOK)], start=True, stop=True).then_inc(proj_q, 1)
                    need(pe, full_v, b)
                    for t in range(KT):
                        last = nc.tensor.matmul(v_bank[:, P * t:P * t + P], ctxT[:, p, P * t:P * t + P], w[:, 2, :], start=True, stop=True)
                    last.then_inc(proj_v, 1)

                def find_logits(b, p, g):
                    pe.wait_ge(full_q, b + 1)
                    pe.wait_ge(full_k, b + 1)
                    for t in range(TPB):
                        need(pe, exp_done, 2 * b + t - 1)
                        nc.tensor.matmul(l_bank[t][:, :], qT[:, p, P * t:P * t + P], kT[:, p, :], start=True, stop=True).then_inc(logits, 1)

                def turn(b, p, g):
                    for t in range(TPB):
                        pe.wait_ge(exp_done, 2 * b + t + 1)
                        need(pe, kept, 2 * b + t - 1)
                        for k in range(KT):
                            last = nc.tensor.transpose(p_bank[t][:, P * k:P * k + P], prob[:, p, t, P * k:P * k + P], c.ident[:, :])
                        last.then_inc(turned, 1)

                def weigh(b, p, g):
                    pe.wait_ge(kept, 2 * b + 2)
                    pe.wait_ge(full_v, b + 1)
                    need(pe, x_done, b)
                    for k in range(KT):
                        last = nc.tensor.matmul(o_bank[:, 0:TOK], v[:, p, k, :], probT[:, k, :], start=(k == 0), stop=(k == KT - 1))
                    last.then_inc(head_out, 1)

                def project_out(b, p, g):
                    pe.wait_ge(head_kept, b + 1)
                    for t in range(TPB):
                        last = nc.tensor.matmul(o_bank[:, TOK + P * t:TOK + P * t + P], headT[:, P * t:P * t + P], w[:, 3, :],
                                                start=True, stop=True)
                    last.then_inc(out_done, 1)

                def step(b, p, g):
                    turn(b, p, g)
                    if not isinstance(b, int) or b < B - 1:
                        project(b + 1, 1 - p, g + p)
                    weigh(b, p, g)
                    if not isinstance(b, int) or b < B - 1:
                        find_logits(b + 1, 1 - p, g + p)
                    project_out(b, p, g)

                pe.wait_ge(loaded, 48)
                project(0, 0, 0)
                find_logits(0, 0, 0)
                slots(pe, (0, 1), step, (6, 7))

            @block.scalar
            def _(act):
                def project(b, p, g):
                    act.wait_ge(proj_k, b + 1)
                    need(act, logits, 2 * b - 2)
                    nc.scalar.activation(kT[:, p, :], k_bank[:, :], ACT.Identity, bias=bias_qk[:, 1:2]).then_inc(full_k, 1)
                    act.wait_ge(proj_q, b + 1)
                    nc.scalar.activation(qT[:, p, :], q_bank[:, 0:TOK], ACT.Identity, bias=bias_q[:, :], scale=scale).then_inc(full_q, 1)

                def exps(b, p, g):
                    for t in range(TPB):
                        act.wait_ge(max_done, 2 * b + t + 1)
                        need(act, turned, 2 * b - 3 + t)
                        need(act, inv_done, b - 1)
                        nc.scalar.activation(prob[:, p, t, :], l_bank[t][:, :], ACT.Exp, bias=neg_max[:, p, t:t + 1],
                                             accum_out=total[:, p, t:t + 1]).then_inc(exp_done, 1)

                def step(b, p, g):
                    more = not isinstance(b, int) or b < B - 1
                    if more:
                        project(b + 1, 1 - p, g + p)
                    act.wait_ge(head_out, b + 1)
                    need(act, out_done, b)
                    nc.scalar.copy(headT[:, :], o_bank[:, 0:TOK]).then_inc(head_kept, 1)
                    if more:
                        exps(b + 1, 1 - p, g + p)

                act.wait_ge(loaded, 48)
                nc.scalar.mul(bias_q[:, :], bias_qk[:, 0:1], scale).then_inc(biased, 1)
                act.wait_ge(biased, 1)
                project(0, 0, 0)
                exps(0, 0, 0)
                slots(act, (0, 1), step, (6, 7))

            @block.vector
            def _(dve):
                def keep_v(b, p, g):
                    dve.wait_ge(proj_v, b + 1)
                    need(dve, head_out, b - 1)
                    nc.vector.tensor_tensor(v[:, p, :, :], v_bank[:, :].rearrange("p (t d) -> p t d", t=KT),
                                            bias_vo[:, 0:1, :].to_broadcast([P, KT, P]), ALU.add).then_inc(full_v, 1)

                def maxima(b, p, g):
                    for t in range(TPB):
                        dve.wait_ge(logits, 2 * b + t + 1)
                        nc.vector.tensor_reduce(neg_max[:, p, t:t + 1], l_bank[t][:, :], AX.X, ALU.max, negate=True).then_inc(max_done, 1)

                def step(b, p, g):
                    more = not isinstance(b, int) or b < B - 1
                    for t in range(TPB):
                        dve.wait_ge(turned, 2 * b + t + 1)
                        need(dve, head_out, b)
                        nc.vector.tensor_copy(probT[:, :, P * t:P * t + P], p_bank[t][:, :].rearrange("p (k q) -> p k q", k=KT)).then_inc(kept, 1)
                    nc.vector.reciprocal(inverse[:, p, :], total[:, p, :]).then_inc(inv_done, 1)
                    if more:
                        keep_v(b + 1, 1 - p, g + p)
                        maxima(b + 1, 1 - p, g + p)
                    dve.wait_ge(out_done, b + 1)
                    dve.wait_ge(inv_done, b + 1)
                    dve.wait_ge(bias_added, 1)
                    for t in range(TPB):
                        xs = c.x[:, ds(TPB * b + TPB + t, 1), :].rearrange("p o d -> p (o d)")
                        last = nc.vector.scalar_tensor_tensor(out=xs, in0=o_bank[:, TOK + P * t:TOK + P * t + P], scalar=inverse[:, p, t:t + 1],
                                                              in1=xs, op0=ALU.mult, op1=ALU.add)
                    last.then_inc(x_done, 1)
                    dve.wait_ge(x_done, b + 1)
                    for t in range(TPB):
                        c.take_stats(TPB * b + (TPB + t))

                dve.wait_ge(loaded, 48)
                keep_v(0, 0, 0)
                maxima(0, 0, 0)
                slots(dve, (0, 1), step, (6, 7))

            @block.gpsimd
            def _(pool):
                pool.wait_ge(loaded, 48)
                xs = c.x[:, TPB:, :]
                nc.gpsimd.tensor_tensor(xs, xs, bias_vo[:, 1:2, :].to_broadcast([P, NT, P]), ALU.add).then_inc(bias_added, 1)


class Experts:

    def __init__(self, layer):
        self.layer = layer
        self.gated = layer != 3
        self.E = E3 if layer == 3 else E_GATED
        self.K = {1: 1, 2: 2, 3: 4}[layer]
        self.last = self.E - 2 if layer == 1 else self.E - 1
        self.before = {1: 0, 2: NT, 3: 3 * NT}[layer]
        self.cols = GATED_COLS if self.gated else 2 * P
        self.tiles = N * self.K // P + self.E
        self.per_step = 1 if self.gated else 4
        self.steps = self.tiles // self.per_step
        assert self.steps % 4 == 0 and self.tiles * P <= TABLE and self.tiles <= P


def in_slots(nc, eng, T, slot, first=2):
    for k in range(first + 4):
        slot(0, k)
    with eng.Fori(4, T - 4, 4) as s:
        s = nc.s_assert_within(s, 4, T - 8, skip_runtime_bounds_check_because="the loop goes by fours")
        for k in range(first, first + 4):
            slot(s, k)
    for k in range(first, 6):
        slot(T - 4, k)


def experts_phase(c, layer, arg):
    nc = c.nc
    m = Experts(layer)
    E, K, T, W = m.E, m.K, m.steps, m.per_step * P
    weights, weights_in = (c.wb, c.w2_in) if layer == 2 else (c.wa, c.w1_in if layer == 1 else c.w3_in)
    with Phase(c, f"e{layer}_") as ph:
        sb, sem = ph.sb, ph.sem
        w_router = sb("w_router", [P, E], F32)
        key = sb("key", [P, NT, E], F32)
        top = sb("top", [P, NT, 8], F32)
        at = sb("at", [P, NT, 8], U32)
        at_f = sb("at_f", [P, NT, K], F32)
        gate = sb("gate", [P, NT, K], F32)
        small = sb("small", [P, 2, NT], F32)
        at_bf = sb("at_bf", [P, NT, K], BF16)
        iota_bf = sb("iota_bf", [P, E], BF16)
        hot = sb("hot", [P, NT, K, E], BF16)
        chosen = sb("chosen", [P, NT, E], BF16)
        sums = sb("sums", [P, 2, NT + 1, E], BF16)
        tri = sb("tri", [P, P], BF16)
        ones_bf = sb("ones_bf", [P, P], BF16)
        tiles_i = sb("tiles_i", [P, E], I32)
        cum = sb("cum", [P, 3, E], F32)
        place = sb("place", [P, NT, E], F32)
        if layer == 3:
            spread = c.wb[:, 0:NT * K * E].rearrange("p (t k e) -> p t k e", t=NT, k=K)
        else:
            spread = sb("spread", [P, NT, K, E], F32)[:, :, :, :]
        pos_f = sb("pos_f", [P, NT * K], F32)
        pos = sb("pos", [P, NT * K], I32)
        owner_f = sb("owner_f", [P, 2], F32)
        owner_row = sb("owner_row", [1, P], F32)
        owner_mix = sb("owner_mix", [1, P], F32)
        owner = sb("owner", [1, P], I32)
        xs = sb("xs", [P, 4, W], F32)
        xT = sb("xT", [P, 2, W], F32)
        silu = sb("silu", [P, 2, HID], F32) if m.gated else None
        h = sb("h", [P, 2, HID], F32)
        hT = sb("hT", [P, 2, HID], F32)
        y = sb("y", [P, 4, W], F32)
        BACK = 16 if layer == 1 else 8
        back = sb("back", [P, BACK, P], F32)

        rows_out = nc.dram_tensor(f"rows_out{layer}", [m.tiles * P, P], F32)

        loaded, logits_done, key_done, step_done = sem("loaded"), sem("logits_done"), sem("key_done"), sem("step_done")
        const_bf, sums_done, counted, pos_done = sem("const_bf"), sem("sums_done"), sem("counted"), sem("pos_done")
        silu_go, gate_go = sem("silu_go"), sem("gate_go")
        owner_done, owner_in = sem("owner_done"), sem("owner_in")
        x_in = [sem(f"x_in{k}") for k in range(4)]
        turned_x, xT_ready, up_done, silu_done, h_done = (sem(n) for n in ("turned_x", "xT_ready", "up_done", "silu_done", "h_done"))
        turned_h, hT_ready, down_done, y_ready = (sem(n) for n in ("turned_h", "hT_ready", "down_done", "y_ready"))
        stored = [sem(f"stored{k}") for k in range(4)]
        back_used = sem("back_used")
        x_bank, h_bank, y_bank = c.bank[4], c.bank[6], (c.bank[5], c.bank[7])

        def rows_of(table, s):
            rows = table[ds(W * s, W), :]
            return rows.rearrange("(j p) d -> p j d", p=P)

        def columns(buffer, k):
            return buffer[:, k % 4, :].rearrange("p (j d) -> p j d", d=P)

        def alive(s, k, d=0):
            return not isinstance(s, int) or 0 <= s + k + d < T

        def scatter(pool):
            pool.wait_ge(c.rows_zero, 16 * 8)
            for t in range(NT):
                pool.wait_ge(pos_done, t // 4 + 1)
                for j in range(K):
                    pool.indirect_dma_start(out=c.rows_in[:, :], out_offset=bass.IndirectOffsetOnAxis(ap=pos[:, K * t + j:K * t + j + 1], axis=0),
                                            in_=c.xn[:, t, :], in_offset=None).then_inc(c.scattered, 16)

        def gather(pool):
            for k in range(4):
                pool.wait_ge(stored[k], 16 * T // 4)
            for n in range(NT * K):
                need(pool, back_used, n - BACK + 1)
                pool.indirect_dma_start(out=back[:, n % BACK, :], out_offset=None, in_=rows_out[:, :],
                                        in_offset=bass.IndirectOffsetOnAxis(ap=pos[:, n:n + 1], axis=0)).then_inc(c.back_in[n % 8], 16)

        def combine(dve):
            for n in range(NT * K):
                dve.wait_ge(c.back_in[n % 8], 16 * ((m.before + (n if BACK == 8 else NT * K - 8 + n % 8)) // 8 + 1))
                xs_t = c.x[:, TPB + n // K, :]
                if n % K:
                    dve.wait_ge(back_used, n)
                nc.vector.scalar_tensor_tensor(out=xs_t, in0=back[:, n % BACK, :], scalar=gate[:, n // K, n % K:n % K + 1], in1=xs_t,
                                               op0=ALU.mult, op1=ALU.add).then_inc(back_used, 1)
                if n % K == 0 and n and layer != 3:
                    dve.wait_ge(back_used, n)
                    c.take_stats(TPB + n // K - 1)
            if layer != 3:
                dve.wait_ge(back_used, NT * K)
                c.take_stats(TPB + NT - 1)

        with nc.Block() as block:
            @block.sync
            def _(sp):
                sp.dma_start(w_router[:, :], arg[f"e{layer}_router"]).then_inc(loaded, 16)
                sp.wait_ge(owner_done, 1)
                sp.dma_start(owner_row[:, :], owner_f[:, 1:2]).then_inc(owner_in, 16)

            @block.gpsimd
            def _(pool):
                if layer != 1:
                    scatter(pool)

            @block.tensor
            def _(pe):
                pe.wait_ge(loaded, 16)
                for t in range(NT):
                    out = c.bank[t * E // 512][:, E * t % 512:E * t % 512 + E]
                    last = nc.tensor.matmul(out, c.xnT[:, P * t:P * t + P], w_router[:, :], start=True, stop=True)
                last.then_inc(logits_done, 1)
                pe.wait_ge(const_bf, 2)
                pe.wait_ge(sums_done, 1)
                half = max(1, NT * E // 512)
                per = NT // half
                for b in range(half):
                    out = c.bank[2 + b][:, 0:per * E]
                    nc.tensor.matmul(out, tri[:, :], chosen[:, per * b:per * b + per, :].rearrange("p t e -> p (t e)"), start=True, stop=False)
                    nc.tensor.matmul(out, ones_bf[:, :], sums[:, 0, per * b:per * b + per, :].rearrange("p t e -> p (t e)"), start=False, stop=True)
                nc.tensor.matmul(c.bank[4][:, 0:E], ones_bf[:, :], sums[:, 0, NT, :], start=True, stop=True).then_inc(counted, 1)

            @block.scalar
            def _(act):
                act.wait_ge(logits_done, 1)
                if layer == 1:
                    act.wait_ge(step_done, 4)
                    nc.scalar.activation(key[:, :, :], key[:, :, :], ACT.Exp).then_inc(key_done, 1)
                if layer == 2:
                    act.wait_ge(gate_go, 1)
                    nc.scalar.activation(gate[:, :, 1], small[:, 0, :], ACT.Exp).then_inc(key_done, 1)
                if layer == 3:
                    for b in range(2):
                        nc.scalar.activation(key[:, 8 * b:8 * b + 8, :], c.bank[b][:, :].rearrange("p (t e) -> p t e", t=8), ACT.Sigmoid).then_inc(key_done, 1)

            @block.vector
            def _(dve):
                v = nc.vector
                step = Count(dve, step_done)
                v.tensor_copy(tri[:, :], c.const[:, TRI_AT:TRI_AT + P]).then_inc(const_bf, 1)
                v.memset(ones_bf[:, :], 1.0).then_inc(const_bf, 1)
                step.add(v.tensor_copy(iota_bf[:, :], c.const[:, IOTA_AT:IOTA_AT + E]))
                step.link(v.memset(sums[:, :, 0:1, :], 0.0))
                dve.wait_ge(logits_done, 1)
                if layer == 1:
                    logits = c.bank[0][:, 0:NT * E].rearrange("p (t e) -> p t e", t=NT)
                    wide = [P, NT, E]
                    step.link(v.tensor_reduce(small[:, 0, :], logits, AX.X, ALU.max))
                    step.add(v.tensor_tensor(key[:, :, :], logits, small[:, 0, :].unsqueeze(2).to_broadcast(wide), ALU.subtract))
                    dve.wait_ge(key_done, 1)
                    step.link(v.tensor_reduce(small[:, 0, :], key[:, :, :], AX.X, ALU.add))
                    step.link(v.reciprocal(small[:, 1, :], small[:, 0, :]))
                    step.link(v.tensor_tensor(key[:, :, :], key[:, :, :], small[:, 1, :].unsqueeze(2).to_broadcast(wide), ALU.mult))
                elif layer == 2:
                    step.link(v.tensor_copy(key[:, :, :], c.bank[0][:, 0:NT * E].rearrange("p (t e) -> p t e", t=NT)))
                else:
                    dve.wait_ge(key_done, 2)
                for t in range(NT):
                    step.add(v.max(top[:, t, :], key[:, t, :]))
                step.wait()
                if layer == 2:
                    v.tensor_tensor(small[:, 0, :], top[:, :, 1], top[:, :, 0], ALU.subtract).then_inc(gate_go, 1)
                for t in range(NT):
                    step.add(v.max_index(at[:, t, :], top[:, t, :], key[:, t, :]))
                step.wait()
                step.add(v.tensor_copy(at_f[:, :, :], at[:, :, 0:K]))
                step.link(v.tensor_copy(at_bf[:, :, :], at[:, :, 0:K]))
                shape = [P, NT, K, E]
                step.add(v.tensor_tensor(hot[:, :, :, :], iota_bf[:, :].unsqueeze(1).unsqueeze(1).to_broadcast(shape),
                                         at_bf[:, :, :].unsqueeze(3).to_broadcast(shape), ALU.is_equal))
                if layer == 1:
                    step.link(v.tensor_scalar(gate[:, :, 0], at_f[:, :, 0], float(m.last) + 0.5, 2.0, ALU.is_lt, ALU.mult))
                    step.link(v.tensor_tensor(gate[:, :, 0], gate[:, :, 0], top[:, :, 0], ALU.mult))
                elif layer == 2:
                    dve.wait_ge(key_done, 1)
                    step.link(v.tensor_scalar(small[:, 1, :], gate[:, :, 1], 1.0, None, ALU.add))
                    step.link(v.reciprocal(gate[:, :, 0], small[:, 1, :]))
                    step.link(v.tensor_tensor(gate[:, :, 1], gate[:, :, 1], gate[:, :, 0], ALU.mult))
                else:
                    step.link(v.tensor_copy(gate[:, :, :], top[:, :, 0:K]))
                with nc.allow_low_precision("counts up to 16 are exact"):
                    if K == 1:
                        step.link(v.tensor_copy(chosen[:, :, :], hot[:, :, 0, :]))
                    else:
                        step.add(v.tensor_tensor(chosen[:, :, :], hot[:, :, 0, :], hot[:, :, 1, :], ALU.add))
                        if K == 4:
                            step.add(v.tensor_tensor(sums[:, 1, 1:, :], hot[:, :, 2, :], hot[:, :, 3, :], ALU.add))
                            step.wait()
                            step.add(v.tensor_tensor(chosen[:, :, :], chosen[:, :, :], sums[:, 1, 1:, :], ALU.add))
                        step.wait()
                    step.link(v.tensor_copy(sums[:, 0, 1:, :], chosen[:, :, :]))
                    for n, d in enumerate((1, 2, 4, 8)):
                        src, dst = sums[:, n % 2], sums[:, 1 - n % 2]
                        step.add(v.tensor_copy(dst[:, 1:1 + d, :], src[:, 1:1 + d, :]))
                        last = v.tensor_tensor(dst[:, 1 + d:, :], src[:, 1 + d:, :], src[:, 1:NT + 1 - d, :], ALU.add)
                        step.link(last)
                    dve.sem_inc(sums_done, 1)
                dve.wait_ge(counted, 1)
                step.link(v.tensor_scalar(tiles_i[:, :], c.bank[4][:, 0:E], float(P - 1), None, ALU.add))
                step.link(v.tensor_scalar(tiles_i[:, :], tiles_i[:, :], 7, None, ALU.logical_shift_right))
                step.link(v.tensor_copy(cum[:, 0, :], tiles_i[:, :]))
                now, d = 0, 1
                while d < E:
                    step.add(v.tensor_copy(cum[:, 1 - now, 0:d], cum[:, now, 0:d]))
                    step.link(v.tensor_tensor(cum[:, 1 - now, d:], cum[:, now, d:], cum[:, now, 0:E - d], ALU.add))
                    now, d = 1 - now, 2 * d
                step.add(v.tensor_scalar(cum[:, 1 - now, :], cum[:, now, :], c.const[:, PART_AT:PART_AT + 1], None, ALU.is_le))
                step.link(v.tensor_tensor(cum[:, 2, :], cum[:, now, :], tiles_i[:, :], ALU.subtract))
                step.link(v.tensor_reduce(owner_f[:, 0:1], cum[:, 1 - now, :], AX.X, ALU.add))
                v.tensor_scalar(owner_f[:, 1:2], owner_f[:, 0:1], float(m.last), None, ALU.min).then_inc(owner_done, 1)
                step.link(v.tensor_scalar(cum[:, 2, :], cum[:, 2, :], float(P), None, ALU.mult))
                per = NT // max(1, NT * E // 512)
                part = NT // 4
                for g in range(4):
                    tiles = slice(part * g, part * g + part)
                    ranks = c.bank[2 + part * g // per][:, part * g % per * E:(part * g % per + part) * E]
                    step.link(v.tensor_tensor(place[:, tiles, :], ranks.rearrange("p (t e) -> p t e", t=part),
                                              cum[:, 2:3, :].to_broadcast([P, part, E]), ALU.add))
                    step.link(v.tensor_tensor(spread[:, tiles, :, :], hot[:, tiles, :, :],
                                              place[:, tiles, :].unsqueeze(2).to_broadcast([P, part, K, E]), ALU.mult))
                    at_pos = slice(part * K * g, part * K * (g + 1))
                    step.link(v.tensor_reduce(pos_f[:, at_pos].rearrange("p (t k) -> p t k", t=part), spread[:, tiles, :, :], AX.X, ALU.add))
                    v.tensor_copy(pos[:, at_pos], pos_f[:, at_pos]).then_inc(pos_done, 1)

                dve.wait_ge(owner_in, 16)
                if m.gated:
                    v.tensor_scalar(owner[:, :], owner_row[:, :], float(m.cols), None, ALU.mult)
                else:
                    fields = c.const[0:1, FIELD_AT:FIELD_AT + 4].unsqueeze(1).to_broadcast([1, T, 4])
                    step.link(v.tensor_tensor(owner_mix[:, :].rearrange("o (s j) -> o s j", j=4), owner_row[:, :].rearrange("o (s j) -> o s j", j=4),
                                              fields, ALU.mult))
                    step.link(v.tensor_reduce(owner_row[:, 0:T], owner_mix[:, :].rearrange("o (s j) -> o s j", j=4), AX.X, ALU.add))
                    v.tensor_copy(owner[:, 0:T], owner_row[:, 0:T])

        if layer == 1:
            layer1_shared(c, "s1_", 0, NC // 2, scatter, lambda dve: None)

        with nc.Block() as block:
            @block.sync
            def _(sp):
                def load(s, k):
                    need(sp, turned_x, s + k - 3)
                    sp.dma_start(columns(xs, k), rows_of(c.rows_in, s + k)).then_inc(x_in[k % 4], 16)

                def store(s, k):
                    sp.wait_ge(y_ready, s + k + 1)
                    sp.dma_start(rows_of(rows_out, s + k), columns(y, k)).then_inc(stored[k % 4], 16)

                def slot(s, k):
                    if alive(s, k, 3):
                        load(s, k + 3)
                    if alive(s, k, -2):
                        store(s, k - 2)

                sp.wait_ge(c.scattered, 16 * (m.before + NT * K))
                for k in range(3):
                    load(0, k)
                in_slots(nc, sp, T, slot, first=1)

            @block.gpsimd
            def _(pool):
                if layer != 1:
                    gather(pool)

            @block.tensor
            def _(pe):
                def entry(s, k):
                    n = s + k
                    at = pe.value_load(owner[0:1, ds(n, 1)] if not isinstance(n, int) else owner[0:1, n:n + 1])
                    if not m.gated:
                        return at
                    return nc.s_assert_within(at, 0, m.last * m.cols, skip_runtime_bounds_check_because="entries are clipped to the last expert")

                held = {}

                def name(s):
                    return s if isinstance(s, int) else "loop"

                def early(s, k):
                    if alive(s, k, 1) and k < 5:
                        held[name(s), k + 1] = entry(s, k + 1)

                def held_entry(s, k):
                    if (name(s), k) not in held:
                        held[name(s), k] = entry(s, k)
                    return held[name(s), k]

                def field(v, j):
                    shift = 6 * j - 8
                    e = ((v >> shift) if shift > 0 else (v << -shift)) & (63 * m.cols)
                    return nc.s_assert_within(e, 0, m.last * m.cols, skip_runtime_bounds_check_because="entries are clipped to the last expert")

                def can_turn_x(s, k):
                    pe.wait_ge(x_in[k % 4], 4 * s + 16 * (k // 4 + 1))
                    need(pe, xT_ready, s + k)

                def can_up(s, k):
                    pe.wait_ge(xT_ready, s + (k + 1))
                    need(pe, h_done, s + (k - 1))

                def can_turn_h(s, k):
                    pe.wait_ge(h_done, s + (k + 1))
                    need(pe, hT_ready, s + k)

                def can_down(s, k):
                    pe.wait_ge(hT_ready, s + (k + 1))
                    need(pe, y_ready, s + (k - 1))

                def turn_x(k, j):
                    return nc.tensor.transpose(x_bank[:, P * j:P * j + P], xs[:, k % 4, P * j:P * j + P], c.ident[:, :])

                def turn_h(k, j):
                    return nc.tensor.transpose(h_bank[:, P * j:P * j + P], h[:, k % 2, P * j:P * j + P], c.ident[:, :])

                def gated_slot(s, k):
                    e = held_entry(s, k) if alive(s, k) else None
                    if alive(s, k, 1):
                        can_turn_x(s, k + 1)
                        turn_x(k + 1, 0).then_inc(turned_x, 1)
                    if alive(s, k):
                        can_up(s, k)
                        nc.tensor.matmul(c.bank[k % 2][:, :], xT[:, k % 2, :], weights[:, ds(e, HID)], start=True, stop=True).then_inc(silu_go, 1)
                    before = held_entry(s, k - 2) if alive(s, k, -2) else None
                    early(s, k)
                    if alive(s, k):
                        nc.tensor.matmul(c.bank[2 + k % 2][:, :], xT[:, k % 2, :], weights[:, ds(e + HID, HID)],
                                         start=True, stop=True).then_inc(up_done, 1)
                    if alive(s, k, -1):
                        can_turn_h(s, k - 1)
                        for j in range(4):
                            last = turn_h(k - 1, j)
                        last.then_inc(turned_h, 1)
                    if alive(s, k, -2):
                        can_down(s, k - 2)
                        for j in range(4):
                            last = nc.tensor.matmul(y_bank[k % 2][:, 0:P], hT[:, k % 2, P * j:P * j + P],
                                                    weights[:, ds(before + (2 * HID + P * j), P)], start=(j == 0), stop=(j == 3))
                        last.then_inc(down_done, 1)

                def narrow_slot(s, k):
                    now = held_entry(s, k) if alive(s, k) else None
                    if alive(s, k, 1):
                        can_turn_x(s, k + 1)
                    if alive(s, k):
                        can_up(s, k)
                    for j in range(4):
                        if j == 1:
                            before = held_entry(s, k - 2) if alive(s, k, -2) else None
                        if j == 2:
                            early(s, k)
                        if alive(s, k, 1):
                            turned = turn_x(k + 1, j)
                        if alive(s, k):
                            up = nc.tensor.matmul(c.bank[k % 2][:, P * j:P * j + P], xT[:, k % 2, P * j:P * j + P], weights[:, ds(field(now, j), P)],
                                                  start=True, stop=True)
                    if alive(s, k, 1):
                        turned.then_inc(turned_x, 1)
                    if alive(s, k):
                        up.then_inc(up_done, 1)
                    if alive(s, k, -1):
                        can_turn_h(s, k - 1)
                    if alive(s, k, -2):
                        can_down(s, k - 2)
                    for j in range(4):
                        if alive(s, k, -1):
                            turned = turn_h(k - 1, j)
                        if alive(s, k, -2):
                            down = nc.tensor.matmul(y_bank[k % 2][:, P * j:P * j + P], hT[:, k % 2, P * j:P * j + P],
                                                    weights[:, ds(field(before, j) + P, P)], start=True, stop=True)
                    if alive(s, k, -1):
                        turned.then_inc(turned_h, 1)
                    if alive(s, k, -2):
                        down.then_inc(down_done, 1)

                pe.wait_ge(weights_in, 16 * 8)
                can_turn_x(0, 0)
                for j in range(m.per_step):
                    last = turn_x(0, j)
                last.then_inc(turned_x, 1)
                in_slots(nc, pe, T, gated_slot if m.gated else narrow_slot)

            @block.scalar
            def _(act):
                def activate(s, k):
                    if m.gated:
                        act.wait_ge(silu_go, s + (k + 1))
                        need(act, h_done, s + (k - 1))
                        nc.scalar.activation(silu[:, k % 2, :], c.bank[k % 2][:, :], ACT.Silu).then_inc(silu_done, 1)
                    else:
                        act.wait_ge(up_done, s + (k + 1))
                        need(act, turned_h, s + (k - 1))
                        nc.scalar.activation(h[:, k % 2, :], c.bank[k % 2][:, :], ACT.Relu).then_inc(h_done, 1)

                def keep_h(s, k):
                    act.wait_ge(turned_h, s + (k + 1))
                    need(act, down_done, s + (k - 1))
                    nc.scalar.copy(hT[:, k % 2, :], h_bank[:, :]).then_inc(hT_ready, 1)

                def slot(s, k):
                    if alive(s, k):
                        activate(s, k)
                    if alive(s, k, -1):
                        keep_h(s, k - 1)

                in_slots(nc, act, T, slot)

            @block.vector
            def _(dve):
                v = nc.vector

                def keep_x(s, k):
                    dve.wait_ge(turned_x, s + (k + 1))
                    need(dve, up_done, s + (k - 1))
                    v.tensor_copy(xT[:, k % 2, :], x_bank[:, 0:W]).then_inc(xT_ready, 1)

                def multiply(s, k):
                    dve.wait_ge(silu_done, s + (k + 1))
                    dve.wait_ge(up_done, s + (k + 1))
                    need(dve, turned_h, s + (k - 1))
                    v.tensor_tensor(h[:, k % 2, :], silu[:, k % 2, :], c.bank[2 + k % 2][:, :], ALU.mult).then_inc(h_done, 1)

                def keep_y(s, k):
                    dve.wait_ge(down_done, s + (k + 1))
                    need(dve, stored[k % 4], 4 * s + 16 * (k // 4))
                    v.tensor_copy(y[:, k % 4, :], y_bank[k % 2][:, 0:W]).then_inc(y_ready, 1)

                def slot(s, k):
                    if alive(s, k, 1):
                        keep_x(s, k + 1)
                    if m.gated and alive(s, k):
                        multiply(s, k)
                    if alive(s, k, -2):
                        keep_y(s, k - 2)

                keep_x(0, 0)
                in_slots(nc, dve, T, slot)
                if layer != 1:
                    combine(dve)

        if layer == 1:
            layer1_shared(c, "s2_", NC // 2, NC - NC // 2, gather, combine)


def layer1_ffn(c, arg):
    experts_phase(c, 1, arg)


def layer2_ffn(c, arg):
    experts_phase(c, 2, arg)


def layer3_ffn(c, arg):
    experts_phase(c, 3, arg)


def layer0_attention(c, arg):
    attention_phase(c, 0, arg)


def layer2_attention(c, arg):
    attention_phase(c, 2, arg)


ALL_PHASES = (layer0_attention, layer0_ffn, layer1_attention, layer1_ffn,
              layer2_attention, layer2_ffn, layer3_attention, layer3_ffn)


def end_phase(c, out):
    nc = c.nc
    stored = c.sem("x_stored")
    with nc.Block() as block:
        @block.sync
        def _(sp):
            sp.dma_start(out.rearrange("b (t p) d -> p (b t) d", p=P), c.x[:, TPB:, :]).then_inc(stored, 16)
            sp.wait_ge(stored, 16)


def build(nc, arg, out, phases=ALL_PHASES):
    with ExitStack() as ctx:
        c = Core(nc, ctx)
        start_phase(c, arg)
        for n, phase in enumerate(phases):
            norm_phase(c, n)
            phase(c, arg)
        end_phase(c, out)
        release_used(c)


def hid_major(w):
    return w.reshape(-1, P, w.shape[-1]).transpose(1, 0, 2).reshape(P, -1)


def gated(gate, up, down):
    return np.concatenate([np.concatenate([gate[e], up[e], hid_major(down[e])], axis=1) for e in range(len(gate))], axis=1)


def laid_out(inputs):
    a = {k: np.asarray(v) for k, v in inputs.items()}
    perm = np.arange(P).reshape(J, 2, D).transpose(1, 2, 0).reshape(P)
    o = {"x": a["x"], "ctxT": a["ctx_1024"].transpose(2, 0, 1), "mask": a["mask_1x1xSxS2_ff0"][0, 0],
         "maskT": a["mask_1x1xSxS2_ff0"][0, 0].T,
         "a0_w": np.stack([a["L0_xattn_Wq"][:, perm], a["L0_xattn_Wk"][:, perm], a["L0_xattn_Wv"], a["L0_xattn_Wo"]], axis=1)}
    wf = a["L2_xattn_Wf"].T
    o["a2_w"] = np.stack([a["L2_xattn_Wq"].T[:, perm], wf[:, :P][:, perm], wf[:, P:], a["L2_xattn_Wp"].T], axis=1)
    o["a2_bias_qk"] = np.stack([a["L2_xattn_bq"][perm], a["L2_xattn_bf"][:P][perm]], axis=1)
    o["a2_bias_row"] = np.stack([a["L2_xattn_bf"][P:], a["L2_xattn_bp"]])[None]
    o["a2_lora_a"] = np.stack([a["L2_xattn_Aq"], a["L2_xattn_Af"], a["L2_xattn_Ap"]], axis=1)
    bf = a["L2_xattn_Bf"].T
    o["a2_lora_b"] = np.stack([a["L2_xattn_Bq"].T[:, perm], bf[:, :P][:, perm], bf[:, P:], a["L2_xattn_Bp"].T], axis=1)
    f0_up = np.concatenate([a["L0_ffn_up_w"].reshape(-1, P), a["L0_ffn_shared_up"]]).T
    f0_down = np.concatenate([a["L0_ffn_down_w"].transpose(0, 2, 1).reshape(-1, P), a["L0_ffn_shared_down"].T])
    o["f0_w"] = np.concatenate([f0_up, hid_major(f0_down), a["L0_ffn_gate_w"].T], axis=1)
    o["f0_bias"] = np.tile(a["L0_ffn_bias_e"], (P, 1))
    o["const"] = np.concatenate([np.tile(np.arange(64), (P, 1)), np.triu(np.ones((P, P)), 1), np.arange(P)[:, None],
                                 np.tile(np.tril(np.ones((4, 4)), -1).reshape(16), (P, 1)),
                                 np.tile(64.0 ** np.arange(4), (P, 1))], axis=1).astype(np.float32)
    o["f1_w"] = gated(*(np.concatenate([a["L1_ffn_w_" + n], a["L1_ffn_ws_" + n][None]]) for n in ("gate", "up", "down")))
    o["f2_w"] = gated(a["L2_ffn_experts_w1"], a["L2_ffn_experts_w3"], a["L2_ffn_experts_w2"])
    o["f3_w"] = np.concatenate([a["L3_ffn_keys"], a["L3_ffn_values"]], axis=2).transpose(1, 0, 2).reshape(P, -1)
    o["e1_router"], o["e2_router"], o["e3_router"] = a["L1_ffn_w_router"], a["L2_ffn_gate"], a["L3_ffn_expert_sel"].T
    o["a1_w"] = np.stack([a["L1_xattn_W"][:, :P].T, a["L1_xattn_W"][:, P:].T])
    o["a1_bias"] = a["L1_xattn_b"][None]
    o["one_hot8"] = np.repeat(np.eye(B, dtype=np.float32)[:, :, None], P, axis=2)
    o["a3_w"] = np.stack([a["L3_xattn_W" + n] for n in "qkvo"], axis=1)
    o["a3_bias_qk"] = np.stack([a["L3_xattn_bq"], a["L3_xattn_bk"]], axis=1)
    o["a3_bias_vo"] = np.tile(np.stack([a["L3_xattn_bv"], a["L3_xattn_bo"]]), (P, 1, 1))
    expert = np.arange(8 * P) // 64
    o["spread0"] = np.tile(expert[None, :] == np.arange(16)[:, None], (PARTS, 1)).astype(np.float32)
    return {k: np.ascontiguousarray(v) for k, v in o.items()}


def kernel(**inputs):
    import concourse.bacc as bacc
    from concourse.bass_utils import run_bass_kernel_spmd

    nc = bacc.Bacc("TRN2", target_bir_lowering=False, num_devices=1)
    arrays = laid_out(inputs)
    arg = {k: nc.dram_tensor("in_" + k, v.shape, mybir.dt.from_np(v.dtype), kind="ExternalInput").ap() for k, v in arrays.items()}
    out = nc.dram_tensor("out", (B, TOK, P), F32, kind="ExternalOutput").ap()
    build(nc, arg, out)
    result = run_bass_kernel_spmd(nc, [{"in_" + k: v for k, v in arrays.items()}], core_ids=[0])
    return result.results[0]["out"]
```
